# Optimizing a Trainium2 kernel written in Bass

```python
import numpy as np
import jax
import jax.numpy as jnp

def _softmax(x, axis=-1):
    return jax.nn.softmax(x, axis=axis)

def _gelu(x):
    return jax.nn.gelu(x, approximate=True)

def _silu(x):
    return jax.nn.silu(x)

def _sigmoid(x):
    return jax.nn.sigmoid(x)

def _layernorm(x, axis=-1, eps=1e-05):
    m = jnp.mean(x, axis=axis, keepdims=True)
    v = jnp.var(x, axis=axis, keepdims=True)
    return (x - m) / jnp.sqrt(v + eps)

def _scatter_add(tgt, idx, src, axis=0):
    return tgt.at[idx].add(src)

def _segment_sum(src, seg, n):
    return jax.ops.segment_sum(src, seg, n)
kernel_name = 'mk_vit_tower_d2_tok_img512_r4_47bc6d'

def setup_inputs(seed: int=0):
    np.random.seed(seed)
    _w = jnp.asarray

    def _rec_inputs():
        import jax
        import jax.numpy as jnp
        _rk = jax.random.key(seed)
        x = -0.000178447 + 0.99995 * jax.random.normal(jax.random.fold_in(_rk, 1), (128, 3, 176, 208), jnp.float32)
        return x
    x = _rec_inputs()

    def _L0_tok_setup():
        import jax, jax.numpy as jnp
        import numpy as np
        P1, P2, C = (16, 16, 3)
        PW, PH = (176 // P1, 208 // P2)
        key = jax.random.key(seed)
        k1, k2, k3, k4, k5 = jax.random.split(key, 5)
        B, D = (64, 128)
        patch_dim = P1 * P2 * C
        return {'x': jax.random.normal(k1, (B, C, PW * P1, PH * P2), dtype=jnp.float32), 'W': jax.random.normal(k2, (D, patch_dim), dtype=jnp.float32) * 0.02, 'b': jax.random.normal(k3, (D,), dtype=jnp.float32) * 0.02, 'cls_token': jax.random.uniform(k4, (1, 1, D), dtype=jnp.float32), 'pos_emb': jax.random.normal(k5, (1, PW * PH + 1, 1), dtype=jnp.float32)}
    _L0_tok_all = _L0_tok_setup()
    _L0_tok_in = {k: v for k, v in _L0_tok_all.items() if k in ('W', 'b', 'cls_token', 'pos_emb')}
    del _L0_tok_all

    def _L0_attn_setup():
        import jax, jax.numpy as jnp
        import numpy as np
        from jax import lax
        D_MODEL = 128
        EXPAND = 2
        INNER = D_MODEL * EXPAND
        K = 4
        B, T = (8, 512)
        LN_EPS = 1e-05

        def _layernorm(x, w, b):
            mu = jnp.mean(x, axis=-1, keepdims=True)
            var = jnp.mean(jnp.square(x - mu), axis=-1, keepdims=True)
            return (x - mu) * lax.rsqrt(var + LN_EPS) * w + b

        def _causal_dw_conv(x_bct, w, b):
            y = lax.conv_general_dilated(x_bct, w, window_strides=(1,), padding=[(K - 1, 0)], dimension_numbers=('NCH', 'OIH', 'NCH'), feature_group_count=INNER)
            return y + b[None, :, None]
        key = jax.random.key(seed)
        ks = jax.random.split(key, 12)
        s_in = 1.0 / np.sqrt(D_MODEL)
        s_out = 1.0 / np.sqrt(INNER)
        return {'x': jax.random.normal(ks[0], (B, T, D_MODEL), dtype=jnp.float32), 'ln_w': jnp.ones((D_MODEL,), jnp.float32), 'ln_b': jnp.zeros((D_MODEL,), jnp.float32), 'in_proj_w': jax.random.uniform(ks[1], (3 * INNER, D_MODEL), jnp.float32, -s_in, s_in), 'in_proj_b': jax.random.uniform(ks[2], (3 * INNER,), jnp.float32, -s_in, s_in), 'conv_w': jax.random.uniform(ks[3], (INNER, 1, K), jnp.float32, -0.5, 0.5), 'conv_b': jax.random.uniform(ks[4], (INNER,), jnp.float32, -0.5, 0.5), 'delta_w': jax.random.uniform(ks[5], (INNER, D_MODEL), jnp.float32, -s_in, s_in), 'delta_b': jax.random.uniform(ks[6], (INNER,), jnp.float32, -s_in, s_in), 'state_mix': jnp.zeros((INNER,), jnp.float32), 'skip_scale': jnp.ones((INNER,), jnp.float32), 'out_proj_w': jax.random.uniform(ks[7], (D_MODEL, INNER), jnp.float32, -s_out, s_out), 'out_proj_b': jax.random.uniform(ks[8], (D_MODEL,), jnp.float32, -s_out, s_out)}
    _L0_attn_all = _L0_attn_setup()
    _L0_attn_in = {k: v for k, v in _L0_attn_all.items() if k in ('ln_w', 'ln_b', 'in_proj_w', 'in_proj_b', 'conv_w', 'conv_b', 'delta_w', 'delta_b', 'state_mix', 'skip_scale', 'out_proj_w', 'out_proj_b')}
    del _L0_attn_all

    def _L0_ffn_setup():
        import jax, jax.numpy as jnp
        import numpy as np
        B, S, D = (2, 256, 128)
        R, V, E, K, FF = (3, 3, 8, 2, 512)

        def _ln(x, g, b):
            m = jnp.mean(x, axis=-1, keepdims=True)
            v = jnp.mean((x - m) ** 2, axis=-1, keepdims=True)
            return (x - m) / jnp.sqrt(v + 1e-05) * g + b
        key = jax.random.key(seed)
        ks = jax.random.split(key, 12)
        w = 0.02
        return {'x': jax.random.normal(ks[0], (B, S, D), jnp.float32), 'mr_w': jax.random.normal(ks[1], (R, D, D), jnp.float32) * w, 'mr_b': jnp.zeros((R, D), jnp.float32), 'mv_w': jax.random.normal(ks[2], (V, D, D), jnp.float32) * w, 'mv_b': jnp.zeros((V, D), jnp.float32), 'mv_alpha': jnp.zeros((V,), jnp.float32), 'gate_w': jax.random.normal(ks[3], (D, E), jnp.float32) * w, 'gate_b': jnp.zeros((E,), jnp.float32), 'e_w1': jax.random.normal(ks[4], (E, D, FF), jnp.float32) * w, 'e_b1': jnp.zeros((E, FF), jnp.float32), 'e_w2': jax.random.normal(ks[5], (E, FF, D), jnp.float32) * w, 'e_b2': jnp.zeros((E, D), jnp.float32), 'ln1_g': jnp.ones((D,), jnp.float32), 'ln1_b': jnp.zeros((D,), jnp.float32), 'ln2_g': jnp.ones((D,), jnp.float32), 'ln2_b': jnp.zeros((D,), jnp.float32), 'ln3_g': jnp.ones((D,), jnp.float32), 'ln3_b': jnp.zeros((D,), jnp.float32)}
    _L0_ffn_all = _L0_ffn_setup()
    _L0_ffn_in = {k: v for k, v in _L0_ffn_all.items() if k in ('mr_w', 'mr_b', 'mv_w', 'mv_b', 'mv_alpha', 'gate_w', 'gate_b', 'e_w1', 'e_b1', 'e_w2', 'e_b2', 'ln1_g', 'ln1_b', 'ln2_g', 'ln2_b', 'ln3_g', 'ln3_b')}
    del _L0_ffn_all

    def _L1_attn_setup():
        import jax, jax.numpy as jnp
        import numpy as np
        D_MODEL = 128
        NHEAD = 8
        WINDOW = 32
        key = jax.random.key(seed)
        ks = jax.random.split(key, 5)
        B, S, D = (2, 512, D_MODEL)
        return {'x': jax.random.normal(ks[0], (B, S, D), dtype=jnp.float32), 'w_qkv': jax.random.normal(ks[1], (D, 3 * D), dtype=jnp.float32) * 0.02, 'b_qkv': jax.random.normal(ks[2], (3 * D,), dtype=jnp.float32) * 0.02, 'w_out': jax.random.normal(ks[3], (D, D), dtype=jnp.float32) * 0.02, 'b_out': jax.random.normal(ks[4], (D,), dtype=jnp.float32) * 0.02}
    _L1_attn_all = _L1_attn_setup()
    _L1_attn_in = {k: v for k, v in _L1_attn_all.items() if k in ('w_qkv', 'b_qkv', 'w_out', 'b_out')}
    del _L1_attn_all

    def _L1_ffn_setup():
        import jax, jax.numpy as jnp
        import numpy as np
        B, S, D, E, O = (256, 64, 128, 16, 128)
        key = jax.random.key(seed)
        k_x, k_wg, k_bg, k_we, k_be = jax.random.split(key, 5)
        scale_g = 1.0 / np.sqrt(D)
        scale_e = 1.0 / np.sqrt(D)
        return {'x': jax.random.normal(k_x, (B, S, D), dtype=jnp.float32), 'Wg': jax.random.uniform(k_wg, (D, E), jnp.float32, -scale_g, scale_g), 'bg': jax.random.uniform(k_bg, (E,), jnp.float32, -scale_g, scale_g), 'We': jax.random.uniform(k_we, (E, D, O), jnp.float32, -scale_e, scale_e), 'be': jax.random.uniform(k_be, (E, O), jnp.float32, -scale_e, scale_e)}
    _L1_ffn_all = _L1_ffn_setup()
    _L1_ffn_in = {k: v for k, v in _L1_ffn_all.items() if k in ('Wg', 'bg', 'We', 'be')}
    del _L1_ffn_all
    return {'x': x, 'L0_tok_W': _L0_tok_in['W'], 'L0_tok_b': _L0_tok_in['b'], 'L0_tok_cls_token': _L0_tok_in['cls_token'], 'L0_tok_pos_emb': _L0_tok_in['pos_emb'], 'L0_attn_ln_w': _L0_attn_in['ln_w'], 'L0_attn_ln_b': _L0_attn_in['ln_b'], 'L0_attn_in_proj_w': _L0_attn_in['in_proj_w'], 'L0_attn_in_proj_b': _L0_attn_in['in_proj_b'], 'L0_attn_conv_w': _L0_attn_in['conv_w'], 'L0_attn_conv_b': _L0_attn_in['conv_b'], 'L0_attn_delta_w': _L0_attn_in['delta_w'], 'L0_attn_delta_b': _L0_attn_in['delta_b'], 'L0_attn_state_mix': _L0_attn_in['state_mix'], 'L0_attn_skip_scale': _L0_attn_in['skip_scale'], 'L0_attn_out_proj_w': _L0_attn_in['out_proj_w'], 'L0_attn_out_proj_b': _L0_attn_in['out_proj_b'], 'L0_ffn_mr_w': _L0_ffn_in['mr_w'], 'L0_ffn_mr_b': _L0_ffn_in['mr_b'], 'L0_ffn_mv_w': _L0_ffn_in['mv_w'], 'L0_ffn_mv_b': _L0_ffn_in['mv_b'], 'L0_ffn_mv_alpha': _L0_ffn_in['mv_alpha'], 'L0_ffn_gate_w': _L0_ffn_in['gate_w'], 'L0_ffn_gate_b': _L0_ffn_in['gate_b'], 'L0_ffn_e_w1': _L0_ffn_in['e_w1'], 'L0_ffn_e_b1': _L0_ffn_in['e_b1'], 'L0_ffn_e_w2': _L0_ffn_in['e_w2'], 'L0_ffn_e_b2': _L0_ffn_in['e_b2'], 'L0_ffn_ln1_g': _L0_ffn_in['ln1_g'], 'L0_ffn_ln1_b': _L0_ffn_in['ln1_b'], 'L0_ffn_ln2_g': _L0_ffn_in['ln2_g'], 'L0_ffn_ln2_b': _L0_ffn_in['ln2_b'], 'L0_ffn_ln3_g': _L0_ffn_in['ln3_g'], 'L0_ffn_ln3_b': _L0_ffn_in['ln3_b'], 'L1_attn_w_qkv': _L1_attn_in['w_qkv'], 'L1_attn_b_qkv': _L1_attn_in['b_qkv'], 'L1_attn_w_out': _L1_attn_in['w_out'], 'L1_attn_b_out': _L1_attn_in['b_out'], 'L1_ffn_Wg': _L1_ffn_in['Wg'], 'L1_ffn_bg': _L1_ffn_in['bg'], 'L1_ffn_We': _L1_ffn_in['We'], 'L1_ffn_be': _L1_ffn_in['be']}

def reference(x, L0_tok_W, L0_tok_b, L0_tok_cls_token, L0_tok_pos_emb, L0_attn_ln_w, L0_attn_ln_b, L0_attn_in_proj_w, L0_attn_in_proj_b, L0_attn_conv_w, L0_attn_conv_b, L0_attn_delta_w, L0_attn_delta_b, L0_attn_state_mix, L0_attn_skip_scale, L0_attn_out_proj_w, L0_attn_out_proj_b, L0_ffn_mr_w, L0_ffn_mr_b, L0_ffn_mv_w, L0_ffn_mv_b, L0_ffn_mv_alpha, L0_ffn_gate_w, L0_ffn_gate_b, L0_ffn_e_w1, L0_ffn_e_b1, L0_ffn_e_w2, L0_ffn_e_b2, L0_ffn_ln1_g, L0_ffn_ln1_b, L0_ffn_ln2_g, L0_ffn_ln2_b, L0_ffn_ln3_g, L0_ffn_ln3_b, L1_attn_w_qkv, L1_attn_b_qkv, L1_attn_w_out, L1_attn_b_out, L1_ffn_Wg, L1_ffn_bg, L1_ffn_We, L1_ffn_be):
    import jax
    import jax.numpy as jnp

    def _L0_tok_ref(x, W, b, cls_token, pos_emb):
        import jax, jax.numpy as jnp
        import numpy as np
        P1, P2, C = (16, 16, 3)
        PW, PH = (176 // P1, 208 // P2)
        B = x.shape[0]
        patches = x.reshape(B, C, PW, P1, PH, P2)
        patches = patches.transpose(0, 2, 4, 3, 5, 1).reshape(B, PW * PH, P1 * P2 * C)
        proj = jnp.einsum('bnp,dp->bnd', patches, W) + b
        cls = jnp.broadcast_to(cls_token, (B, 1, cls_token.shape[-1]))
        out = jnp.concatenate([cls, proj], axis=1) + pos_emb
        return out

    def _L0_attn_ref(x, ln_w, ln_b, in_proj_w, in_proj_b, conv_w, conv_b, delta_w, delta_b, state_mix, skip_scale, out_proj_w, out_proj_b):
        import jax, jax.numpy as jnp
        import numpy as np
        from jax import lax
        D_MODEL = 128
        EXPAND = 2
        INNER = D_MODEL * EXPAND
        K = 4
        B, T = (8, 512)
        LN_EPS = 1e-05

        def _layernorm(x, w, b):
            mu = jnp.mean(x, axis=-1, keepdims=True)
            var = jnp.mean(jnp.square(x - mu), axis=-1, keepdims=True)
            return (x - mu) * lax.rsqrt(var + LN_EPS) * w + b

        def _causal_dw_conv(x_bct, w, b):
            y = lax.conv_general_dilated(x_bct, w, window_strides=(1,), padding=[(K - 1, 0)], dimension_numbers=('NCH', 'OIH', 'NCH'), feature_group_count=INNER)
            return y + b[None, :, None]
        residual = x
        xn = _layernorm(x, ln_w, ln_b)
        h = xn @ in_proj_w.T + in_proj_b
        proj, gate, drive = jnp.split(h, 3, axis=-1)
        proj = jax.nn.silu(proj)
        gate = jax.nn.sigmoid(gate)
        conv_out = _causal_dw_conv(jnp.swapaxes(proj, 1, 2), conv_w, conv_b)
        conv_out = jnp.swapaxes(conv_out, 1, 2)
        delta = jnp.maximum(jax.nn.sigmoid(xn @ delta_w.T + delta_b), 0.0001)
        drive = jnp.tanh(drive)
        a = jax.nn.sigmoid(state_mix)
        d = delta * drive

        def step(state, d_t):
            state = a * state + d_t
            return (state, state)
        _, states = lax.scan(step, jnp.zeros((x.shape[0], INNER), x.dtype), jnp.swapaxes(d, 0, 1))
        states = jnp.swapaxes(states, 0, 1)
        y = (states + skip_scale * conv_out) * gate
        y = y @ out_proj_w.T + out_proj_b
        return residual + y

    def _L0_ffn_ref(x, mr_w, mr_b, mv_w, mv_b, mv_alpha, gate_w, gate_b, e_w1, e_b1, e_w2, e_b2, ln1_g, ln1_b, ln2_g, ln2_b, ln3_g, ln3_b):
        import jax, jax.numpy as jnp
        import numpy as np
        B, S, D = (2, 256, 128)
        R, V, E, K, FF = (3, 3, 8, 2, 512)

        def _ln(x, g, b):
            m = jnp.mean(x, axis=-1, keepdims=True)
            v = jnp.mean((x - m) ** 2, axis=-1, keepdims=True)
            return (x - m) / jnp.sqrt(v + 1e-05) * g + b
        b, s, d = x.shape
        mr = jnp.zeros_like(x)
        for r in range(R):
            k = 2 ** r
            pooled = x.reshape(b, s // k, k, d).mean(axis=2)
            y = jnp.einsum('bsd,de->bse', pooled, mr_w[r]) + mr_b[r]
            mr = mr + jnp.repeat(y, k, axis=1)
        mr = mr / R
        x = _ln(mr + x, ln1_g, ln1_b)
        views = jax.nn.gelu(jnp.einsum('bsd,vde->vbse', x, mv_w) + mv_b[:, None, None, :])
        alpha = jax.nn.softmax(mv_alpha)
        mv = jnp.einsum('vbsd,v->bsd', views, alpha)
        x = _ln(mv + x, ln2_g, ln2_b)
        logits = x @ gate_w + gate_b
        topv, topi = jax.lax.top_k(logits, K)
        probs = jax.nn.softmax(topv, axis=-1)
        w = jnp.sum(jax.nn.one_hot(topi, E, dtype=x.dtype) * probs[..., None], axis=-2)
        h = jax.nn.gelu(jnp.einsum('bsd,edf->ebsf', x, e_w1) + e_b1[:, None, None, :])
        ye = jnp.einsum('ebsf,efd->ebsd', h, e_w2) + e_b2[:, None, None, :]
        moe = jnp.einsum('ebsd,bse->bsd', ye, w)
        x = _ln(moe + x, ln3_g, ln3_b)
        return x

    def _L1_attn_ref(x, w_qkv, b_qkv, w_out, b_out):
        import jax, jax.numpy as jnp
        import numpy as np
        D_MODEL = 128
        NHEAD = 8
        WINDOW = 32
        B, S, D = x.shape
        H = NHEAD
        hd = D // H
        w = WINDOW
        W = 2 * w + 1
        qkv = (x @ w_qkv + b_qkv).reshape(B, S, 3, H, hd)
        q, k, v = (qkv[:, :, 0], qkv[:, :, 1], qkv[:, :, 2])
        idx = jnp.arange(S)[:, None] + jnp.arange(-w, w + 1)[None, :]
        valid = (idx >= 0) & (idx < S)
        idx_c = jnp.clip(idx, 0, S - 1)
        k_win = k[:, idx_c]
        v_win = v[:, idx_c]
        scale = 1.0 / hd ** 0.5
        scores = jnp.einsum('bshd,bswhd->bshw', q, k_win) * scale
        scores = jnp.where(valid[None, :, None, :], scores, -1000000000.0)
        attn = jax.nn.softmax(scores, axis=-1)
        out = jnp.einsum('bshw,bswhd->bshd', attn, v_win).reshape(B, S, D)
        return out @ w_out + b_out

    def _L1_ffn_ref(x, Wg, bg, We, be):
        import jax, jax.numpy as jnp
        import numpy as np
        B, S, D, E, O = (256, 64, 128, 16, 128)
        scores = jax.nn.softmax(jnp.mean(x, axis=1) @ Wg + bg, axis=-1)
        idx = jnp.argmax(scores, axis=-1)
        gate = jnp.take_along_axis(scores, idx[:, None], axis=-1)
        W_sel = We[idx]
        b_sel = be[idx]
        y = jnp.einsum('bsd,bdo->bso', x, W_sel) + b_sel[:, None, :]
        return gate[:, :, None] * y
    h = _L0_tok_ref(x, L0_tok_W, L0_tok_b, L0_tok_cls_token, L0_tok_pos_emb)
    h = h + _L0_attn_ref(_layernorm(h, axis=-1), L0_attn_ln_w, L0_attn_ln_b, L0_attn_in_proj_w, L0_attn_in_proj_b, L0_attn_conv_w, L0_attn_conv_b, L0_attn_delta_w, L0_attn_delta_b, L0_attn_state_mix, L0_attn_skip_scale, L0_attn_out_proj_w, L0_attn_out_proj_b)
    h = h + _L0_ffn_ref(_layernorm(h, axis=-1), L0_ffn_mr_w, L0_ffn_mr_b, L0_ffn_mv_w, L0_ffn_mv_b, L0_ffn_mv_alpha, L0_ffn_gate_w, L0_ffn_gate_b, L0_ffn_e_w1, L0_ffn_e_b1, L0_ffn_e_w2, L0_ffn_e_b2, L0_ffn_ln1_g, L0_ffn_ln1_b, L0_ffn_ln2_g, L0_ffn_ln2_b, L0_ffn_ln3_g, L0_ffn_ln3_b)
    h = h + _L1_attn_ref(_layernorm(h, axis=-1), L1_attn_w_qkv, L1_attn_b_qkv, L1_attn_w_out, L1_attn_b_out)
    h = h + _L1_ffn_ref(_layernorm(h, axis=-1), L1_ffn_Wg, L1_ffn_bg, L1_ffn_We, L1_ffn_be)
    return h

_drawn_inputs = setup_inputs


def setup_inputs(seed=0):
    import zlib

    import numpy as np

    out = dict(_drawn_inputs(seed))
    spreads = {'L0_attn_ln_w': (1.0, 0.6),
     'L0_attn_ln_b': (0.0, 0.602),
     'L0_attn_state_mix': (0.0, 0.8),
     'L0_attn_skip_scale': (1.0, 0.6),
     'L0_ffn_mr_b': (0.0, 0.381),
     'L0_ffn_mv_b': (0.0, 0.604),
     'L0_ffn_mv_alpha': (0.0, 0.8),
     'L0_ffn_gate_b': (0.0, 0.374),
     'L0_ffn_e_b1': (0.0, 0.8),
     'L0_ffn_e_b2': (0.0, 0.315),
     'L0_ffn_ln1_g': (1.0, 0.2),
     'L0_ffn_ln1_b': (0.0, 0.1),
     'L0_ffn_ln2_g': (1.0, 0.2),
     'L0_ffn_ln2_b': (0.0, 0.1),
     'L0_ffn_ln3_g': (1.0, 0.2),
     'L0_ffn_ln3_b': (0.0, 0.1)}
    factors = {'L0_attn_in_proj_b': 5.669,
     'L0_attn_delta_w': 3.903,
     'L0_attn_delta_b': 8.0,
     'L0_ffn_e_w1': 3.921,
     'L0_ffn_e_w2': 3.58,
     'L1_attn_w_qkv': 8.0,
     'L1_attn_b_qkv': 8.0,
     'L1_attn_w_out': 8.0,
     'L1_attn_b_out': 6.887,
     'L1_ffn_Wg': 3.796,
     'L1_ffn_bg': 3.891,
     'L1_ffn_We': 3.756,
     'L1_ffn_be': 8.0}
    for name, (base, spread) in spreads.items():
        noise = np.random.default_rng([zlib.crc32(name.encode()), seed]).standard_normal(out[name].shape)
        drawn = base * np.exp(spread * noise) if base else spread * noise
        out[name] = jnp.asarray(drawn.astype(out[name].dtype))
    for name, factor in factors.items():
        out[name] = (out[name] * factor).astype(out[name].dtype)
    return out
```

```python
from contextlib import ExitStack

import numpy as np

import concourse.bass as bass
from concourse import mybir

F32 = mybir.dt.float32
I32 = mybir.dt.int32
ALU = mybir.AluOpType
ACT = mybir.ActivationFunctionType
AX_X = mybir.AxisListType.X

D = 128
PATCH = 16
CHANNELS = 3
KC = CHANNELS * PATCH * PATCH // 128
GW, GH = 176 // PATCH, 208 // PATCH
NPATCH = GW * GH
S = NPATCH + 1
IMGS = 4
T = IMGS * S
T2 = T // 2
G = 96
NG = T // G
E = 8
FF = 512
FC = FF // 128
BLK = 512
CB = BLK // 128
HEADS = 8
HD = D // HEADS
WIN = 32
QB = 16
NQB = S // QB
KW = 96
KPAD = 224
NWIN = (NQB + 1) // 2
UB = 4
NU = IMGS * NQB // UB
E2 = 16
EPS = 1e-5
NEG = -1e30

COLS = {}
for _name, _n in (("ln_w", 1), ("ln_b", 1), ("in_b", 8), ("conv_w", 8), ("conv_b", 2), ("state_mix", 2),
                  ("skip", 2), ("out_b", 1), ("tok_b", 1), ("cls", 1), ("mr_b", 3), ("ln1_g", 1), ("ln1_b", 1),
                  ("mv_b", 3), ("ln2_g", 1), ("ln2_b", 1), ("ln3_g", 1), ("ln3_b", 1), ("q_b", 1), ("k_b", 1),
                  ("v_b", 1), ("attn_b", 1)):
    COLS[_name] = (sum(n for _, n in COLS.values()), _n)
NCOLS = sum(n for _, n in COLS.values())
ROWS = {}
for _name, _n in (("pos", S), ("alpha", 3), ("gate_b", E), ("bg", E2)):
    ROWS[_name] = (sum(n for _, n in ROWS.values()), _n)
NROWS = sum(n for _, n in ROWS.values())


def sizes(images):
    tokens = images * S
    region = -(-tokens // BLK) * BLK + BLK
    blocks = (2 * tokens + E * (BLK - 1)) // BLK
    blocks += blocks % 2
    return tokens, region, blocks


def const_rows(images):
    tokens, region, blocks = sizes(images)
    kmax = -(-tokens // BLK) + 1
    parts = {
        "first": np.arange(E) * region,
        "rev": np.arange(E, 0, -1),
        "rev16": np.arange(E2, 0, -1),
        "blk": np.arange(blocks),
        "kblk": np.arange(kmax) * BLK,
    }
    where, at = {}, 0
    for k, v in parts.items():
        where[k] = (at, len(v))
        at += len(v)
    return where, np.concatenate(list(parts.values())).astype(np.float32)[None, :]


def const_tiles():
    p = np.arange(128)
    same_head = (p[:, None] // HD == p[None, :] // HD)
    band = np.full((128, NQB, KW), NEG, np.float32)
    for b in range(NQB):
        q = b * QB + np.arange(128) % QB
        key = WIN * (b // 2) - WIN + np.arange(KW)
        ok = (abs(key[None, :] - q[:, None]) <= WIN) & (key >= 0)[None, :] & (key < S)[None, :]
        band[:, b, :][ok] = 0.0
    band = np.concatenate([band, band[:, :UB - 1]], axis=1)
    parts = {
        "center": np.eye(128) - 1.0 / D,
        "mean": np.full((128, 128), 1.0 / D),
        "ident": np.eye(128),
        "before": (p[:, None] < p[None, :])[:, :G],
        "ones": np.ones((128, 128)),
        "head_rows": (p[:, None] // HD == np.arange(HEADS)[None, :]),
        "head_block": same_head,
        "query": (p[:, None] % QB == np.arange(QB)[None, :]),
        "band": band.reshape(128, -1),
    }
    where, at = {}, 0
    for k, v in parts.items():
        where[k] = (at, v.shape[1])
        at += v.shape[1]
    return where, np.concatenate([np.asarray(v, np.float32) for v in parts.values()], axis=1)


def build(nc, images, a):
    tokens, REGION, NB = sizes(images)
    ITERS = images // (2 * IMGS)
    cw, _ = const_tiles()
    rw, _ = const_rows(images)
    KMAX = rw["kblk"][1]
    assert S % QB == 0 and S % 4 == 0 and T % G == 0 and IMGS * NQB % UB == 0

    with ExitStack() as ctx:
        def sem(name):
            return ctx.enter_context(nc.semaphore(name))

        def sems(name):
            return [sem(f"{name}{s}") for s in range(2)]

        def sb(name, shape, dt=F32, where=ctx):
            return where.enter_context(nc.sbuf_tensor(name, shape, dt))

        expert_in = nc.dram_tensor("expert_in", (E * REGION + BLK, D), F32, kind="Internal").ap()
        expert_out = nc.dram_tensor("expert_out", (NB * BLK, D), F32, kind="Internal").ap()
        h1_dram = nc.dram_tensor("h1_dram", (128, tokens), F32, kind="Internal").ap()
        x2_dram = nc.dram_tensor("x2_dram", (128, tokens), F32, kind="Internal").ap()

        P = [[ctx.enter_context(nc.psum_tensor(f"psum{s}{k}", [128, 2, 512], F32)) for k in range(2)]
             for s in range(2)]

        def pv(s, k):
            return P[s][k][:, :, 0:T2]

        def two(ap):
            return ap.rearrange("p (g n) -> p g n", g=2)

        def four(ap):
            return ap.rearrange("p (m n) -> p m n", m=IMGS)

        def two_two(ap):
            return ap.rearrange("p (g m) n -> p g m n", g=2)

        def pv4(s, k):
            return pv(s, k).rearrange("p g (m n) -> p g m n", m=2)

        cst = sb("cst", [128, sum(n for _, n in cw.values())])
        crow = sb("crow", [128, sum(n for _, n in rw.values())])
        col = sb("col", [128, NCOLS])
        row = sb("row", [128, NROWS])

        def C(name):
            o, n = cw[name]
            return cst[:, o:o + n]

        def R(name):
            o, n = rw[name]
            return crow[:, o:o + n]

        def V(name, k=0):
            o, n = COLS[name]
            return col[:, o + k:o + k + 1]

        def RR(name):
            o, n = ROWS[name]
            return row[:, o:o + n]

        slots = sb("slots", [G, ITERS * 4 * NG])
        weights = sb("weights", [G, ITERS * 4 * NG])
        out_rows = sb("out_rows", [G, ITERS * 4 * NG])
        chosen = sb("chosen", [G, E])
        table = sb("table", [1, 2 * NB], I32)
        tails = sb("tails", [1, E], I32)

        loaded = sem("loaded")
        prep = sem("prep")
        prep_act = sem("prep_act")
        prep_pe = sem("prep_pe")
        consts_ready = sem("consts_ready")
        centered, squared, variance = sems("centered"), sems("squared"), sems("variance")
        logvar, rstd, normed = sems("logvar"), sems("rstd"), sems("normed")

        held = {"sync": sem("held_sync"), "pool": sem("held_pool")}

        def hold(eng, s, value):
            eng.wait_ge(s, value)
            eng.sem_inc(held["pool" if eng is nc.gpsimd else "sync"], 1)

        def ln_pe(pe, s, src, k):
            for g in range(2):
                last = nc.tensor.matmul(P[s][1][:, g, 0:T2], C("center"), two(src)[:, g, :], start=True, stop=True)
            last.then_inc(centered[s], 1)

        def ln_pe_var(pe, s, sq, k):
            pe.wait_ge(squared[s], k + 1)
            for g in range(2):
                last = nc.tensor.matmul(P[s][0][:, g, 0:T2], C("mean"), two(sq)[:, g, :], start=True, stop=True)
            last.then_inc(variance[s], 1)

        def ln_act_square(act, s, sq, k):
            act.wait_ge(centered[s], k + 1)
            nc.scalar.activation(two(sq), pv(s, 1), ACT.Square).then_inc(squared[s], 1)

        def ln_act_rstd(act, s, r, k, kr):
            act.wait_ge(variance[s], k + 1)
            nc.scalar.activation(two(r), pv(s, 0), ACT.Ln, bias=eps_col[:, 0:1]).then_inc(logvar[s], 1)
            act.wait_ge(logvar[s], kr + 1)
            nc.scalar.activation(r, r, ACT.Exp, scale=-0.5).then_inc(rstd[s], 1)

        eps_col = sb("eps_col", [128, 2])

        mem_a = ExitStack()
        w_tok = sb("w_tok", [128, KC, D], F32, mem_a)
        w_in = sb("w_in", [128, 8, 128], F32, mem_a)
        w_out = sb("w_out", [128, 2, D], F32, mem_a)
        w_mr = sb("w_mr", [128, 3, D], F32, mem_a)
        w_mv = sb("w_mv", [128, 3, D], F32, mem_a)
        w_gate = sb("w_gate", [128, E], F32, mem_a)
        in_bias = sb("in_bias", [128, 8], F32, mem_a)
        in_half = sb("in_half", [128, 8], F32, mem_a)
        taps = sb("taps", [128, 8], F32, mem_a)
        conv_b = sb("conv_b", [128, 2], F32, mem_a)
        decay = sb("decay", [128, 2], F32, mem_a)
        posb = sb("posb", [128, S], F32, mem_a)
        mr_bias = sb("mr_bias", [128, 1], F32, mem_a)
        alpha = sb("alpha", [128, 3], F32, mem_a)
        tiny = sb("tiny", [128, 8], F32, mem_a)

        def pair(name, shape, dt=F32, where=None):
            return [sb(f"{name}{s}", shape, dt, where or mem_a) for s in range(2)]

        xin = pair("xin", [128, KC, IMGS * NPATCH])
        h0, sq, ra, rb = pair("h0", [128, T]), pair("sq", [128, T]), pair("ra", [128, T]), pair("rb", [128, T])
        xn1, xn2, res = pair("xn1", [128, T]), pair("xn2", [128, T]), pair("res", [128, T])
        unit = [[sb(f"unit{s}{u}", [128, T], F32, mem_a) for u in range(8)] for s in range(2)]
        zproj = [[sb(f"zproj{s}{c}", [128, T], F32, mem_a) for c in range(2)] for s in range(2)]
        pj = [[sb(f"pj{s}{c}", [128, IMGS, S + 3], F32, mem_a) for c in range(2)] for s in range(2)]
        acc = [[sb(f"acc{s}{c}", [128, T], F32, mem_a) for c in range(2)] for s in range(2)]
        h1, x2 = pair("h1", [128, T]), pair("x2", [128, T])
        pool2, pool4 = pair("pool2", [128, T // 2]), pair("pool4", [128, T // 4])
        rows = pair("rows", [G, NG, D])
        logit, lmask, cand = pair("logit", [G, NG, E]), pair("lmask", [G, NG, E]), pair("cand", [G, NG, E])
        pick1, pick2, picks = pair("pick1", [G, NG, E]), pair("pick2", [G, NG, E]), pair("picks", [G, NG, E])
        top1, top2, best = pair("top1", [G, NG]), pair("top2", [G, NG]), pair("best", [G, NG])
        wexp, wsum = pair("wexp", [G, NG]), pair("wsum", [G, NG])
        newly = pair("newly", [G, E])
        slot = pair("slot", [G, 2 * NG])
        slot_i = pair("slot_i", [G, 2 * NG], I32)
        DELTA, DRIVE, PROJ, GATE = (0, 1), (2, 3), (4, 5), (6, 7)

        x_landed, tok_done, embedded = sems("x_landed"), sems("tok_done"), sems("embedded")
        res_done = sems("res_done")
        unit_done, unit_act = sems("unit_done"), sems("unit_act")
        delta_step = sems("delta_step")
        mix_step = sems("mix_step")
        out_done, h1_ready, h1_stored = sems("out_done"), sems("h1_ready"), sems("h1_stored")
        ffn_step, mr_done = sems("ffn_step"), sems("mr_done")
        mv_done, gelu_done = sems("mv_done"), sems("gelu_done")
        x2_stored, logits_done = sems("x2_stored"), sems("logits_done")
        turned, rows_ready, route_step = sems("turned"), sems("rows_ready"), sems("route_step")
        wexp_done, rank_done, slots_ready, scattered = (sems("wexp_done"), sems("rank_done"), sems("slots_ready"),
                                                        sems("scattered"))
        chosen_new = sem("chosen_new")
        LNA = 4
        RSA = LNA + 1
        MIX = 11
        FFN = 11
        x0, x1, view = xn1, xn2, [[unit[s][u] for u in (0, 1, 2)] for s in range(2)]
        pre = rb

        def a_range(i, s):
            return bass.DynSlice((2 * i + s) * T, T)

        def a_sync(sp):
            for dst, src in ((cst, "cst"), (crow, "crow"), (col, "col"), (row, "row"), (w_tok, "w_tok"),
                             (w_in, "w_in"), (w_out, "w_out"), (w_mr, "w_mr"), (w_mv, "w_mv"), (w_gate, "w_gate")):
                src = a[src]
                if src.shape[0] == 1:
                    src = src.to_broadcast([128, src.shape[1]])
                sp.dma_start(dst[:], src).then_inc(loaded, 16)
            with sp.Fori(0, ITERS) as i:
                for s in range(2):
                    hold(sp, tok_done[s], i)
                    sp.dma_start(xin[s][:], a["x"][bass.DynSlice(2 * i + s, 1)].rearrange("o p k n -> (o p) k n")
                                 ).then_inc(x_landed[s], 16)
                for s in range(2):
                    hold(sp, h1_ready[s], i + 1)
                    sp.dma_start(h1_dram[:, a_range(i, s)], h1[s][:]).then_inc(h1_stored[s], 16)
                for s in range(2):
                    hold(sp, ffn_step[s], FFN * i + 11)
                    sp.dma_start(x2_dram[:, a_range(i, s)], x2[s][:]).then_inc(x2_stored[s], 16)
            for s in range(2):
                sp.wait_ge(h1_stored[s], 16 * ITERS)
                sp.wait_ge(x2_stored[s], 16 * ITERS)

        NLOADS = 10

        def a_prep_vector(v):
            n = [0]

            def step(ins):
                n[0] += 1
                ins.then_inc(prep, 1)

            def settle():
                v.wait_ge(prep, n[0])

            step(v.memset(eps_col[:, 0:1], EPS))
            step(v.memset(eps_col[:, 1:2], EPS * EPS))
            step(v.memset(chosen[:], 0.0))
            for s in range(2):
                for c in range(2):
                    step(v.memset(pj[s][c][:], 0.0))
            v.wait_ge(loaded, 16 * NLOADS)
            v.wait_ge(prep_pe, 1)
            step(v.tensor_scalar(w_in[:], w_in[:], V("ln_w"), None, ALU.mult))
            o, _ = COLS["in_b"]
            step(v.tensor_tensor(in_bias[:], P[0][0][:, 0, 0:8], col[:, o:o + 8], ALU.add))
            settle()
            step(v.tensor_scalar(in_half[:], in_bias[:], 0.5, None, ALU.mult))
            for c in range(2):
                o, _ = COLS["conv_w"]
                step(v.tensor_scalar(taps[:, 4 * c:4 * c + 4], col[:, o + 4 * c:o + 4 * c + 4], V("skip", c), None,
                                     ALU.mult))
                step(v.tensor_scalar(conv_b[:, c:c + 1], V("conv_b", c), V("skip", c), 2.0, ALU.mult, ALU.mult))
            step(v.tensor_scalar(w_out[:], w_out[:], 0.25, None, ALU.mult))
            v.wait_ge(prep_act, 1)
            step(v.tensor_scalar(decay[:], decay[:], 0.5, 0.5, ALU.mult, ALU.add))
            step(v.tensor_scalar(posb[:], RR("pos"), V("tok_b"), None, ALU.add))
            settle()
            step(v.tensor_tensor(posb[:, 0:1], RR("pos")[:, 0:1], V("cls"), ALU.add))
            settle()
            for s in range(2):
                step(v.tensor_copy(four(h0[s][:])[:, :, 0], posb[:, 0:1].to_broadcast([128, IMGS])))
            for r in range(3):
                step(v.tensor_scalar(w_mr[:, r, :], w_mr[:, r, :], 1.0 / (3 * 2 ** r), None, ALU.mult))
            step(v.tensor_tensor(tiny[:, 0:1], V("mr_b", 0), V("mr_b", 1), ALU.add))
            settle()
            step(v.tensor_tensor(tiny[:, 1:2], tiny[:, 0:1], V("mr_b", 2), ALU.add))
            settle()
            step(v.tensor_scalar(mr_bias[:], tiny[:, 1:2], 1.0 / 3, None, ALU.mult))
            step(v.tensor_reduce(tiny[:, 2:3], RR("alpha"), AX_X, ALU.max))
            settle()
            step(v.tensor_scalar(alpha[:], RR("alpha"), tiny[:, 2:3], None, ALU.subtract))
            settle()
            v.sem_inc(consts_ready, 1)
            v.wait_ge(prep_act, 2)
            step(v.tensor_reduce(tiny[:, 3:4], alpha[:], AX_X, ALU.add))
            settle()
            step(v.reciprocal(tiny[:, 4:5], tiny[:, 3:4]))
            settle()
            step(v.tensor_scalar(alpha[:], alpha[:], tiny[:, 4:5], None, ALU.mult))
            settle()
            v.sem_inc(consts_ready, 1)

        def a_prep_scalar(act):
            act.wait_ge(loaded, 16 * NLOADS)
            o, _ = COLS["state_mix"]
            nc.scalar.activation(decay[:], col[:, o:o + 2], ACT.Tanh, scale=0.5).then_inc(prep_act, 1)
            act.wait_ge(consts_ready, 1)
            nc.scalar.activation(alpha[:], alpha[:], ACT.Exp).then_inc(prep_act, 1)

        def a_prep_tensor(pe):
            pe.wait_ge(loaded, 16 * NLOADS)
            for u in range(8):
                last = nc.tensor.matmul(P[0][0][:, 0, u:u + 1], w_in[:, u, :], V("ln_b"), start=True, stop=True)
            last.then_inc(prep_pe, 1)

        def a_tensor(pe):
            a_prep_tensor(pe)
            pe.wait_ge(consts_ready, 2)
            with pe.Fori(0, ITERS) as i:
                for s in range(2):
                    pe.wait_ge(x_landed[s], 16 * i + 16)
                    pe.wait_ge(slots_ready[s], i)
                    for g in range(2):
                        for k in range(KC):
                            last = nc.tensor.matmul(P[s][0][:, g, 0:2 * NPATCH], w_tok[:, k, :],
                                                    xin[s][:, k, g * 2 * NPATCH:(g + 1) * 2 * NPATCH],
                                                    start=(k == 0), stop=(k == KC - 1))
                    last.then_inc(tok_done[s], 1)
                for s in range(2):
                    pe.wait_ge(embedded[s], 2 * i + 2)
                    pe.wait_ge(rows_ready[s], 2 * i)
                    ln_pe(pe, s, h0[s][:], LNA * i)
                for s in range(2):
                    ln_pe_var(pe, s, sq[s][:], LNA * i)
                for u in range(8):
                    for s in range(2):
                        if u == 0:
                            pe.wait_ge(normed[s], 2 * i + 2)
                        if u >= 2:
                            pe.wait_ge(unit_act[s], 8 * i + u - 1)
                        for g in range(2):
                            last = nc.tensor.matmul(P[s][u % 2][:, g, 0:T2], w_in[:, u, :], two(xn2[s][:])[:, g, :],
                                                    start=True, stop=True)
                        last.then_inc(unit_done[s], 1)
                for s in range(2):
                    pe.wait_ge(mix_step[s], 2 * MIX * (i + 1))
                    pe.wait_ge(unit_act[s], 8 * i + 8)
                    for g in range(2):
                        for c in range(2):
                            last = nc.tensor.matmul(P[s][0][:, g, 0:T2], w_out[:, c, :], two(acc[s][c][:])[:, g, :],
                                                    start=(c == 0), stop=(c == 1))
                    last.then_inc(out_done[s], 1)
                for s in range(2):
                    pe.wait_ge(h1_ready[s], i + 1)
                    ln_pe(pe, s, h1[s][:], LNA * i + 1)
                for s in range(2):
                    ln_pe_var(pe, s, sq[s][:], LNA * i + 1)
                for s in range(2):
                    pe.wait_ge(ffn_step[s], FFN * i + 3)
                    for g in range(2):
                        dst = P[s][0][:, g, 0:T2]
                        nc.tensor.matmul(dst, w_mr[:, 0, :], two(x0[s][:])[:, g, :], start=True, stop=False)
                        nc.tensor.matmul(dst, w_mr[:, 1, :], two(pool2[s][:])[:, g, :].unsqueeze(2)
                                         .to_broadcast([128, T2 // 2, 2]), start=False, stop=False)
                        last = nc.tensor.matmul(dst, w_mr[:, 2, :], two(pool4[s][:])[:, g, :].unsqueeze(2)
                                                .to_broadcast([128, T2 // 4, 4]), start=False, stop=True)
                    last.then_inc(mr_done[s], 1)
                for s in range(2):
                    pe.wait_ge(ffn_step[s], FFN * i + 4)
                    ln_pe(pe, s, pre[s][:], LNA * i + 2)
                for s in range(2):
                    ln_pe_var(pe, s, sq[s][:], LNA * i + 2)
                for k in range(3):
                    for s in range(2):
                        if k == 0:
                            pe.wait_ge(ffn_step[s], FFN * i + 6)
                        if k == 2:
                            pe.wait_ge(gelu_done[s], 3 * i + 1)
                        for g in range(2):
                            last = nc.tensor.matmul(P[s][k % 2][:, g, 0:T2], w_mv[:, k, :], two(x1[s][:])[:, g, :],
                                                    start=True, stop=True)
                        last.then_inc(mv_done[s], 1)
                for s in range(2):
                    pe.wait_ge(ffn_step[s], FFN * i + 9)
                    ln_pe(pe, s, pre[s][:], LNA * i + 3)
                for s in range(2):
                    ln_pe_var(pe, s, sq[s][:], LNA * i + 3)
                for s in range(2):
                    pe.wait_ge(ffn_step[s], FFN * i + 11)
                    for g in range(NG):
                        last = nc.tensor.matmul(P[s][0][0:G, 0, g * E:(g + 1) * E], x2[s][:, g * G:(g + 1) * G],
                                                w_gate[:], start=True, stop=True)
                    last.then_inc(logits_done[s], 1)
                    for g in range(NG):
                        last = nc.tensor.transpose(P[s][1][0:G, g // 4, (g % 4) * 128:(g % 4 + 1) * 128],
                                                   x2[s][:, g * G:(g + 1) * G], C("ident"))
                    last.then_inc(turned[s], 1)
                for s in range(2):
                    pe.wait_ge(route_step[s], ROUTE * i + 13)
                    pe.wait_ge(chosen_new, 2 * i + s)
                    dst = P[s][0][0:G, 1, 0:NG * E].rearrange("p (g e) -> p g e", e=E)
                    nc.tensor.matmul(dst, C("before")[0:G, :], picks[s][:], start=True, stop=False)
                    for g in range(NG - 1):
                        nc.tensor.matmul(dst[:, g + 1:NG, :], C("ones")[0:G, 0:G],
                                         picks[s][:, g:g + 1, :].to_broadcast([G, NG - 1 - g, E]),
                                         start=False, stop=False)
                    nc.tensor.matmul(dst, C("ones")[0:G, 0:G], chosen[:].unsqueeze(1).to_broadcast([G, NG, E]),
                                     start=False, stop=True).then_inc(rank_done[s], 1)

        ROUTE = 25

        def a_scalar(act):
            a_prep_scalar(act)
            act.wait_ge(consts_ready, 2)
            act.preload_act_table_set("natural_log_exp_and_others")
            with act.Fori(0, ITERS) as i:
                for s in range(2):
                    ln_act_square(act, s, sq[s][:], LNA * i)
                for s in range(2):
                    act.wait_ge(variance[s], LNA * i + 1)
                    nc.scalar.activation(two(ra[s][:]), pv(s, 0), ACT.Ln, bias=eps_col[:, 0:1]).then_inc(logvar[s], 1)
                    nc.scalar.activation(two(rb[s][:]), pv(s, 0), ACT.Ln, bias=eps_col[:, 1:2], scale=1.0 + EPS
                                         ).then_inc(logvar[s], 1)
                    act.wait_ge(logvar[s], RSA * i + 1)
                    nc.scalar.activation(ra[s][:], ra[s][:], ACT.Exp, scale=-0.5).then_inc(rstd[s], 1)
                    act.wait_ge(logvar[s], RSA * i + 2)
                    nc.scalar.activation(rb[s][:], rb[s][:], ACT.Exp, scale=-0.5).then_inc(rstd[s], 1)
                for u in range(8):
                    for s in range(2):
                        act.wait_ge(unit_done[s], 8 * i + u + 1)
                        half = u not in DRIVE
                        ins = nc.scalar.activation(two(unit[s][u][:]), pv(s, u % 2), ACT.Tanh,
                                                   bias=(in_half if half else in_bias)[:, u:u + 1],
                                                   scale=0.5 if half else 1.0)
                        if u in PROJ:
                            ins = nc.scalar.activation(two(zproj[s][u - PROJ[0]][:]), pv(s, u % 2), ACT.Identity,
                                                       bias=in_bias[:, u:u + 1])
                        ins.then_inc(unit_act[s], 1)
                act.preload_act_table_set("natural_log_exp_and_others")
                for n in (1, 2):
                    for s in range(2):
                        ln_act_square(act, s, sq[s][:], LNA * i + n)
                    for s in range(2):
                        ln_act_rstd(act, s, ra[s][:], LNA * i + n, RSA * i + n + 1)
                for k in range(3):
                    for s in range(2):
                        act.wait_ge(mv_done[s], 3 * i + k + 1)
                        nc.scalar.activation(two(view[s][k][:]), pv(s, k % 2), ACT.Gelu_apprx_tanh,
                                             bias=V("mv_b", k)).then_inc(gelu_done[s], 1)
                act.preload_act_table_set("natural_log_exp_and_others")
                for s in range(2):
                    ln_act_square(act, s, sq[s][:], LNA * i + 3)
                for s in range(2):
                    ln_act_rstd(act, s, ra[s][:], LNA * i + 3, RSA * i + 4)
                for s in range(2):
                    act.wait_ge(turned[s], i + 1)
                    act.wait_ge(scattered[s], 16 * 2 * NG * i)
                    for b, (g0, g1) in enumerate(((0, 4), (4, NG))):
                        nc.scalar.activation(rows[s][:, g0:g1, :].rearrange("p g d -> p (g d)"),
                                             P[s][1][0:G, b, 0:(g1 - g0) * 128], ACT.Copy).then_inc(rows_ready[s], 1)
                for s in range(2):
                    act.wait_ge(route_step[s], ROUTE * i + 14)
                    nc.scalar.activation(wexp[s][:], wexp[s][:], ACT.Exp).then_inc(wexp_done[s], 1)

        def a_vector(v):
            a_prep_vector(v)
            with v.Fori(0, ITERS) as i:
                for s in range(2):
                    v.wait_ge(tok_done[s], i + 1)
                    for g in range(2):
                        v.tensor_tensor(four(h0[s][:])[:, 2 * g:2 * g + 2, 1:S],
                                        P[s][0][:, g, 0:2 * NPATCH].rearrange("p (m n) -> p m n", m=2),
                                        posb[:, 1:S].unsqueeze(1).to_broadcast([128, 2, NPATCH]),
                                        ALU.add).then_inc(embedded[s], 1)
                for s in range(2):
                    v.wait_ge(rstd[s], RSA * i + 1)
                    v.tensor_tensor(two(xn1[s][:]), pv(s, 1), two(ra[s][:]), ALU.mult).then_inc(normed[s], 1)
                    v.wait_ge(rstd[s], RSA * i + 2)
                    v.tensor_tensor(two(xn2[s][:]), pv(s, 1), two(rb[s][:]), ALU.mult).then_inc(normed[s], 1)
                for c in range(2):
                    for s in range(2):
                        v.wait_ge(unit_act[s], 8 * i + PROJ[c] + 1)
                        v.scalar_tensor_tensor(out=pj[s][c][:, :, 3:], in0=four(unit[s][PROJ[c]][:]), scalar=1.0,
                                               in1=four(zproj[s][c][:]), op0=ALU.add, op1=ALU.mult
                                               ).then_inc(mix_step[s], 1)
                    for s in range(2):
                        v.wait_ge(mix_step[s], MIX * (2 * i + c) + 1)
                        v.tensor_scalar(four(acc[s][c][:]), pj[s][c][:, :, 3:], taps[:, 4 * c + 3:4 * c + 4],
                                        conv_b[:, c:c + 1], ALU.mult, ALU.add).then_inc(mix_step[s], 1)
                    for n, tap in enumerate((2, 1, 0)):
                        for s in range(2):
                            v.wait_ge(mix_step[s], MIX * (2 * i + c) + 2 + n)
                            v.scalar_tensor_tensor(out=four(acc[s][c][:]), in0=pj[s][c][:, :, tap:tap + S],
                                                   scalar=taps[:, 4 * c + tap:4 * c + tap + 1],
                                                   in1=four(acc[s][c][:]), op0=ALU.mult, op1=ALU.add
                                                   ).then_inc(mix_step[s], 1)
                    for s in range(2):
                        v.wait_ge(delta_step[s], 4 * i + 2 * c + 2)
                        for m in range(IMGS):
                            v.tensor_tensor_scan(four(unit[s][DRIVE[c]][:])[:, m, :],
                                                 decay[:, c:c + 1].to_broadcast([128, S]),
                                                 four(unit[s][DELTA[c]][:])[:, m, :], 0.0, ALU.mult, ALU.add
                                                 ).then_inc(mix_step[s], 1)
                    for s in range(2):
                        v.wait_ge(mix_step[s], MIX * (2 * i + c) + 5 + IMGS)
                        v.tensor_tensor(acc[s][c][:], acc[s][c][:], unit[s][DRIVE[c]][:], ALU.add
                                        ).then_inc(mix_step[s], 1)
                    for s in range(2):
                        v.wait_ge(mix_step[s], MIX * (2 * i + c) + 6 + IMGS)
                        v.wait_ge(unit_act[s], 8 * i + GATE[c] + 1)
                        v.scalar_tensor_tensor(out=acc[s][c][:], in0=unit[s][GATE[c]][:], scalar=1.0,
                                               in1=acc[s][c][:], op0=ALU.add, op1=ALU.mult).then_inc(mix_step[s], 1)
                for s in range(2):
                    v.wait_ge(out_done[s], i + 1)
                    v.wait_ge(res_done[s], i + 1)
                    v.wait_ge(h1_stored[s], 16 * i)
                    v.scalar_tensor_tensor(out=two(h1[s][:]), in0=pv(s, 0), scalar=V("out_b"), in1=two(res[s][:]),
                                           op0=ALU.add, op1=ALU.add).then_inc(h1_ready[s], 1)
                for s in range(2):
                    v.wait_ge(rstd[s], RSA * i + 3)
                    v.tensor_tensor(two(x0[s][:]), pv(s, 1), two(ra[s][:]), ALU.mult).then_inc(ffn_step[s], 1)
                for s in range(2):
                    v.wait_ge(ffn_step[s], FFN * i + 1)
                    p2 = x0[s][:].rearrange("p (n k) -> p n k", k=2)
                    v.tensor_tensor(pool2[s][:], p2[:, :, 0], p2[:, :, 1], ALU.add).then_inc(ffn_step[s], 1)
                for s in range(2):
                    v.wait_ge(ffn_step[s], FFN * i + 2)
                    p4 = pool2[s][:].rearrange("p (n k) -> p n k", k=2)
                    v.tensor_tensor(pool4[s][:], p4[:, :, 0], p4[:, :, 1], ALU.add).then_inc(ffn_step[s], 1)
                for s in range(2):
                    v.wait_ge(mr_done[s], i + 1)
                    v.scalar_tensor_tensor(out=two(pre[s][:]), in0=pv(s, 0), scalar=mr_bias[:, 0:1],
                                           in1=two(x0[s][:]), op0=ALU.add, op1=ALU.add).then_inc(ffn_step[s], 1)
                for s in range(2):
                    v.wait_ge(rstd[s], RSA * i + 4)
                    v.scalar_tensor_tensor(out=two(x1[s][:]), in0=pv(s, 1), scalar=V("ln1_g"), in1=two(ra[s][:]),
                                           op0=ALU.mult, op1=ALU.mult).then_inc(ffn_step[s], 1)
                for s in range(2):
                    v.wait_ge(ffn_step[s], FFN * i + 5)
                    v.tensor_scalar(x1[s][:], x1[s][:], V("ln1_b"), None, ALU.add).then_inc(ffn_step[s], 1)
                for k in range(3):
                    for s in range(2):
                        v.wait_ge(gelu_done[s], 3 * i + k + 1)
                        if k:
                            v.wait_ge(ffn_step[s], FFN * i + 6 + k)
                        v.scalar_tensor_tensor(out=pre[s][:], in0=view[s][k][:], scalar=alpha[:, k:k + 1],
                                               in1=(pre if k else x1)[s][:], op0=ALU.mult, op1=ALU.add
                                               ).then_inc(ffn_step[s], 1)
                for s in range(2):
                    v.wait_ge(rstd[s], RSA * i + 5)
                    v.wait_ge(x2_stored[s], 16 * i)
                    v.scalar_tensor_tensor(out=two(x2[s][:]), in0=pv(s, 1), scalar=V("ln2_g"), in1=two(ra[s][:]),
                                           op0=ALU.mult, op1=ALU.mult).then_inc(ffn_step[s], 1)
                for s in range(2):
                    v.wait_ge(ffn_step[s], FFN * i + 10)
                    v.tensor_scalar(x2[s][:], x2[s][:], V("ln2_b"), None, ALU.add).then_inc(ffn_step[s], 1)
                a_route(v, i)

        def a_route(v, i):
            def over_e(ap):
                return ap.unsqueeze(2).to_broadcast([G, NG, E])

            rev = R("rev")[0:G, :].unsqueeze(1).to_broadcast([G, NG, E])
            done = [[0, 0]]

            def both(make):
                n = done[0][0]
                for s in range(2):
                    if n:
                        v.wait_ge(route_step[s], ROUTE * i + n)
                    make(s).then_inc(route_step[s], 1)
                done[0][0] += 1

            for s in range(2):
                v.wait_ge(logits_done[s], i + 1)
                v.tensor_tensor(logit[s][:], P[s][0][0:G, 0, 0:NG * E].rearrange("p (g e) -> p g e", e=E),
                                RR("gate_b")[0:G, :].unsqueeze(1).to_broadcast([G, NG, E]), ALU.add
                                ).then_inc(route_step[s], 1)
            done[0][0] = 1
            for top, pick, src in ((top1, pick1, logit), (top2, pick2, lmask)):
                both(lambda s: v.tensor_reduce(top[s][:], src[s][:], AX_X, ALU.max))
                both(lambda s: v.tensor_tensor(cand[s][:], src[s][:], over_e(top[s][:]), ALU.is_equal))
                both(lambda s: v.tensor_tensor(cand[s][:], cand[s][:], rev, ALU.mult))
                both(lambda s: v.tensor_reduce(best[s][:], cand[s][:], AX_X, ALU.max))
                both(lambda s: v.tensor_tensor(pick[s][:], cand[s][:], over_e(best[s][:]), ALU.is_equal))
                if top is top1:
                    both(lambda s: v.scalar_tensor_tensor(out=lmask[s][:], in0=pick1[s][:], scalar=-3e38,
                                                          in1=logit[s][:], op0=ALU.mult, op1=ALU.add))
            both(lambda s: v.tensor_tensor(picks[s][:], pick1[s][:], pick2[s][:], ALU.add))
            both(lambda s: v.tensor_tensor(wexp[s][:], top2[s][:], top1[s][:], ALU.subtract))
            both(lambda s: v.tensor_reduce(newly[s][:], picks[s][:].rearrange("p g e -> p e g"), AX_X, ALU.add))
            for s in range(2):
                v.wait_ge(wexp_done[s], i + 1)
            both(lambda s: v.tensor_scalar(wsum[s][:], wexp[s][:], 1.0, None, ALU.add))

            def at(tile, s, choice):
                return tile[:, bass.DynSlice(i * 4 * NG + s * 2 * NG + choice * NG, NG)]

            both(lambda s: v.reciprocal(wsum[s][:], wsum[s][:]))
            both(lambda s: v.tensor_copy(at(weights, s, 0), wsum[s][:]))
            both(lambda s: v.tensor_tensor(at(weights, s, 1), wexp[s][:], wsum[s][:], ALU.mult))
            for s in range(2):
                v.wait_ge(rank_done[s], i + 1)
                v.wait_ge(chosen_new, 2 * i + s)
                v.wait_ge(route_step[s], ROUTE * i + 19)
                v.tensor_tensor(chosen[:], chosen[:], newly[s][:], ALU.add).then_inc(chosen_new, 1)
                v.tensor_tensor(cand[s][:], P[s][0][0:G, 1, 0:NG * E].rearrange("p (g e) -> p g e", e=E),
                                R("first")[0:G, :].unsqueeze(1).to_broadcast([G, NG, E]), ALU.add
                                ).then_inc(route_step[s], 1)
            done[0][0] = 20
            for choice, pick in ((0, pick1), (1, pick2)):
                both(lambda s: v.tensor_tensor(logit[s][:], cand[s][:], pick[s][:], ALU.mult))
                both(lambda s: v.tensor_reduce(slot[s][:, choice * NG:(choice + 1) * NG], logit[s][:], AX_X,
                                               ALU.add))
            both(lambda s: v.tensor_copy(slots[:, bass.DynSlice(i * 4 * NG + s * 2 * NG, 2 * NG)], slot[s][:]))
            assert done[0][0] == ROUTE
            for s in range(2):
                v.wait_ge(scattered[s], 16 * 2 * NG * i)
                v.tensor_copy(slot_i[s][:], slot[s][:]).then_inc(slots_ready[s], 1)

        def a_pool(pool):
            with pool.Fori(0, ITERS) as i:
                for s in range(2):
                    pool.wait_ge(embedded[s], 2 * i + 2)
                    pool.wait_ge(normed[s], 2 * i + 1)
                    pool.tensor_tensor(res[s][:], h0[s][:], xn1[s][:], ALU.add).then_inc(res_done[s], 1)
                for c in range(2):
                    for s in range(2):
                        hold(pool, unit_act[s], 8 * i + DELTA[c] + 1)
                        pool.tensor_scalar(unit[s][DELTA[c]][:], unit[s][DELTA[c]][:], 1.0, 2e-4, ALU.add, ALU.max
                                           ).then_inc(delta_step[s], 1)
                    for s in range(2):
                        pool.wait_ge(unit_act[s], 8 * i + DRIVE[c] + 1)
                        pool.wait_ge(delta_step[s], 4 * i + 2 * c + 1)
                        pool.tensor_tensor(unit[s][DELTA[c]][:], unit[s][DELTA[c]][:], unit[s][DRIVE[c]][:], ALU.mult
                                           ).then_inc(delta_step[s], 1)
                for s in range(2):
                    hold(pool, rows_ready[s], 2 * i + 2)
                    hold(pool, slots_ready[s], i + 1)
                    for choice in range(2):
                        for g in range(NG):
                            n = choice * NG + g
                            pool.indirect_dma_start(
                                out=expert_in[:, :],
                                out_offset=bass.IndirectOffsetOnAxis(ap=slot_i[s][:, n:n + 1], axis=0),
                                in_=rows[s][:, g, :], in_offset=None).then_inc(scattered[s], 16)
            for s in range(2):
                pool.wait_ge(scattered[s], 16 * 2 * NG * ITERS)

        mem_a.close()

        mem_b = ExitStack()
        WCOLS = FF + FC * D + FC + 1
        w_blk = pair("w_blk", [128, WCOLS], F32, mem_b)
        rows_in, rows_out = pair("rows_in", [128, CB, D], F32, mem_b), pair("rows_out", [128, CB, D], F32, mem_b)
        x_t, y_t = pair("x_t", [128, BLK], F32, mem_b), pair("y_t", [128, BLK], F32, mem_b)
        hid = pair("hid", [128, FC, BLK], F32, mem_b)
        zeros = sb("zeros", [128, CB * D], F32, mem_b)
        count = sb("count", [128, E], F32, mem_b)
        nblk, ends, ones_e = (sb("nblk", [128, E], F32, mem_b), sb("ends", [128, E], F32, mem_b),
                              sb("ones_e", [128, E], F32, mem_b))
        over = sb("over", [128, E, KMAX], F32, mem_b)
        past = sb("past", [1, NB, E], F32, mem_b)
        blk_e, blk_done = sb("blk_e", [1, NB], F32, mem_b), sb("blk_done", [1, NB], F32, mem_b)
        shift = sb("shift", [128, E], F32, mem_b)
        moved = sb("moved", [G, ITERS * 4 * NG], F32, mem_b)

        count_done, table_step, table_ready = sem("count_done"), sem("table_step"), sem("table_ready")
        out_rows_step, zero_filled = sem("out_rows_step"), sem("zero_filled")
        w_landed, r_landed, block_stored = sems("w_landed"), sems("r_landed"), sems("block_stored")
        in_turned, xt_ready, hid_done, hid_ready = (sems("in_turned"), sems("xt_ready"), sems("hid_done"),
                                                    sems("hid_ready"))
        y_done, yt_ready, out_turned, rows_out_ready = (sems("y_done"), sems("yt_ready"), sems("out_turned"),
                                                        sems("rows_out_ready"))
        TB = [P[s][0][:, 0, :] for s in range(2)]
        HB = [[P[s][0][:, 1, :], P[s][1][:, 0, :]] for s in range(2)]
        YB = [P[s][1][:, 1, :] for s in range(2)]

        def b_sync(sp):
            sp.wait_ge(table_ready, 1)
            for s in range(2):
                sp.wait_ge(scattered[s], 16 * 2 * NG * ITERS)
            for e in range(E + 1):
                if e < E:
                    n = sp.value_load(tails[0:1, e:e + 1], min_val=0, max_val=tokens)
                    at = bass.DynSlice(n + e * REGION, BLK)
                else:
                    at = slice(E * REGION, E * REGION + BLK)
                sp.dma_start(expert_in[at, :].rearrange("(p c) d -> p (c d)", c=CB), zeros[:]
                             ).then_inc(zero_filled, 16)
            sp.wait_ge(zero_filled, 16 * (E + 1))

            def load(n, s, k, first):
                if not first:
                    hold(sp, yt_ready[s], k)
                e = sp.value_load(table[0:1, bass.DynSlice(NB + n, 1)], min_val=0, max_val=E - 1)
                sp.dma_start(w_blk[s][:], a["w_exp"][bass.DynSlice(e * 128, 128), :]).then_inc(w_landed[s], 16)
                r = sp.value_load(table[0:1, bass.DynSlice(n, 1)], min_val=0, max_val=E * REGION)
                sp.dma_start(rows_in[s][:].rearrange("p c d -> p (c d)"),
                             expert_in[bass.DynSlice(r, BLK), :].rearrange("(p c) d -> p (c d)", c=CB)
                             ).then_inc(r_landed[s], 16)

            def store(n, s, k):
                hold(sp, rows_out_ready[s], k + 1)
                sp.dma_start(expert_out[bass.DynSlice(n * BLK, BLK), :].rearrange("(p c) d -> p (c d)", c=CB),
                             rows_out[s][:].rearrange("p c d -> p (c d)")).then_inc(block_stored[s], 16)

            for s in range(2):
                load(s, s, 0, True)
            with sp.Fori(1, NB // 2) as i:
                for s in range(2):
                    load(2 * i + s, s, i, False)
                    store(2 * i + s - 2, s, i - 1)
            for s in range(2):
                store(NB - 2 + s, s, NB // 2 - 1)
            for s in range(2):
                sp.wait_ge(block_stored[s], 16 * (NB // 2))

        def b_tensor(pe):
            pe.wait_ge(chosen_new, 2 * ITERS)
            for s in range(2):
                pe.wait_ge(rows_ready[s], 2 * ITERS)
                pe.wait_ge(slots_ready[s], ITERS)
            nc.tensor.matmul(YB[0][:, 0:E], C("ones")[0:G, :], chosen[:], start=True, stop=True).then_inc(count_done, 1)

            def turn_in(s, k):
                pe.wait_ge(r_landed[s], 16 * k + 16)
                for c in range(CB):
                    last = nc.tensor.transpose(TB[s][:, c * 128:(c + 1) * 128], rows_in[s][:, c, :], C("ident"))
                last.then_inc(in_turned[s], 1)

            def hidden(s, k, c):
                if c == 0:
                    pe.wait_ge(w_landed[s], 16 * k + 16)
                    pe.wait_ge(xt_ready[s], k + 1)
                if c >= 2:
                    pe.wait_ge(hid_ready[s], FC * k + c - 1)
                nc.tensor.matmul(HB[s][c % 2], w_blk[s][:, c * 128:(c + 1) * 128], x_t[s][:], start=True, stop=True
                                 ).then_inc(hid_done[s], 1)

            def outputs(s, k):
                for c in range(FC):
                    pe.wait_ge(hid_ready[s], FC * k + c + 1)
                    last = nc.tensor.matmul(YB[s], w_blk[s][:, FF + c * D:FF + (c + 1) * D], hid[s][:, c, :],
                                            start=(c == 0), stop=(c == FC - 1))
                last.then_inc(y_done[s], 1)

            def turn_out(s, k):
                pe.wait_ge(yt_ready[s], k + 1)
                for c in range(CB):
                    last = nc.tensor.transpose(TB[s][:, c * 128:(c + 1) * 128], y_t[s][:, c * 128:(c + 1) * 128],
                                               C("ident"))
                last.then_inc(out_turned[s], 1)

            def block(s, k, first=False, final=False):
                hidden(s, k, 0)
                hidden(s, k, 1)
                if not first:
                    turn_out(1 - s, k - 1 + s)
                hidden(s, k, 2)
                hidden(s, k, 3)
                if not final:
                    if not first:
                        pe.wait_ge(rows_out_ready[1 - s], k + s)
                    turn_in(1 - s, k + s)
                outputs(s, k)

            pe.wait_ge(table_ready, 1)
            turn_in(0, 0)
            block(0, 0, first=True)
            block(1, 0)
            with pe.Fori(1, NB // 2 - 1) as i:
                block(0, i)
                block(1, i)
            block(0, NB // 2 - 1)
            block(1, NB // 2 - 1, final=True)
            turn_out(1, NB // 2 - 1)

        def b_scalar(act):
            act.preload_act_table(ACT.Gelu_apprx_tanh)
            with act.Fori(0, NB // 2) as i:
                for s in range(2):
                    for c in range(FC):
                        act.wait_ge(hid_done[s], FC * i + c + 1)
                        if c == 0:
                            act.wait_ge(y_done[s], i)
                        nc.scalar.activation(hid[s][:, c, :], HB[s][c % 2], ACT.Gelu_apprx_tanh,
                                             bias=w_blk[s][:, FF + FC * D + c:FF + FC * D + c + 1]
                                             ).then_inc(hid_ready[s], 1)

        def b_vector(v):
            n = [0]

            def chain(ins):
                n[0] += 1
                ins.then_inc(table_step, 1)
                v.wait_ge(table_step, n[0])

            chain(v.memset(zeros[:], 0.0))
            chain(v.memset(ones_e[:], 1.0))
            v.wait_ge(count_done, 1)
            chain(v.tensor_copy(count[:], YB[0][:, 0:E]))
            chain(v.tensor_tensor(over[:], count[:].unsqueeze(2).to_broadcast([128, E, KMAX]),
                                  R("kblk").unsqueeze(1).to_broadcast([128, E, KMAX]), ALU.is_gt))
            chain(v.tensor_reduce(nblk[:], over[:], AX_X, ALU.add))
            chain(v.tensor_tensor_scan(ends[:], ones_e[:], nblk[:], 0.0, ALU.mult, ALU.add))
            blk = R("blk")[0:1, :]
            chain(v.tensor_tensor(past[:], blk.unsqueeze(2).to_broadcast([1, NB, E]),
                                  ends[0:1, :].unsqueeze(1).to_broadcast([1, NB, E]), ALU.is_ge))
            chain(v.tensor_reduce(blk_e[:], past[:], AX_X, ALU.add))
            chain(v.tensor_tensor(past[:], past[:], nblk[0:1, :].unsqueeze(1).to_broadcast([1, NB, E]), ALU.mult))
            chain(v.tensor_reduce(blk_done[:], past[:], AX_X, ALU.add))
            chain(v.tensor_tensor(blk_done[:], blk, blk_done[:], ALU.subtract))
            chain(v.tensor_scalar(blk_done[:], blk_done[:], float(BLK), None, ALU.mult))
            chain(v.scalar_tensor_tensor(out=blk_done[:], in0=blk_e[:], scalar=float(REGION), in1=blk_done[:],
                                         op0=ALU.mult, op1=ALU.add))
            chain(v.tensor_scalar(table[:, 0:NB], blk_done[:], float(E * REGION), None, ALU.min))
            chain(v.tensor_scalar(table[:, NB:2 * NB], blk_e[:], float(E - 1), None, ALU.min))
            v.tensor_copy(tails[:], count[0:1, :]).then_inc(table_ready, 1)
            chain(v.tensor_tensor(shift[:], ends[:], nblk[:], ALU.subtract))
            chain(v.tensor_scalar(shift[:], shift[:], float(BLK), None, ALU.mult))
            chain(v.tensor_tensor(shift[:], shift[:], R("first"), ALU.subtract))
            chain(v.tensor_tensor(over[:, 1:E, 0], shift[:, 1:E], shift[:, 0:E - 1], ALU.subtract))
            chain(v.tensor_scalar(out_rows[:], slots[:], shift[0:G, 0:1], None, ALU.add))
            for e in range(1, E):
                chain(v.tensor_scalar(moved[:], slots[:], float(e * REGION), over[0:G, e:e + 1, 0], ALU.is_ge, ALU.mult))
                chain(v.tensor_tensor(out_rows[:], out_rows[:], moved[:], ALU.add))
            v.sem_inc(out_rows_step, 1)

            def take_in(s, k):
                v.wait_ge(in_turned[s], k + 1)
                v.tensor_copy(x_t[s][:], TB[s]).then_inc(xt_ready[s], 1)

            def block(s, k, first=False, final=False):
                if not first:
                    v.wait_ge(out_turned[1 - s], k + s)
                    v.wait_ge(block_stored[1 - s], 16 * (k - 1 + s))
                    v.tensor_copy(rows_out[1 - s][:].rearrange("p c d -> p (c d)"), TB[1 - s]
                                  ).then_inc(rows_out_ready[1 - s], 1)
                if not final:
                    take_in(1 - s, k + s)
                v.wait_ge(y_done[s], k + 1)
                v.tensor_scalar(y_t[s][:], YB[s], w_blk[s][:, WCOLS - 1:WCOLS], None, ALU.add
                                ).then_inc(yt_ready[s], 1)

            take_in(0, 0)
            block(0, 0, first=True)
            block(1, 0)
            with v.Fori(1, NB // 2 - 1) as i:
                block(0, i)
                block(1, i)
            block(0, NB // 2 - 1)
            block(1, NB // 2 - 1, final=True)
            v.wait_ge(out_turned[1], NB // 2)
            v.wait_ge(block_stored[1], 16 * (NB // 2 - 1))
            v.tensor_copy(rows_out[1][:].rearrange("p c d -> p (c d)"), TB[1]).then_inc(rows_out_ready[1], 1)

        mem_b.close()

        mem_c = ExitStack()

        def pair_c(name, shape, dt=F32):
            return pair(name, shape, dt, mem_c)

        w_qkv, w_att, w_g = (sb("w_qkv", [128, 3 * D], F32, mem_c), sb("w_att", [128, D], F32, mem_c),
                             sb("w_g", [128, E2], F32, mem_c))
        q_half = sb("q_bias", [128, 1], F32, mem_c)
        h1c, x2c = pair_c("h1c", [128, T]), pair_c("x2c", [128, T])
        ycho = pair_c("ycho", [G, 2 * NG, D])
        place, wdiag = pair_c("place", [G, 2 * NG], I32), pair_c("wdiag", [G, 2 * NG, G])
        sqc, rc, prec = pair_c("sqc", [128, T]), pair_c("rc", [128, T]), pair_c("prec", [128, T])
        h2, h3, xm = pair_c("h2", [128, T]), pair_c("h3", [128, T]), pair_c("xm", [128, T])
        xpad, kpad = pair_c("xpad", [128, IMGS, KPAD]), pair_c("kpad", [128, IMGS, KPAD])
        qs = pair_c("qs", [128, T])
        val = pair_c("val", [KW, IMGS * NWIN, D])
        qdiag = [[sb(f"qdiag{s}{k}", [128, UB, HEADS, QB], F32, mem_c) for k in range(2)] for s in range(2)]
        sc, ex = pair_c("sc", [128, UB, KW]), pair_c("ex", [128, UB, KW])
        smax, ssum = pair_c("smax", [128, UB]), pair_c("ssum", [128, UB])
        qsel = pair_c("qsel", [128, UB, QB])
        ex_t = pair_c("ex_t", [KW, UB, 128])
        own = pair_c("own", [128, UB, 128])
        att = pair_c("att", [128, T])
        means = pair_c("means", [128, IMGS])
        l16, c16, p16 = (pair_c("l16", [1, IMGS, E2]), pair_c("c16", [1, IMGS, E2]), pair_c("p16", [1, IMGS, E2]))
        m16, b16, g16 = pair_c("m16", [1, IMGS]), pair_c("b16", [1, IMGS]), pair_c("g16", [1, IMGS])
        pick_i = pair_c("pick_i", [1, IMGS], I32)
        gate_bc = pair_c("gate_bc", [128, IMGS])
        wsel = pair_c("wsel", [128, IMGS, D + 1])
        outs = pair_c("outs", [128, T])

        loaded_c, c_ready = sem("loaded_c"), sem("c_ready")
        h_landed, choice_step, gathered = sems("h_landed"), sems("choice_step"), sems("gathered")
        moe_done, trunk_step = sems("moe_done"), sems("trunk_step")
        qk_done, qk_ready = sems("qk_done"), sems("qk_ready")
        val_done, val_ready, qdiag_ready = sems("val_done"), sems("val_ready"), sems("qdiag_ready")
        scores_done, soft_step, ex_ready = sems("scores_done"), sems("soft_step"), sems("ex_ready")
        ext_done, ext_ready, pv_done, own_ready = sems("ext_done"), sems("ext_ready"), sems("pv_done"), sems("own_ready")
        heads_done, att_ready, proj_done = sems("heads_done"), sems("att_ready"), sems("proj_done")
        tail_step, router_pe, pick_step, pick_exp = (sems("tail_step"), sems("router_pe"), sems("pick_step"),
                                                     sems("pick_exp"))
        gate_ready, wsel_landed = sems("gate_ready"), sems("wsel_landed")
        last_done, out_step, out_stored = sems("last_done"), sems("out_step"), sems("out_stored")
        LNC = 3
        LN0 = LNA * ITERS
        RS0 = RSA * ITERS
        TRUNK = 4
        TAIL = 4
        SOFT = 6

        def c_sync(sp):
            for dst, src in ((w_qkv, "w_qkv"), (w_att, "w_att"), (w_g, "w_g")):
                sp.dma_start(dst[:], a[src]).then_inc(loaded_c, 16)
            with sp.Fori(0, ITERS) as i:
                for s in range(2):
                    hold(sp, trunk_step[s], TRUNK * i)
                    sp.dma_start(h1c[s][:], h1_dram[:, a_range(i, s)]).then_inc(h_landed[s], 16)
                    sp.dma_start(x2c[s][:], x2_dram[:, a_range(i, s)]).then_inc(h_landed[s], 16)
                for s in range(2):
                    hold(sp, pick_step[s], PICK * (i + 1))
                    hold(sp, out_step[s], (IMGS + 1) * i)
                    for m in range(IMGS):
                        e = sp.value_load(pick_i[s][0:1, m:m + 1], min_val=0, max_val=E2 - 1)
                        sp.dma_start(wsel[s][:, m, :], a["w_last"][bass.DynSlice(e * 128, 128), :]
                                     ).then_inc(wsel_landed[s], 16)
                for s in range(2):
                    hold(sp, out_step[s], (IMGS + 1) * (i + 1))
                    sp.dma_start(a["out"][:, a_range(i, s)], outs[s][:]).then_inc(out_stored[s], 16)
            for s in range(2):
                sp.wait_ge(out_stored[s], 16 * ITERS)

        def c_pool(pool):
            for s in range(2):
                pool.wait_ge(block_stored[s], 16 * (NB // 2))
            with pool.Fori(0, ITERS) as i:
                for s in range(2):
                    hold(pool, choice_step[s], 2 * i + 1)
                    hold(pool, moe_done[s], i)
                    for n in range(2 * NG):
                        pool.indirect_dma_start(
                            out=ycho[s][:, n, :], out_offset=None, in_=expert_out[:, :],
                            in_offset=bass.IndirectOffsetOnAxis(ap=place[s][:, n:n + 1], axis=0)
                        ).then_inc(gathered[s], 16)
                for u in range(NU):
                    for s in range(2):
                        if u == 0:
                            pool.wait_ge(qk_ready[s], 2 * i + 1)
                        if u >= 2:
                            pool.wait_ge(scores_done[s], NU * i + u - 1)
                        pool.tensor_tensor(
                            qdiag[s][u % 2][:],
                            qs[s][:, u * UB * QB:(u + 1) * UB * QB].rearrange("p (b q) -> p b q", b=UB).unsqueeze(2)
                            .to_broadcast([128, UB, HEADS, QB]),
                            C("head_rows").unsqueeze(1).unsqueeze(3).to_broadcast([128, UB, HEADS, QB]),
                            ALU.mult).then_inc(qdiag_ready[s], 1)

        def c_tensor(pe):
            pe.wait_ge(c_ready, 1)
            for s in range(2):
                pe.wait_ge(rows_out_ready[s], NB // 2)
            with pe.Fori(0, ITERS) as i:
                for s in range(2):
                    pe.wait_ge(gathered[s], 16 * 2 * NG * (i + 1))
                    pe.wait_ge(choice_step[s], 2 * i + 2)
                    pe.wait_ge(gate_ready[s], i)
                    for g in range(NG):
                        dst = P[s][0][:, g // 3, (g % 3) * G:(g % 3 + 1) * G]
                        for choice in range(2):
                            n = choice * NG + g
                            last = nc.tensor.matmul(dst, ycho[s][:, n, :], wdiag[s][:, n, :],
                                                    start=(choice == 0), stop=(choice == 1))
                    last.then_inc(moe_done[s], 1)
                for s in range(2):
                    pe.wait_ge(trunk_step[s], TRUNK * i + 1)
                    pe.wait_ge(out_step[s], (IMGS + 1) * i)
                    ln_pe(pe, s, prec[s][:], LN0 + LNC * i)
                for s in range(2):
                    ln_pe_var(pe, s, sqc[s][:], LN0 + LNC * i)
                for s in range(2):
                    pe.wait_ge(trunk_step[s], TRUNK * i + 3)
                    ln_pe(pe, s, h2[s][:], LN0 + LNC * i + 1)
                for s in range(2):
                    ln_pe_var(pe, s, sqc[s][:], LN0 + LNC * i + 1)
                for k in range(2):
                    for s in range(2):
                        if k == 0:
                            pe.wait_ge(trunk_step[s], TRUNK * i + 4)
                        for g in range(2):
                            last = nc.tensor.matmul(
                                P[s][k][:, g, 0:T2].rearrange("p (m n) -> p m n", m=2), w_qkv[:, k * D:(k + 1) * D],
                                xpad[s][:, 2 * g:2 * g + 2, WIN:WIN + S], start=True, stop=True)
                        last.then_inc(qk_done[s], 1)
                for r in range(NWIN):
                    for s in range(2):
                        if r < 4:
                            pe.wait_ge(qk_ready[s], 2 * i + (1 if r < 2 else 2))
                        else:
                            pe.wait_ge(val_ready[s], NWIN * i + r - 3)
                        for w in range(UB):
                            n = r * UB + w
                            m, j = n // NWIN, n % NWIN
                            last = nc.tensor.matmul(P[s][(r // 2) % 2][0:KW, r % 2, w * D:(w + 1) * D],
                                                    xpad[s][:, m, j * WIN:j * WIN + KW], w_qkv[:, 2 * D:3 * D],
                                                    start=True, stop=True)
                        last.then_inc(val_done[s], 1)

                def scores(s, u):
                    pe.wait_ge(qdiag_ready[s], NU * i + u + 1)
                    if u == 0:
                        pe.wait_ge(val_ready[s], NWIN * (i + 1))
                    else:
                        pe.wait_ge(soft_step[s], SOFT * (NU * i + u - 1) + 1)
                    for b in range(UB):
                        n = u * UB + b
                        m, qb = n // NQB, n % NQB
                        last = nc.tensor.matmul(P[s][0][:, 0, b * KW:(b + 1) * KW],
                                                qdiag[s][u % 2][:, b, :, :].rearrange("p h q -> p (h q)"),
                                                kpad[s][:, m, WIN * (qb // 2):WIN * (qb // 2) + KW],
                                                start=True, stop=True)
                    last.then_inc(scores_done[s], 1)

                for s in range(2):
                    scores(s, 0)
                for u in range(NU):
                    for s in range(2):
                        pe.wait_ge(ex_ready[s], NU * i + u + 1)
                        if u:
                            pe.wait_ge(ext_ready[s], NU * i + u)
                        for b in range(UB):
                            last = nc.tensor.transpose(P[s][0][0:KW, 1, b * 128:(b + 1) * 128], ex[s][:, b, :],
                                                       C("ident"))
                        last.then_inc(ext_done[s], 1)
                    if u + 1 < NU:
                        for s in range(2):
                            scores(s, u + 1)
                    for s in range(2):
                        pe.wait_ge(ext_ready[s], NU * i + u + 1)
                        if u:
                            pe.wait_ge(own_ready[s], NU * i + u)
                        for b in range(UB):
                            n = u * UB + b
                            m, qb = n // NQB, n % NQB
                            last = nc.tensor.matmul(P[s][1][:, 0, b * 128:(b + 1) * 128], ex_t[s][:, b, :],
                                                    val[s][:, m * NWIN + qb // 2, :], start=True, stop=True)
                        last.then_inc(pv_done[s], 1)
                    for s in range(2):
                        pe.wait_ge(own_ready[s], NU * i + u + 1)
                        pe.wait_ge(soft_step[s], SOFT * (NU * i + u + 1))
                        if u:
                            pe.wait_ge(att_ready[s], NU * i + u)
                        for b in range(UB):
                            last = nc.tensor.matmul(P[s][1][:, 1, b * QB:(b + 1) * QB], own[s][:, b, :],
                                                    qsel[s][:, b, :], start=True, stop=True)
                        last.then_inc(heads_done[s], 1)
                for s in range(2):
                    pe.wait_ge(att_ready[s], NU * (i + 1))
                    for g in range(2):
                        last = nc.tensor.matmul(P[s][0][:, g, 0:T2], w_att[:], two(att[s][:])[:, g, :],
                                                start=True, stop=True)
                    last.then_inc(proj_done[s], 1)
                for s in range(2):
                    pe.wait_ge(tail_step[s], TAIL * i + 1)
                    ln_pe(pe, s, h3[s][:], LN0 + LNC * i + 2)
                for s in range(2):
                    ln_pe_var(pe, s, sqc[s][:], LN0 + LNC * i + 2)
                for s in range(2):
                    pe.wait_ge(tail_step[s], TAIL * i + 4)
                    for m in range(IMGS):
                        last = nc.tensor.matmul(P[s][0][0:1, 0, m * E2:(m + 1) * E2], means[s][:, m:m + 1], w_g[:],
                                                start=True, stop=True)
                    last.then_inc(router_pe[s], 1)
                for s in range(2):
                    pe.wait_ge(pick_step[s], PICK * (i + 1))
                    nc.tensor.matmul(P[s][0][:, 0, 128:128 + IMGS], C("ones")[0:1, :], g16[s][:],
                                     start=True, stop=True).then_inc(router_pe[s], 1)
                for s in range(2):
                    pe.wait_ge(wsel_landed[s], 16 * IMGS * (i + 1))
                    for m in range(IMGS):
                        last = nc.tensor.matmul(P[s][1][:, m // 2, (m % 2) * S:(m % 2 + 1) * S], wsel[s][:, m, 0:D],
                                                four(xm[s][:])[:, m, :], start=True, stop=True)
                    last.then_inc(last_done[s], 1)

        PICK = 12

        def c_scalar(act):
            act.preload_act_table_set("natural_log_exp_and_others")
            act.wait_ge(c_ready, 1)
            with act.Fori(0, ITERS) as i:
                for n in range(2):
                    for s in range(2):
                        ln_act_square(act, s, sqc[s][:], LN0 + LNC * i + n)
                    for s in range(2):
                        ln_act_rstd(act, s, rc[s][:], LN0 + LNC * i + n, RS0 + LNC * i + n)
                for s in range(2):
                    act.wait_ge(qk_done[s], 2 * i + 1)
                    nc.scalar.activation(two(qs[s][:]), pv(s, 0), ACT.Identity, bias=q_half[:, 0:1],
                                         scale=float(HD) ** -0.5).then_inc(qk_ready[s], 1)
                for s in range(2):
                    act.wait_ge(qk_done[s], 2 * i + 2)
                    nc.scalar.activation(two_two(kpad[s][:])[:, :, :, WIN:WIN + S], pv4(s, 1), ACT.Identity,
                                         bias=V("k_b")).then_inc(qk_ready[s], 1)
                for r in range(NWIN):
                    for s in range(2):
                        act.wait_ge(val_done[s], NWIN * i + r + 1)
                        nc.scalar.activation(val[s][:, r * UB:(r + 1) * UB, :].rearrange("p w d -> p (w d)"),
                                             P[s][(r // 2) % 2][0:KW, r % 2, :], ACT.Copy).then_inc(val_ready[s], 1)
                for u in range(NU):
                    for s in range(2):
                        act.wait_ge(soft_step[s], SOFT * (NU * i + u) + 3)
                        nc.scalar.activation(ex[s][:], sc[s][:], ACT.Exp).then_inc(ex_ready[s], 1)
                    for s in range(2):
                        act.wait_ge(ext_done[s], NU * i + u + 1)
                        nc.scalar.activation(ex_t[s][:].rearrange("p b r -> p (b r)"), P[s][0][0:KW, 1, :], ACT.Copy
                                             ).then_inc(ext_ready[s], 1)
                    for s in range(2):
                        act.wait_ge(heads_done[s], NU * i + u + 1)
                        nc.scalar.activation(att[s][:, u * UB * QB:(u + 1) * UB * QB], P[s][1][:, 1, 0:UB * QB],
                                             ACT.Identity, bias=V("v_b")).then_inc(att_ready[s], 1)
                for s in range(2):
                    ln_act_square(act, s, sqc[s][:], LN0 + LNC * i + 2)
                for s in range(2):
                    ln_act_rstd(act, s, rc[s][:], LN0 + LNC * i + 2, RS0 + LNC * i + 2)
                for s in range(2):
                    act.wait_ge(pick_step[s], PICK * i + 9)
                    nc.scalar.activation(p16[s][:], l16[s][:], ACT.Exp).then_inc(pick_exp[s], 1)

        def c_vector(v):
            v.wait_ge(loaded_c, 16 * 3)
            for s in range(2):
                v.memset(xpad[s][:], 0.0)
                v.memset(kpad[s][:], 0.0)
            v.tensor_scalar(q_half[:], V("q_b"), float(HD) ** -0.5, None, ALU.mult).then_inc(c_ready, 1)
            v.wait_ge(c_ready, 1)
            v.wait_ge(out_rows_step, 1)
            with v.Fori(0, ITERS) as i:
                for s in range(2):
                    v.wait_ge(gathered[s], 16 * 2 * NG * i)
                    v.tensor_copy(place[s][:], out_rows[:, bass.DynSlice(i * 4 * NG + s * 2 * NG, 2 * NG)]
                                  ).then_inc(choice_step[s], 1)
                for s in range(2):
                    w = weights[:, bass.DynSlice(i * 4 * NG + s * 2 * NG, 2 * NG)]
                    v.wait_ge(moe_done[s], i)
                    v.tensor_tensor(wdiag[s][:], C("ident")[0:G, 0:G].unsqueeze(1).to_broadcast([G, 2 * NG, G]),
                                    w.unsqueeze(2).to_broadcast([G, 2 * NG, G]), ALU.mult).then_inc(choice_step[s], 1)
                for s in range(2):
                    v.wait_ge(moe_done[s], i + 1)
                    v.wait_ge(h_landed[s], 32 * i + 32)
                    v.tensor_tensor(two(prec[s][:]), pv(s, 0), two(x2c[s][:]), ALU.add).then_inc(trunk_step[s], 1)
                for s in range(2):
                    v.wait_ge(rstd[s], RS0 + LNC * i + 1)
                    v.scalar_tensor_tensor(out=two(xm[s][:]), in0=pv(s, 1), scalar=V("ln3_g"), in1=two(rc[s][:]),
                                           op0=ALU.mult, op1=ALU.mult).then_inc(trunk_step[s], 1)
                for s in range(2):
                    v.wait_ge(trunk_step[s], TRUNK * i + 2)
                    v.scalar_tensor_tensor(out=h2[s][:], in0=xm[s][:], scalar=V("ln3_b"), in1=h1c[s][:],
                                           op0=ALU.add, op1=ALU.add).then_inc(trunk_step[s], 1)
                for s in range(2):
                    v.wait_ge(rstd[s], RS0 + LNC * i + 2)
                    v.tensor_tensor(two_two(xpad[s][:])[:, :, :, WIN:WIN + S], pv4(s, 1),
                                    two(rc[s][:]).rearrange("p g (m n) -> p g m n", m=2), ALU.mult
                                    ).then_inc(trunk_step[s], 1)
                for u in range(NU):
                    k = NU * i + u
                    o, _ = cw["band"]
                    b0 = (u * UB) % NQB
                    band = cst[:, o + b0 * KW:o + (b0 + UB) * KW].rearrange("p (b k) -> p b k", b=UB)
                    for s in range(2):
                        v.wait_ge(scores_done[s], k + 1)
                        if u:
                            v.wait_ge(ex_ready[s], k)
                        v.tensor_tensor(sc[s][:], P[s][0][:, 0, 0:UB * KW].rearrange("p (b k) -> p b k", b=UB), band,
                                        ALU.add).then_inc(soft_step[s], 1)
                    for s in range(2):
                        v.wait_ge(soft_step[s], SOFT * k + 1)
                        v.tensor_reduce(smax[s][:], sc[s][:], AX_X, ALU.max).then_inc(soft_step[s], 1)
                    for s in range(2):
                        v.wait_ge(soft_step[s], SOFT * k + 2)
                        v.tensor_tensor(sc[s][:], sc[s][:], smax[s][:].unsqueeze(2).to_broadcast([128, UB, KW]),
                                        ALU.subtract).then_inc(soft_step[s], 1)
                    for s in range(2):
                        v.wait_ge(ex_ready[s], k + 1)
                        v.tensor_reduce(ssum[s][:], ex[s][:], AX_X, ALU.add).then_inc(soft_step[s], 1)
                    for s in range(2):
                        v.wait_ge(soft_step[s], SOFT * k + 4)
                        v.reciprocal(ssum[s][:], ssum[s][:]).then_inc(soft_step[s], 1)
                    for s in range(2):
                        v.wait_ge(soft_step[s], SOFT * k + 5)
                        v.wait_ge(heads_done[s], k)
                        v.tensor_tensor(qsel[s][:], C("query").unsqueeze(1).to_broadcast([128, UB, QB]),
                                        ssum[s][:].unsqueeze(2).to_broadcast([128, UB, QB]), ALU.mult
                                        ).then_inc(soft_step[s], 1)
                    for s in range(2):
                        v.wait_ge(pv_done[s], k + 1)
                        v.tensor_tensor(own[s][:], P[s][1][:, 0, :].rearrange("p (b r) -> p b r", b=UB),
                                        C("head_block").unsqueeze(1).to_broadcast([128, UB, 128]), ALU.mult
                                        ).then_inc(own_ready[s], 1)
                for s in range(2):
                    v.wait_ge(proj_done[s], i + 1)
                    v.scalar_tensor_tensor(out=two(h3[s][:]), in0=pv(s, 0), scalar=V("attn_b"), in1=two(h2[s][:]),
                                           op0=ALU.add, op1=ALU.add).then_inc(tail_step[s], 1)
                for s in range(2):
                    v.wait_ge(rstd[s], RS0 + LNC * i + 3)
                    v.tensor_tensor(two(xm[s][:]), pv(s, 1), two(rc[s][:]), ALU.mult).then_inc(tail_step[s], 1)
                for s in range(2):
                    v.wait_ge(tail_step[s], TAIL * i + 2)
                    v.tensor_reduce(means[s][:], four(xm[s][:]), AX_X, ALU.add).then_inc(tail_step[s], 1)
                for s in range(2):
                    v.wait_ge(tail_step[s], TAIL * i + 3)
                    v.tensor_scalar(means[s][:], means[s][:], 1.0 / S, None, ALU.mult).then_inc(tail_step[s], 1)
                c_pick(v, i)
                for s in range(2):
                    v.wait_ge(router_pe[s], 2 * i + 2)
                    v.tensor_copy(gate_bc[s][:], P[s][0][:, 0, 128:128 + IMGS]).then_inc(gate_ready[s], 1)
                for s in range(2):
                    v.wait_ge(last_done[s], i + 1)
                    v.wait_ge(gate_ready[s], i + 1)
                    v.wait_ge(out_stored[s], 16 * i)
                    for m in range(IMGS):
                        v.tensor_scalar(four(outs[s][:])[:, m, :], P[s][1][:, m // 2, (m % 2) * S:(m % 2 + 1) * S],
                                        wsel[s][:, m, D:D + 1], gate_bc[s][:, m:m + 1], ALU.add, ALU.mult
                                        ).then_inc(out_step[s], 1)
                for s in range(2):
                    v.wait_ge(out_step[s], (IMGS + 1) * i + IMGS)
                    v.tensor_tensor(outs[s][:], outs[s][:], h3[s][:], ALU.add).then_inc(out_step[s], 1)

        def c_pick(v, i):
            done = [0]

            def over(ap):
                return ap.unsqueeze(2).to_broadcast([1, IMGS, E2])

            def both(make):
                for s in range(2):
                    if done[0]:
                        v.wait_ge(pick_step[s], PICK * i + done[0])
                    make(s).then_inc(pick_step[s], 1)
                done[0] += 1

            for s in range(2):
                v.wait_ge(router_pe[s], 2 * i + 1)
            both(lambda s: v.tensor_tensor(l16[s][:], P[s][0][0:1, 0, 0:IMGS * E2].rearrange("p (m e) -> p m e", e=E2),
                                           RR("bg")[0:1, :].unsqueeze(1).to_broadcast([1, IMGS, E2]), ALU.add))
            both(lambda s: v.tensor_reduce(m16[s][:], l16[s][:], AX_X, ALU.max))
            both(lambda s: v.tensor_tensor(c16[s][:], l16[s][:], over(m16[s][:]), ALU.is_equal))
            both(lambda s: v.tensor_tensor(c16[s][:], c16[s][:], R("rev16")[0:1, :].unsqueeze(1)
                                           .to_broadcast([1, IMGS, E2]), ALU.mult))
            both(lambda s: v.tensor_reduce(b16[s][:], c16[s][:], AX_X, ALU.max))
            both(lambda s: v.tensor_scalar(b16[s][:], b16[s][:], -1.0, float(E2), ALU.mult, ALU.add))
            for s in range(2):
                v.wait_ge(wsel_landed[s], 16 * IMGS * i)
            both(lambda s: v.tensor_copy(pick_i[s][:], b16[s][:]))
            both(lambda s: v.tensor_tensor(l16[s][:], l16[s][:], over(m16[s][:]), ALU.subtract))
            both(lambda s: v.tensor_copy(b16[s][:], m16[s][:]))
            for s in range(2):
                v.wait_ge(pick_exp[s], i + 1)
            both(lambda s: v.tensor_reduce(b16[s][:], p16[s][:], AX_X, ALU.add))
            both(lambda s: v.reciprocal(b16[s][:], b16[s][:]))
            for s in range(2):
                v.wait_ge(router_pe[s], 2 * i)
            both(lambda s: v.tensor_copy(g16[s][:], b16[s][:]))
            assert done[0] == PICK

        mem_c.close()

        block = ctx.enter_context(nc.Block())

        @block.sync
        def _(sp):
            a_sync(sp)
            b_sync(sp)
            c_sync(sp)

        @block.gpsimd
        def _(pool):
            a_pool(pool)
            c_pool(pool)

        @block.scalar
        def _(act):
            a_scalar(act)
            b_scalar(act)
            c_scalar(act)

        @block.vector
        def _(v):
            a_vector(v)
            b_vector(v)
            c_vector(v)

        @block.tensor
        def _(pe):
            a_tensor(pe)
            b_tensor(pe)
            c_tensor(pe)


def kernel(**inputs):
    import concourse.bacc as _bacc
    from concourse.bass_utils import run_bass_kernel_spmd as _run

    f = {k: np.asarray(v) for k, v in inputs.items()}
    images = f["x"].shape[0]
    steps = images // IMGS

    def chunks(w, n):
        return w.reshape(n, 128)

    x = f["x"].reshape(steps, IMGS, CHANNELS, GW, PATCH, GH, PATCH).transpose(0, 2, 4, 6, 1, 3, 5)
    x = x.reshape(steps, KC, 128, IMGS * NPATCH).transpose(0, 2, 1, 3)
    w_tok = f["L0_tok_W"].reshape(D, PATCH, PATCH, CHANNELS).transpose(3, 1, 2, 0).reshape(KC, 128, D).transpose(1, 0, 2)
    in_w, in_b = f["L0_attn_in_proj_w"].reshape(6, 128, D), f["L0_attn_in_proj_b"].reshape(6, 128)
    de_w, de_b = f["L0_attn_delta_w"].reshape(2, 128, D), f["L0_attn_delta_b"].reshape(2, 128)
    order_w = np.stack([de_w[0], de_w[1], in_w[4], in_w[5], in_w[0], in_w[1], in_w[2], in_w[3]])
    order_b = np.stack([de_b[0], de_b[1], in_b[4], in_b[5], in_b[0], in_b[1], in_b[2], in_b[3]])
    conv_w = f["L0_attn_conv_w"].reshape(2, 128, 4).transpose(1, 0, 2).reshape(128, 8)
    parts = {
        "ln_w": f["L0_attn_ln_w"], "ln_b": f["L0_attn_ln_b"], "in_b": order_b.T, "conv_w": conv_w,
        "conv_b": f["L0_attn_conv_b"].reshape(2, 128).T, "state_mix": f["L0_attn_state_mix"].reshape(2, 128).T,
        "skip": f["L0_attn_skip_scale"].reshape(2, 128).T, "out_b": f["L0_attn_out_proj_b"], "tok_b": f["L0_tok_b"],
        "cls": f["L0_tok_cls_token"], "mr_b": f["L0_ffn_mr_b"].T, "ln1_g": f["L0_ffn_ln1_g"],
        "ln1_b": f["L0_ffn_ln1_b"], "mv_b": f["L0_ffn_mv_b"].T, "ln2_g": f["L0_ffn_ln2_g"],
        "ln2_b": f["L0_ffn_ln2_b"], "ln3_g": f["L0_ffn_ln3_g"], "ln3_b": f["L0_ffn_ln3_b"],
        "q_b": f["L1_attn_b_qkv"][0:D], "k_b": f["L1_attn_b_qkv"][D:2 * D], "v_b": f["L1_attn_b_qkv"][2 * D:],
        "attn_b": f["L1_attn_b_out"],
    }
    col = np.concatenate([parts[k].reshape(128, n) for k, (_, n) in COLS.items()], axis=1)
    rparts = {"pos": f["L0_tok_pos_emb"], "alpha": f["L0_ffn_mv_alpha"], "gate_b": f["L0_ffn_gate_b"],
              "bg": f["L1_ffn_bg"]}
    row = np.concatenate([rparts[k].reshape(1, n) for k, (_, n) in ROWS.items()], axis=1)
    w_exp = np.concatenate([
        f["L0_ffn_e_w1"],
        f["L0_ffn_e_w2"].reshape(E, FC, 128, D).transpose(0, 2, 1, 3).reshape(E, 128, FC * D),
        f["L0_ffn_e_b1"].reshape(E, FC, 128).transpose(0, 2, 1),
        f["L0_ffn_e_b2"][:, :, None],
    ], axis=2).reshape(E * 128, -1)
    w_last = np.concatenate([f["L1_ffn_We"], f["L1_ffn_be"][:, :, None]], axis=2).reshape(E2 * 128, D + 1)
    arrays = {
        "x": x, "w_tok": w_tok, "w_in": order_w.transpose(2, 0, 1),
        "w_out": f["L0_attn_out_proj_w"].reshape(D, 2, 128).transpose(2, 1, 0),
        "w_mr": f["L0_ffn_mr_w"].transpose(1, 0, 2), "w_mv": f["L0_ffn_mv_w"].transpose(1, 0, 2),
        "w_gate": f["L0_ffn_gate_w"], "col": col, "row": row, "w_exp": w_exp, "w_last": w_last,
        "w_qkv": f["L1_attn_w_qkv"], "w_att": f["L1_attn_w_out"], "w_g": f["L1_ffn_Wg"],
        "cst": const_tiles()[1], "crow": const_rows(images)[1],
    }
    arrays = {k: np.ascontiguousarray(v) for k, v in arrays.items()}
    nc = _bacc.Bacc("TRN2", target_bir_lowering=False, num_devices=1)
    a = {k: nc.dram_tensor(f"{k}_in", v.shape, mybir.dt.from_np(v.dtype), kind="ExternalInput").ap()
         for k, v in arrays.items()}
    a["out"] = nc.dram_tensor("out", (128, images * S), F32, kind="ExternalOutput").ap()
    build(nc, images, a)
    r = _run(nc, [{f"{k}_in": v for k, v in arrays.items()}], core_ids=[0])
    out = r.results[0]["out"]
    return np.ascontiguousarray(out.reshape(D, images, S).transpose(1, 2, 0))
```

```python
from contextlib import ExitStack

import numpy as np

import concourse.bass as bass
from concourse import mybir

F32 = mybir.dt.float32
I32 = mybir.dt.int32
BF16 = mybir.dt.bfloat16
ALU = mybir.AluOpType
ACT = mybir.ActivationFunctionType
AX_X = mybir.AxisListType.X

D = 128
PATCH = 16
CHANNELS = 3
KC = CHANNELS * PATCH * PATCH // 128
GW, GH = 176 // PATCH, 208 // PATCH
NPATCH = GW * GH
S = NPATCH + 1
IMGS = 4
T = IMGS * S
T2 = T // 2
G = 96
NG = T // G
E = 8
FF = 512
FC = FF // 128
BLK = 512
CB = BLK // 128
HEADS = 8
HD = D // HEADS
WIN = 32
QB = 16
NQB = S // QB
KW = 96
KPAD = 224
NWIN = (NQB + 1) // 2
UB = 4
NU = IMGS * NQB // UB
NI = 2 * IMGS
E2 = 16
EPS = 1e-5
OUT = 1e30

COLS = {}
for _name, _n in (("ln_w", 1), ("ln_b", 1), ("in_b", 8), ("conv_w", 8), ("conv_b", 2), ("state_mix", 2),
                  ("skip", 2), ("out_b", 1), ("tok_b", 1), ("cls", 1), ("mr_b", 3), ("ln1_g", 1), ("ln1_b", 1),
                  ("mv_b", 3), ("ln2_g", 1), ("ln2_b", 1), ("ln3_g", 1), ("ln3_b", 1), ("q_b", 1), ("k_b", 1),
                  ("v_b", 1), ("attn_b", 1)):
    COLS[_name] = (sum(n for _, n in COLS.values()), _n)
NCOLS = sum(n for _, n in COLS.values())
ROWS = {}
for _name, _n in (("pos", S), ("alpha", 3), ("gate_b", E), ("bg", E2)):
    ROWS[_name] = (sum(n for _, n in ROWS.values()), _n)
NROWS = sum(n for _, n in ROWS.values())


def sizes(images):
    tokens = images * S
    region = -(-tokens // BLK) * BLK + BLK
    blocks = (2 * tokens + E * (BLK - 1)) // BLK
    blocks += blocks % 2
    return tokens, region, blocks


def const_rows(images):
    tokens, region, blocks = sizes(images)
    kmax = -(-tokens // BLK) + 1
    parts = {
        "first": np.arange(E) * region,
        "rev": np.arange(E, 0, -1),
        "rev16": np.arange(E2, 0, -1),
        "blk": np.arange(blocks),
        "kblk": np.arange(kmax) * BLK,
    }
    where, at = {}, 0
    for k, v in parts.items():
        where[k] = (at, len(v))
        at += len(v)
    return where, np.concatenate(list(parts.values())).astype(np.float32)[None, :]


def const_tiles():
    p = np.arange(128)
    same_head = (p[:, None] // HD == p[None, :] // HD)
    band = np.full((128, NQB, KW), OUT, np.float32)
    for b in range(NQB):
        q = b * QB + np.arange(128) % QB
        key = WIN * (b // 2) - WIN + np.arange(KW)
        ok = (abs(key[None, :] - q[:, None]) <= WIN) & (key >= 0)[None, :] & (key < S)[None, :]
        band[:, b, :][ok] = 0.0
    band = np.concatenate([band, band[:, :UB - 1]], axis=1)
    parts = {
        "center": np.eye(128) - 1.0 / D,
        "mean": np.full((128, 128), 1.0 / D),
        "ident": np.eye(128),
        "before": (p[:, None] < p[None, :])[:, :G],
        "ones": np.ones((128, 128)),
        "head_rows": (p[:, None] // HD == np.arange(HEADS)[None, :]),
        "head_block": same_head,
        "query": (p[:, None] % QB == np.arange(QB)[None, :]),
        "band": band.reshape(128, -1),
    }
    where, at = {}, 0
    for k, v in parts.items():
        where[k] = (at, v.shape[1])
        at += v.shape[1]
    return where, np.concatenate([np.asarray(v, np.float32) for v in parts.values()], axis=1)


def build(nc, images, a):
    tokens, REGION, NB = sizes(images)
    ITERS = images // (2 * IMGS)
    cw, _ = const_tiles()
    rw, _ = const_rows(images)
    KMAX = rw["kblk"][1]
    assert S % QB == 0 and S % 4 == 0 and T % G == 0 and IMGS * NQB % UB == 0

    with ExitStack() as ctx:
        def sem(name):
            return ctx.enter_context(nc.semaphore(name))

        def sems(name):
            return [sem(f"{name}{s}") for s in range(2)]

        def sb(name, shape, dt=F32, where=ctx):
            return where.enter_context(nc.sbuf_tensor(name, shape, dt))

        expert_in = nc.dram_tensor("expert_in", (E * REGION + BLK, D), F32, kind="Internal").ap()
        expert_out = nc.dram_tensor("expert_out", (NB * BLK, D), F32, kind="Internal").ap()
        h1_dram = nc.dram_tensor("h1_dram", (128, tokens), F32, kind="Internal").ap()
        x2_dram = nc.dram_tensor("x2_dram", (128, tokens), F32, kind="Internal").ap()

        P = [[ctx.enter_context(nc.psum_tensor(f"psum{s}{k}", [128, 2, 512], F32)) for k in range(2)]
             for s in range(2)]

        def pv(s, k):
            return P[s][k][:, :, 0:T2]

        def two(ap):
            return ap.rearrange("p (g n) -> p g n", g=2)

        def four(ap):
            return ap.rearrange("p (m n) -> p m n", m=IMGS)

        def two_two(ap):
            return ap.rearrange("p (g m) n -> p g m n", g=2)

        def pv4(s, k):
            return pv(s, k).rearrange("p g (m n) -> p g m n", m=2)

        cst = sb("cst", [128, sum(n for _, n in cw.values())])
        crow = sb("crow", [128, sum(n for _, n in rw.values())])
        col = sb("col", [128, NCOLS])
        row = sb("row", [128, NROWS])

        def C(name):
            o, n = cw[name]
            return cst[:, o:o + n]

        def R(name):
            o, n = rw[name]
            return crow[:, o:o + n]

        def V(name, k=0):
            o, n = COLS[name]
            return col[:, o + k:o + k + 1]

        def RR(name):
            o, n = ROWS[name]
            return row[:, o:o + n]

        slots = sb("slots", [G, ITERS * 4 * NG])
        weights = sb("weights", [G, ITERS * 4 * NG])
        out_rows = sb("out_rows", [G, ITERS * 4 * NG])
        chosen = sb("chosen", [G, E])
        table = sb("table", [1, 2 * NB], I32)
        tails = sb("tails", [1, E], I32)

        loaded = sem("loaded")
        prep = sem("prep")
        prep_act = sem("prep_act")
        prep_pe = sem("prep_pe")
        consts_ready = sem("consts_ready")
        centered, squared, variance = sems("centered"), sems("squared"), sems("variance")
        logvar, rstd, normed = sems("logvar"), sems("rstd"), sems("normed")

        held = {"sync": sem("held_sync"), "pool": sem("held_pool")}

        def hold(eng, s, value):
            eng.wait_ge(s, value)
            eng.sem_inc(held["pool" if eng is nc.gpsimd else "sync"], 1)

        def ln_pe(pe, s, src, k):
            for g in range(2):
                last = nc.tensor.matmul(P[s][1][:, g, 0:T2], C("center"), two(src)[:, g, :], start=True, stop=True)
            last.then_inc(centered[s], 1)

        def ln_pe_var(pe, s, sq, k):
            pe.wait_ge(squared[s], k + 1)
            for g in range(2):
                last = nc.tensor.matmul(P[s][0][:, g, 0:T2], C("mean"), two(sq)[:, g, :], start=True, stop=True)
            last.then_inc(variance[s], 1)

        def ln_act_square(act, s, sq, k):
            act.wait_ge(centered[s], k + 1)
            nc.scalar.activation(two(sq), pv(s, 1), ACT.Square).then_inc(squared[s], 1)

        def ln_act_rstd(act, s, r, k, kr):
            act.wait_ge(variance[s], k + 1)
            nc.scalar.activation(two(r), pv(s, 0), ACT.Ln, bias=eps_col[:, 0:1]).then_inc(logvar[s], 1)
            act.wait_ge(logvar[s], kr + 1)
            nc.scalar.activation(r, r, ACT.Exp, scale=-0.5).then_inc(rstd[s], 1)

        eps_col = sb("eps_col", [128, 2])

        mem_a = ExitStack()
        w_tok = sb("w_tok", [128, KC, D], F32, mem_a)
        w_in = sb("w_in", [128, 8, 128], F32, mem_a)
        w_out = sb("w_out", [128, 2, D], F32, mem_a)
        w_mr = sb("w_mr", [128, 3, D], F32, mem_a)
        w_mv = sb("w_mv", [128, 3, D], F32, mem_a)
        w_gate = sb("w_gate", [128, E], F32, mem_a)
        in_bias = sb("in_bias", [128, 8], F32, mem_a)
        in_half = sb("in_half", [128, 8], F32, mem_a)
        taps = sb("taps", [128, 8], F32, mem_a)
        conv_b = sb("conv_b", [128, 2], F32, mem_a)
        decay = sb("decay", [128, 2], F32, mem_a)
        posb = sb("posb", [128, S], F32, mem_a)
        mr_bias = sb("mr_bias", [128, 1], F32, mem_a)
        alpha = sb("alpha", [128, 3], F32, mem_a)
        tiny = sb("tiny", [128, 8], F32, mem_a)

        def pair(name, shape, dt=F32, where=None):
            return [sb(f"{name}{s}", shape, dt, where or mem_a) for s in range(2)]

        xin = pair("xin", [128, KC, IMGS * NPATCH])
        h0, sq, ra, rb = pair("h0", [128, T]), pair("sq", [128, T]), pair("ra", [128, T]), pair("rb", [128, T])
        xn1, xn2, res = pair("xn1", [128, T]), pair("xn2", [128, T]), pair("res", [128, T])
        unit = [[sb(f"unit{s}{u}", [128, T], F32, mem_a) for u in range(8)] for s in range(2)]
        zproj = [[sb(f"zproj{s}{c}", [128, T], F32, mem_a) for c in range(2)] for s in range(2)]
        pj = [[sb(f"pj{s}{c}", [128, IMGS, S + 3], F32, mem_a) for c in range(2)] for s in range(2)]
        acc = [[sb(f"acc{s}{c}", [128, T], F32, mem_a) for c in range(2)] for s in range(2)]
        h1, x2 = pair("h1", [128, T]), pair("x2", [128, T])
        pool2, pool4 = pair("pool2", [128, T // 2]), pair("pool4", [128, T // 4])
        rows = pair("rows", [G, NG, D])
        logit, lmask, cand = pair("logit", [G, NG, E]), pair("lmask", [G, NG, E]), pair("cand", [G, NG, E])
        pick1, pick2, picks = pair("pick1", [G, NG, E]), pair("pick2", [G, NG, E]), pair("picks", [G, NG, E])
        top1, top2, best = pair("top1", [G, NG]), pair("top2", [G, NG]), pair("best", [G, NG])
        wexp, wsum = pair("wexp", [G, NG]), pair("wsum", [G, NG])
        newly = pair("newly", [G, E])
        slot = pair("slot", [G, 2 * NG])
        slot_i = pair("slot_i", [G, 2 * NG], I32)
        DELTA, DRIVE, PROJ, GATE = (0, 1), (2, 3), (4, 5), (6, 7)

        x_landed, tok_done, embedded = sems("x_landed"), sems("tok_done"), sems("embedded")
        res_done = sems("res_done")
        unit_done, unit_act = sems("unit_done"), sems("unit_act")
        delta_step = sems("delta_step")
        mix_step = sems("mix_step")
        out_done, h1_ready, h1_stored = sems("out_done"), sems("h1_ready"), sems("h1_stored")
        ffn_step, mr_done = sems("ffn_step"), sems("mr_done")
        mv_done, gelu_done = sems("mv_done"), sems("gelu_done")
        x2_stored, logits_done = sems("x2_stored"), sems("logits_done")
        turned, rows_ready, route_step = sems("turned"), sems("rows_ready"), sems("route_step")
        wexp_done, rank_done, slots_ready, scattered = (sems("wexp_done"), sems("rank_done"), sems("slots_ready"),
                                                        sems("scattered"))
        chosen_new = sem("chosen_new")
        LNA = 4
        RSA = LNA + 1
        MIX = 11
        FFN = 11
        x0, x1, view = xn1, xn2, [[unit[s][u] for u in (0, 1, 2)] for s in range(2)]
        pre = rb

        def a_range(i, s):
            return bass.DynSlice((2 * i + s) * T, T)

        def a_sync(sp):
            for dst, src in ((cst, "cst"), (crow, "crow"), (col, "col"), (row, "row"), (w_tok, "w_tok"),
                             (w_in, "w_in"), (w_out, "w_out"), (w_mr, "w_mr"), (w_mv, "w_mv"), (w_gate, "w_gate")):
                src = a[src]
                if src.shape[0] == 1:
                    src = src.to_broadcast([128, src.shape[1]])
                sp.dma_start(dst[:], src).then_inc(loaded, 16)
            with sp.Fori(0, ITERS) as i:
                for s in range(2):
                    hold(sp, tok_done[s], i)
                    sp.dma_start(xin[s][:], a["x"][bass.DynSlice(2 * i + s, 1)].rearrange("o p k n -> (o p) k n")
                                 ).then_inc(x_landed[s], 16)
                for s in range(2):
                    hold(sp, h1_ready[s], i + 1)
                    sp.dma_start(h1_dram[:, a_range(i, s)], h1[s][:]).then_inc(h1_stored[s], 16)
                for s in range(2):
                    hold(sp, ffn_step[s], FFN * i + 11)
                    sp.dma_start(x2_dram[:, a_range(i, s)], x2[s][:]).then_inc(x2_stored[s], 16)
            for s in range(2):
                sp.wait_ge(h1_stored[s], 16 * ITERS)
                sp.wait_ge(x2_stored[s], 16 * ITERS)

        NLOADS = 10

        def a_prep_vector(v):
            n = [0]

            def step(ins):
                n[0] += 1
                ins.then_inc(prep, 1)

            def settle():
                v.wait_ge(prep, n[0])

            step(v.memset(eps_col[:, 0:1], EPS))
            step(v.memset(eps_col[:, 1:2], EPS * EPS))
            step(v.memset(chosen[:], 0.0))
            for s in range(2):
                for c in range(2):
                    step(v.memset(pj[s][c][:], 0.0))
            v.wait_ge(loaded, 16 * NLOADS)
            v.wait_ge(prep_pe, 1)
            step(v.tensor_scalar(w_in[:], w_in[:], V("ln_w"), None, ALU.mult))
            o, _ = COLS["in_b"]
            step(v.tensor_tensor(in_bias[:], P[0][0][:, 0, 0:8], col[:, o:o + 8], ALU.add))
            settle()
            step(v.tensor_scalar(in_half[:], in_bias[:], 0.5, None, ALU.mult))
            for c in range(2):
                o, _ = COLS["conv_w"]
                step(v.tensor_scalar(taps[:, 4 * c:4 * c + 4], col[:, o + 4 * c:o + 4 * c + 4], V("skip", c), None,
                                     ALU.mult))
                step(v.tensor_scalar(conv_b[:, c:c + 1], V("conv_b", c), V("skip", c), 2.0, ALU.mult, ALU.mult))
            step(v.tensor_scalar(w_out[:], w_out[:], 0.25, None, ALU.mult))
            v.wait_ge(prep_act, 1)
            step(v.tensor_scalar(decay[:], decay[:], 0.5, 0.5, ALU.mult, ALU.add))
            step(v.tensor_scalar(posb[:], RR("pos"), V("tok_b"), None, ALU.add))
            settle()
            step(v.tensor_tensor(posb[:, 0:1], RR("pos")[:, 0:1], V("cls"), ALU.add))
            settle()
            for s in range(2):
                step(v.tensor_copy(four(h0[s][:])[:, :, 0], posb[:, 0:1].to_broadcast([128, IMGS])))
            for r in range(3):
                step(v.tensor_scalar(w_mr[:, r, :], w_mr[:, r, :], 1.0 / (3 * 2 ** r), None, ALU.mult))
            step(v.tensor_tensor(tiny[:, 0:1], V("mr_b", 0), V("mr_b", 1), ALU.add))
            settle()
            step(v.tensor_tensor(tiny[:, 1:2], tiny[:, 0:1], V("mr_b", 2), ALU.add))
            settle()
            step(v.tensor_scalar(mr_bias[:], tiny[:, 1:2], 1.0 / 3, None, ALU.mult))
            step(v.tensor_reduce(tiny[:, 2:3], RR("alpha"), AX_X, ALU.max))
            settle()
            step(v.tensor_scalar(alpha[:], RR("alpha"), tiny[:, 2:3], None, ALU.subtract))
            settle()
            v.sem_inc(consts_ready, 1)
            v.wait_ge(prep_act, 2)
            step(v.tensor_reduce(tiny[:, 3:4], alpha[:], AX_X, ALU.add))
            settle()
            step(v.reciprocal(tiny[:, 4:5], tiny[:, 3:4]))
            settle()
            step(v.tensor_scalar(alpha[:], alpha[:], tiny[:, 4:5], None, ALU.mult))
            settle()
            v.sem_inc(consts_ready, 1)

        def a_prep_scalar(act):
            act.wait_ge(loaded, 16 * NLOADS)
            o, _ = COLS["state_mix"]
            nc.scalar.activation(decay[:], col[:, o:o + 2], ACT.Tanh, scale=0.5).then_inc(prep_act, 1)
            act.wait_ge(consts_ready, 1)
            nc.scalar.activation(alpha[:], alpha[:], ACT.Exp).then_inc(prep_act, 1)

        def a_prep_tensor(pe):
            pe.wait_ge(loaded, 16 * NLOADS)
            for u in range(8):
                last = nc.tensor.matmul(P[0][0][:, 0, u:u + 1], w_in[:, u, :], V("ln_b"), start=True, stop=True)
            last.then_inc(prep_pe, 1)

        def a_tensor(pe):
            a_prep_tensor(pe)
            pe.wait_ge(consts_ready, 2)
            with pe.Fori(0, ITERS) as i:
                for s in range(2):
                    pe.wait_ge(x_landed[s], 16 * i + 16)
                    pe.wait_ge(slots_ready[s], i)
                    for g in range(2):
                        for k in range(KC):
                            last = nc.tensor.matmul(P[s][0][:, g, 0:2 * NPATCH], w_tok[:, k, :],
                                                    xin[s][:, k, g * 2 * NPATCH:(g + 1) * 2 * NPATCH],
                                                    start=(k == 0), stop=(k == KC - 1))
                    last.then_inc(tok_done[s], 1)
                for s in range(2):
                    pe.wait_ge(embedded[s], 2 * i + 2)
                    pe.wait_ge(rows_ready[s], 2 * i)
                    ln_pe(pe, s, h0[s][:], LNA * i)
                for s in range(2):
                    ln_pe_var(pe, s, sq[s][:], LNA * i)
                for u in range(8):
                    for s in range(2):
                        if u == 0:
                            pe.wait_ge(normed[s], 2 * i + 2)
                        if u >= 2:
                            pe.wait_ge(unit_act[s], 8 * i + u - 1)
                        for g in range(2):
                            last = nc.tensor.matmul(P[s][u % 2][:, g, 0:T2], w_in[:, u, :], two(xn2[s][:])[:, g, :],
                                                    start=True, stop=True)
                        last.then_inc(unit_done[s], 1)
                for s in range(2):
                    pe.wait_ge(mix_step[s], 2 * MIX * (i + 1))
                    pe.wait_ge(unit_act[s], 8 * i + 8)
                    for g in range(2):
                        for c in range(2):
                            last = nc.tensor.matmul(P[s][0][:, g, 0:T2], w_out[:, c, :], two(acc[s][c][:])[:, g, :],
                                                    start=(c == 0), stop=(c == 1))
                    last.then_inc(out_done[s], 1)
                for s in range(2):
                    pe.wait_ge(h1_ready[s], i + 1)
                    ln_pe(pe, s, h1[s][:], LNA * i + 1)
                for s in range(2):
                    ln_pe_var(pe, s, sq[s][:], LNA * i + 1)
                for s in range(2):
                    pe.wait_ge(ffn_step[s], FFN * i + 3)
                    for g in range(2):
                        dst = P[s][0][:, g, 0:T2]
                        nc.tensor.matmul(dst, w_mr[:, 0, :], two(x0[s][:])[:, g, :], start=True, stop=False)
                        nc.tensor.matmul(dst, w_mr[:, 1, :], two(pool2[s][:])[:, g, :].unsqueeze(2)
                                         .to_broadcast([128, T2 // 2, 2]), start=False, stop=False)
                        last = nc.tensor.matmul(dst, w_mr[:, 2, :], two(pool4[s][:])[:, g, :].unsqueeze(2)
                                                .to_broadcast([128, T2 // 4, 4]), start=False, stop=True)
                    last.then_inc(mr_done[s], 1)
                for s in range(2):
                    pe.wait_ge(ffn_step[s], FFN * i + 4)
                    ln_pe(pe, s, pre[s][:], LNA * i + 2)
                for s in range(2):
                    ln_pe_var(pe, s, sq[s][:], LNA * i + 2)
                for k in range(3):
                    for s in range(2):
                        if k == 0:
                            pe.wait_ge(ffn_step[s], FFN * i + 6)
                        if k == 2:
                            pe.wait_ge(gelu_done[s], 3 * i + 1)
                        for g in range(2):
                            last = nc.tensor.matmul(P[s][k % 2][:, g, 0:T2], w_mv[:, k, :], two(x1[s][:])[:, g, :],
                                                    start=True, stop=True)
                        last.then_inc(mv_done[s], 1)
                for s in range(2):
                    pe.wait_ge(ffn_step[s], FFN * i + 9)
                    ln_pe(pe, s, pre[s][:], LNA * i + 3)
                for s in range(2):
                    ln_pe_var(pe, s, sq[s][:], LNA * i + 3)
                for s in range(2):
                    pe.wait_ge(ffn_step[s], FFN * i + 11)
                    for g in range(NG):
                        last = nc.tensor.matmul(P[s][0][0:G, 0, g * E:(g + 1) * E], x2[s][:, g * G:(g + 1) * G],
                                                w_gate[:], start=True, stop=True)
                    last.then_inc(logits_done[s], 1)
                    for g in range(NG):
                        last = nc.tensor.transpose(P[s][1][0:G, g // 4, (g % 4) * 128:(g % 4 + 1) * 128],
                                                   x2[s][:, g * G:(g + 1) * G], C("ident"))
                    last.then_inc(turned[s], 1)
                for s in range(2):
                    pe.wait_ge(route_step[s], ROUTE * i + 13)
                    pe.wait_ge(chosen_new, 2 * i + s)
                    dst = P[s][0][0:G, 1, 0:NG * E].rearrange("p (g e) -> p g e", e=E)
                    nc.tensor.matmul(dst, C("before")[0:G, :], picks[s][:], start=True, stop=False)
                    for g in range(NG - 1):
                        nc.tensor.matmul(dst[:, g + 1:NG, :], C("ones")[0:G, 0:G],
                                         picks[s][:, g:g + 1, :].to_broadcast([G, NG - 1 - g, E]),
                                         start=False, stop=False)
                    nc.tensor.matmul(dst, C("ones")[0:G, 0:G], chosen[:].unsqueeze(1).to_broadcast([G, NG, E]),
                                     start=False, stop=True).then_inc(rank_done[s], 1)

        ROUTE = 25

        def a_scalar(act):
            a_prep_scalar(act)
            act.wait_ge(consts_ready, 2)
            act.preload_act_table_set("natural_log_exp_and_others")
            with act.Fori(0, ITERS) as i:
                for s in range(2):
                    ln_act_square(act, s, sq[s][:], LNA * i)
                for s in range(2):
                    act.wait_ge(variance[s], LNA * i + 1)
                    nc.scalar.activation(two(ra[s][:]), pv(s, 0), ACT.Ln, bias=eps_col[:, 0:1]).then_inc(logvar[s], 1)
                    nc.scalar.activation(two(rb[s][:]), pv(s, 0), ACT.Ln, bias=eps_col[:, 1:2], scale=1.0 + EPS
                                         ).then_inc(logvar[s], 1)
                    act.wait_ge(logvar[s], RSA * i + 1)
                    nc.scalar.activation(ra[s][:], ra[s][:], ACT.Exp, scale=-0.5).then_inc(rstd[s], 1)
                    act.wait_ge(logvar[s], RSA * i + 2)
                    nc.scalar.activation(rb[s][:], rb[s][:], ACT.Exp, scale=-0.5).then_inc(rstd[s], 1)
                for u in range(8):
                    for s in range(2):
                        act.wait_ge(unit_done[s], 8 * i + u + 1)
                        half = u not in DRIVE
                        ins = nc.scalar.activation(two(unit[s][u][:]), pv(s, u % 2), ACT.Tanh,
                                                   bias=(in_half if half else in_bias)[:, u:u + 1],
                                                   scale=0.5 if half else 1.0)
                        if u in PROJ:
                            ins = nc.scalar.activation(two(zproj[s][u - PROJ[0]][:]), pv(s, u % 2), ACT.Identity,
                                                       bias=in_bias[:, u:u + 1])
                        ins.then_inc(unit_act[s], 1)
                act.preload_act_table_set("natural_log_exp_and_others")
                for n in (1, 2):
                    for s in range(2):
                        ln_act_square(act, s, sq[s][:], LNA * i + n)
                    for s in range(2):
                        ln_act_rstd(act, s, ra[s][:], LNA * i + n, RSA * i + n + 1)
                for k in range(3):
                    for s in range(2):
                        act.wait_ge(mv_done[s], 3 * i + k + 1)
                        nc.scalar.activation(two(view[s][k][:]), pv(s, k % 2), ACT.Gelu_apprx_tanh,
                                             bias=V("mv_b", k)).then_inc(gelu_done[s], 1)
                act.preload_act_table_set("natural_log_exp_and_others")
                for s in range(2):
                    ln_act_square(act, s, sq[s][:], LNA * i + 3)
                for s in range(2):
                    ln_act_rstd(act, s, ra[s][:], LNA * i + 3, RSA * i + 4)
                for s in range(2):
                    act.wait_ge(turned[s], i + 1)
                    act.wait_ge(scattered[s], 16 * 2 * NG * i)
                    for b, (g0, g1) in enumerate(((0, 4), (4, NG))):
                        nc.scalar.activation(rows[s][:, g0:g1, :].rearrange("p g d -> p (g d)"),
                                             P[s][1][0:G, b, 0:(g1 - g0) * 128], ACT.Copy).then_inc(rows_ready[s], 1)
                for s in range(2):
                    act.wait_ge(route_step[s], ROUTE * i + 14)
                    nc.scalar.activation(wexp[s][:], wexp[s][:], ACT.Exp).then_inc(wexp_done[s], 1)

        def a_vector(v):
            a_prep_vector(v)
            with v.Fori(0, ITERS) as i:
                for s in range(2):
                    v.wait_ge(tok_done[s], i + 1)
                    for g in range(2):
                        v.tensor_tensor(four(h0[s][:])[:, 2 * g:2 * g + 2, 1:S],
                                        P[s][0][:, g, 0:2 * NPATCH].rearrange("p (m n) -> p m n", m=2),
                                        posb[:, 1:S].unsqueeze(1).to_broadcast([128, 2, NPATCH]),
                                        ALU.add).then_inc(embedded[s], 1)
                for s in range(2):
                    v.wait_ge(rstd[s], RSA * i + 1)
                    v.tensor_tensor(two(xn1[s][:]), pv(s, 1), two(ra[s][:]), ALU.mult).then_inc(normed[s], 1)
                    v.wait_ge(rstd[s], RSA * i + 2)
                    v.tensor_tensor(two(xn2[s][:]), pv(s, 1), two(rb[s][:]), ALU.mult).then_inc(normed[s], 1)
                for c in range(2):
                    for s in range(2):
                        v.wait_ge(unit_act[s], 8 * i + PROJ[c] + 1)
                        v.scalar_tensor_tensor(out=pj[s][c][:, :, 3:], in0=four(unit[s][PROJ[c]][:]), scalar=1.0,
                                               in1=four(zproj[s][c][:]), op0=ALU.add, op1=ALU.mult
                                               ).then_inc(mix_step[s], 1)
                    for s in range(2):
                        v.wait_ge(mix_step[s], MIX * (2 * i + c) + 1)
                        v.tensor_scalar(four(acc[s][c][:]), pj[s][c][:, :, 3:], taps[:, 4 * c + 3:4 * c + 4],
                                        conv_b[:, c:c + 1], ALU.mult, ALU.add).then_inc(mix_step[s], 1)
                    for n, tap in enumerate((2, 1, 0)):
                        for s in range(2):
                            v.wait_ge(mix_step[s], MIX * (2 * i + c) + 2 + n)
                            v.scalar_tensor_tensor(out=four(acc[s][c][:]), in0=pj[s][c][:, :, tap:tap + S],
                                                   scalar=taps[:, 4 * c + tap:4 * c + tap + 1],
                                                   in1=four(acc[s][c][:]), op0=ALU.mult, op1=ALU.add
                                                   ).then_inc(mix_step[s], 1)
                    for s in range(2):
                        v.wait_ge(delta_step[s], 4 * i + 2 * c + 2)
                        for m in range(IMGS):
                            v.tensor_tensor_scan(four(unit[s][DRIVE[c]][:])[:, m, :],
                                                 decay[:, c:c + 1].to_broadcast([128, S]),
                                                 four(unit[s][DELTA[c]][:])[:, m, :], 0.0, ALU.mult, ALU.add
                                                 ).then_inc(mix_step[s], 1)
                    for s in range(2):
                        v.wait_ge(mix_step[s], MIX * (2 * i + c) + 5 + IMGS)
                        v.tensor_tensor(acc[s][c][:], acc[s][c][:], unit[s][DRIVE[c]][:], ALU.add
                                        ).then_inc(mix_step[s], 1)
                    for s in range(2):
                        v.wait_ge(mix_step[s], MIX * (2 * i + c) + 6 + IMGS)
                        v.wait_ge(unit_act[s], 8 * i + GATE[c] + 1)
                        v.scalar_tensor_tensor(out=acc[s][c][:], in0=unit[s][GATE[c]][:], scalar=1.0,
                                               in1=acc[s][c][:], op0=ALU.add, op1=ALU.mult).then_inc(mix_step[s], 1)
                for s in range(2):
                    v.wait_ge(out_done[s], i + 1)
                    v.wait_ge(res_done[s], i + 1)
                    v.wait_ge(h1_stored[s], 16 * i)
                    v.scalar_tensor_tensor(out=two(h1[s][:]), in0=pv(s, 0), scalar=V("out_b"), in1=two(res[s][:]),
                                           op0=ALU.add, op1=ALU.add).then_inc(h1_ready[s], 1)
                for s in range(2):
                    v.wait_ge(rstd[s], RSA * i + 3)
                    v.tensor_tensor(two(x0[s][:]), pv(s, 1), two(ra[s][:]), ALU.mult).then_inc(ffn_step[s], 1)
                for s in range(2):
                    v.wait_ge(ffn_step[s], FFN * i + 1)
                    p2 = x0[s][:].rearrange("p (n k) -> p n k", k=2)
                    v.tensor_tensor(pool2[s][:], p2[:, :, 0], p2[:, :, 1], ALU.add).then_inc(ffn_step[s], 1)
                for s in range(2):
                    v.wait_ge(ffn_step[s], FFN * i + 2)
                    p4 = pool2[s][:].rearrange("p (n k) -> p n k", k=2)
                    v.tensor_tensor(pool4[s][:], p4[:, :, 0], p4[:, :, 1], ALU.add).then_inc(ffn_step[s], 1)
                for s in range(2):
                    v.wait_ge(mr_done[s], i + 1)
                    v.scalar_tensor_tensor(out=two(pre[s][:]), in0=pv(s, 0), scalar=mr_bias[:, 0:1],
                                           in1=two(x0[s][:]), op0=ALU.add, op1=ALU.add).then_inc(ffn_step[s], 1)
                for s in range(2):
                    v.wait_ge(rstd[s], RSA * i + 4)
                    v.scalar_tensor_tensor(out=two(x1[s][:]), in0=pv(s, 1), scalar=V("ln1_g"), in1=two(ra[s][:]),
                                           op0=ALU.mult, op1=ALU.mult).then_inc(ffn_step[s], 1)
                for s in range(2):
                    v.wait_ge(ffn_step[s], FFN * i + 5)
                    v.tensor_scalar(x1[s][:], x1[s][:], V("ln1_b"), None, ALU.add).then_inc(ffn_step[s], 1)
                for k in range(3):
                    for s in range(2):
                        v.wait_ge(gelu_done[s], 3 * i + k + 1)
                        if k:
                            v.wait_ge(ffn_step[s], FFN * i + 6 + k)
                        v.scalar_tensor_tensor(out=pre[s][:], in0=view[s][k][:], scalar=alpha[:, k:k + 1],
                                               in1=(pre if k else x1)[s][:], op0=ALU.mult, op1=ALU.add
                                               ).then_inc(ffn_step[s], 1)
                for s in range(2):
                    v.wait_ge(rstd[s], RSA * i + 5)
                    v.wait_ge(x2_stored[s], 16 * i)
                    v.scalar_tensor_tensor(out=two(x2[s][:]), in0=pv(s, 1), scalar=V("ln2_g"), in1=two(ra[s][:]),
                                           op0=ALU.mult, op1=ALU.mult).then_inc(ffn_step[s], 1)
                for s in range(2):
                    v.wait_ge(ffn_step[s], FFN * i + 10)
                    v.tensor_scalar(x2[s][:], x2[s][:], V("ln2_b"), None, ALU.add).then_inc(ffn_step[s], 1)
                a_route(v, i)

        def a_route(v, i):
            def over_e(ap):
                return ap.unsqueeze(2).to_broadcast([G, NG, E])

            rev = R("rev")[0:G, :].unsqueeze(1).to_broadcast([G, NG, E])
            done = [[0, 0]]

            def both(make):
                n = done[0][0]
                for s in range(2):
                    if n:
                        v.wait_ge(route_step[s], ROUTE * i + n)
                    make(s).then_inc(route_step[s], 1)
                done[0][0] += 1

            for s in range(2):
                v.wait_ge(logits_done[s], i + 1)
                v.tensor_tensor(logit[s][:], P[s][0][0:G, 0, 0:NG * E].rearrange("p (g e) -> p g e", e=E),
                                RR("gate_b")[0:G, :].unsqueeze(1).to_broadcast([G, NG, E]), ALU.add
                                ).then_inc(route_step[s], 1)
            done[0][0] = 1
            for top, pick, src in ((top1, pick1, logit), (top2, pick2, lmask)):
                both(lambda s: v.tensor_reduce(top[s][:], src[s][:], AX_X, ALU.max))
                both(lambda s: v.tensor_tensor(cand[s][:], src[s][:], over_e(top[s][:]), ALU.is_equal))
                both(lambda s: v.tensor_tensor(cand[s][:], cand[s][:], rev, ALU.mult))
                both(lambda s: v.tensor_reduce(best[s][:], cand[s][:], AX_X, ALU.max))
                both(lambda s: v.tensor_tensor(pick[s][:], cand[s][:], over_e(best[s][:]), ALU.is_equal))
                if top is top1:
                    both(lambda s: v.scalar_tensor_tensor(out=lmask[s][:], in0=pick1[s][:], scalar=-3e38,
                                                          in1=logit[s][:], op0=ALU.mult, op1=ALU.add))
            both(lambda s: v.tensor_tensor(picks[s][:], pick1[s][:], pick2[s][:], ALU.add))
            both(lambda s: v.tensor_tensor(wexp[s][:], top2[s][:], top1[s][:], ALU.subtract))
            both(lambda s: v.tensor_reduce(newly[s][:], picks[s][:].rearrange("p g e -> p e g"), AX_X, ALU.add))
            for s in range(2):
                v.wait_ge(wexp_done[s], i + 1)
            both(lambda s: v.tensor_scalar(wsum[s][:], wexp[s][:], 1.0, None, ALU.add))

            def at(tile, s, choice):
                return tile[:, bass.DynSlice(i * 4 * NG + s * 2 * NG + choice * NG, NG)]

            both(lambda s: v.reciprocal(wsum[s][:], wsum[s][:]))
            both(lambda s: v.tensor_copy(at(weights, s, 0), wsum[s][:]))
            both(lambda s: v.tensor_tensor(at(weights, s, 1), wexp[s][:], wsum[s][:], ALU.mult))
            for s in range(2):
                v.wait_ge(rank_done[s], i + 1)
                v.wait_ge(chosen_new, 2 * i + s)
                v.wait_ge(route_step[s], ROUTE * i + 19)
                v.tensor_tensor(chosen[:], chosen[:], newly[s][:], ALU.add).then_inc(chosen_new, 1)
                v.tensor_tensor(cand[s][:], P[s][0][0:G, 1, 0:NG * E].rearrange("p (g e) -> p g e", e=E),
                                R("first")[0:G, :].unsqueeze(1).to_broadcast([G, NG, E]), ALU.add
                                ).then_inc(route_step[s], 1)
            done[0][0] = 20
            for choice, pick in ((0, pick1), (1, pick2)):
                both(lambda s: v.tensor_tensor(logit[s][:], cand[s][:], pick[s][:], ALU.mult))
                both(lambda s: v.tensor_reduce(slot[s][:, choice * NG:(choice + 1) * NG], logit[s][:], AX_X,
                                               ALU.add))
            both(lambda s: v.tensor_copy(slots[:, bass.DynSlice(i * 4 * NG + s * 2 * NG, 2 * NG)], slot[s][:]))
            assert done[0][0] == ROUTE
            for s in range(2):
                v.wait_ge(scattered[s], 16 * 2 * NG * i)
                v.tensor_copy(slot_i[s][:], slot[s][:]).then_inc(slots_ready[s], 1)

        def a_pool(pool):
            with pool.Fori(0, ITERS) as i:
                for s in range(2):
                    pool.wait_ge(embedded[s], 2 * i + 2)
                    pool.wait_ge(normed[s], 2 * i + 1)
                    pool.tensor_tensor(res[s][:], h0[s][:], xn1[s][:], ALU.add).then_inc(res_done[s], 1)
                for c in range(2):
                    for s in range(2):
                        hold(pool, unit_act[s], 8 * i + DELTA[c] + 1)
                        pool.tensor_scalar(unit[s][DELTA[c]][:], unit[s][DELTA[c]][:], 1.0, 2e-4, ALU.add, ALU.max
                                           ).then_inc(delta_step[s], 1)
                    for s in range(2):
                        pool.wait_ge(unit_act[s], 8 * i + DRIVE[c] + 1)
                        pool.wait_ge(delta_step[s], 4 * i + 2 * c + 1)
                        pool.tensor_tensor(unit[s][DELTA[c]][:], unit[s][DELTA[c]][:], unit[s][DRIVE[c]][:], ALU.mult
                                           ).then_inc(delta_step[s], 1)
                for s in range(2):
                    hold(pool, rows_ready[s], 2 * i + 2)
                    hold(pool, slots_ready[s], i + 1)
                    for choice in range(2):
                        for g in range(NG):
                            n = choice * NG + g
                            pool.indirect_dma_start(
                                out=expert_in[:, :],
                                out_offset=bass.IndirectOffsetOnAxis(ap=slot_i[s][:, n:n + 1], axis=0),
                                in_=rows[s][:, g, :], in_offset=None).then_inc(scattered[s], 16)
            for s in range(2):
                pool.wait_ge(scattered[s], 16 * 2 * NG * ITERS)

        mem_a.close()

        mem_b = ExitStack()
        WCOLS = FF + FC * D + FC + 1
        w_blk = pair("w_blk", [128, WCOLS], F32, mem_b)
        rows_in, rows_out = pair("rows_in", [128, CB, D], F32, mem_b), pair("rows_out", [128, CB, D], F32, mem_b)
        x_t, y_t = pair("x_t", [128, BLK], F32, mem_b), pair("y_t", [128, BLK], F32, mem_b)
        hid = pair("hid", [128, FC, BLK], F32, mem_b)
        zeros = sb("zeros", [128, CB * D], F32, mem_b)
        count = sb("count", [128, E], F32, mem_b)
        nblk, ends, ones_e = (sb("nblk", [128, E], F32, mem_b), sb("ends", [128, E], F32, mem_b),
                              sb("ones_e", [128, E], F32, mem_b))
        over = sb("over", [128, E, KMAX], F32, mem_b)
        past = sb("past", [1, NB, E], F32, mem_b)
        blk_e, blk_done = sb("blk_e", [1, NB], F32, mem_b), sb("blk_done", [1, NB], F32, mem_b)
        shift = sb("shift", [128, E], F32, mem_b)
        moved = sb("moved", [G, ITERS * 4 * NG], F32, mem_b)

        count_done, table_step, table_ready = sem("count_done"), sem("table_step"), sem("table_ready")
        out_rows_step, zero_filled = sem("out_rows_step"), sem("zero_filled")
        w_landed, r_landed, block_stored = sems("w_landed"), sems("r_landed"), sems("block_stored")
        in_turned, xt_ready, hid_done, hid_ready = (sems("in_turned"), sems("xt_ready"), sems("hid_done"),
                                                    sems("hid_ready"))
        y_done, yt_ready, out_turned, rows_out_ready = (sems("y_done"), sems("yt_ready"), sems("out_turned"),
                                                        sems("rows_out_ready"))
        TB = [P[s][0][:, 0, :] for s in range(2)]
        HB = [[P[s][0][:, 1, :], P[s][1][:, 0, :]] for s in range(2)]
        YB = [P[s][1][:, 1, :] for s in range(2)]

        def b_sync(sp):
            sp.wait_ge(table_ready, 1)
            for s in range(2):
                sp.wait_ge(scattered[s], 16 * 2 * NG * ITERS)
            for e in range(E + 1):
                if e < E:
                    n = sp.value_load(tails[0:1, e:e + 1], min_val=0, max_val=tokens)
                    at = bass.DynSlice(n + e * REGION, BLK)
                else:
                    at = slice(E * REGION, E * REGION + BLK)
                sp.dma_start(expert_in[at, :].rearrange("(p c) d -> p (c d)", c=CB), zeros[:]
                             ).then_inc(zero_filled, 16)
            sp.wait_ge(zero_filled, 16 * (E + 1))

            def load(n, s, k, first):
                if not first:
                    hold(sp, yt_ready[s], k)
                e = sp.value_load(table[0:1, bass.DynSlice(NB + n, 1)], min_val=0, max_val=E - 1)
                sp.dma_start(w_blk[s][:], a["w_exp"][bass.DynSlice(e * 128, 128), :]).then_inc(w_landed[s], 16)
                r = sp.value_load(table[0:1, bass.DynSlice(n, 1)], min_val=0, max_val=E * REGION)
                sp.dma_start(rows_in[s][:].rearrange("p c d -> p (c d)"),
                             expert_in[bass.DynSlice(r, BLK), :].rearrange("(p c) d -> p (c d)", c=CB)
                             ).then_inc(r_landed[s], 16)

            def store(n, s, k):
                hold(sp, rows_out_ready[s], k + 1)
                sp.dma_start(expert_out[bass.DynSlice(n * BLK, BLK), :].rearrange("(p c) d -> p (c d)", c=CB),
                             rows_out[s][:].rearrange("p c d -> p (c d)")).then_inc(block_stored[s], 16)

            for s in range(2):
                load(s, s, 0, True)
            with sp.Fori(1, NB // 2) as i:
                for s in range(2):
                    load(2 * i + s, s, i, False)
                    store(2 * i + s - 2, s, i - 1)
            for s in range(2):
                store(NB - 2 + s, s, NB // 2 - 1)
            for s in range(2):
                sp.wait_ge(block_stored[s], 16 * (NB // 2))

        def b_tensor(pe):
            pe.wait_ge(chosen_new, 2 * ITERS)
            for s in range(2):
                pe.wait_ge(rows_ready[s], 2 * ITERS)
                pe.wait_ge(slots_ready[s], ITERS)
            nc.tensor.matmul(YB[0][:, 0:E], C("ones")[0:G, :], chosen[:], start=True, stop=True).then_inc(count_done, 1)

            def turn_in(s, k):
                pe.wait_ge(r_landed[s], 16 * k + 16)
                for c in range(CB):
                    last = nc.tensor.transpose(TB[s][:, c * 128:(c + 1) * 128], rows_in[s][:, c, :], C("ident"))
                last.then_inc(in_turned[s], 1)

            def hidden(s, k, c):
                if c == 0:
                    pe.wait_ge(w_landed[s], 16 * k + 16)
                    pe.wait_ge(xt_ready[s], k + 1)
                if c >= 2:
                    pe.wait_ge(hid_ready[s], FC * k + c - 1)
                nc.tensor.matmul(HB[s][c % 2], w_blk[s][:, c * 128:(c + 1) * 128], x_t[s][:], start=True, stop=True
                                 ).then_inc(hid_done[s], 1)

            def outputs(s, k):
                for c in range(FC):
                    pe.wait_ge(hid_ready[s], FC * k + c + 1)
                    last = nc.tensor.matmul(YB[s], w_blk[s][:, FF + c * D:FF + (c + 1) * D], hid[s][:, c, :],
                                            start=(c == 0), stop=(c == FC - 1))
                last.then_inc(y_done[s], 1)

            def turn_out(s, k):
                pe.wait_ge(yt_ready[s], k + 1)
                for c in range(CB):
                    last = nc.tensor.transpose(TB[s][:, c * 128:(c + 1) * 128], y_t[s][:, c * 128:(c + 1) * 128],
                                               C("ident"))
                last.then_inc(out_turned[s], 1)

            def block(s, k, first=False, final=False):
                hidden(s, k, 0)
                hidden(s, k, 1)
                if not first:
                    turn_out(1 - s, k - 1 + s)
                hidden(s, k, 2)
                hidden(s, k, 3)
                if not final:
                    if not first:
                        pe.wait_ge(rows_out_ready[1 - s], k + s)
                    turn_in(1 - s, k + s)
                outputs(s, k)

            pe.wait_ge(table_ready, 1)
            turn_in(0, 0)
            block(0, 0, first=True)
            block(1, 0)
            with pe.Fori(1, NB // 2 - 1) as i:
                block(0, i)
                block(1, i)
            block(0, NB // 2 - 1)
            block(1, NB // 2 - 1, final=True)
            turn_out(1, NB // 2 - 1)

        def b_scalar(act):
            act.preload_act_table(ACT.Gelu_apprx_tanh)
            with act.Fori(0, NB // 2) as i:
                for s in range(2):
                    for c in range(FC):
                        act.wait_ge(hid_done[s], FC * i + c + 1)
                        if c == 0:
                            act.wait_ge(y_done[s], i)
                        nc.scalar.activation(hid[s][:, c, :], HB[s][c % 2], ACT.Gelu_apprx_tanh,
                                             bias=w_blk[s][:, FF + FC * D + c:FF + FC * D + c + 1]
                                             ).then_inc(hid_ready[s], 1)

        def b_vector(v):
            n = [0]

            def chain(ins):
                n[0] += 1
                ins.then_inc(table_step, 1)
                v.wait_ge(table_step, n[0])

            chain(v.memset(zeros[:], 0.0))
            chain(v.memset(ones_e[:], 1.0))
            v.wait_ge(count_done, 1)
            chain(v.tensor_copy(count[:], YB[0][:, 0:E]))
            chain(v.tensor_tensor(over[:], count[:].unsqueeze(2).to_broadcast([128, E, KMAX]),
                                  R("kblk").unsqueeze(1).to_broadcast([128, E, KMAX]), ALU.is_gt))
            chain(v.tensor_reduce(nblk[:], over[:], AX_X, ALU.add))
            chain(v.tensor_tensor_scan(ends[:], ones_e[:], nblk[:], 0.0, ALU.mult, ALU.add))
            blk = R("blk")[0:1, :]
            chain(v.tensor_tensor(past[:], blk.unsqueeze(2).to_broadcast([1, NB, E]),
                                  ends[0:1, :].unsqueeze(1).to_broadcast([1, NB, E]), ALU.is_ge))
            chain(v.tensor_reduce(blk_e[:], past[:], AX_X, ALU.add))
            chain(v.tensor_tensor(past[:], past[:], nblk[0:1, :].unsqueeze(1).to_broadcast([1, NB, E]), ALU.mult))
            chain(v.tensor_reduce(blk_done[:], past[:], AX_X, ALU.add))
            chain(v.tensor_tensor(blk_done[:], blk, blk_done[:], ALU.subtract))
            chain(v.tensor_scalar(blk_done[:], blk_done[:], float(BLK), None, ALU.mult))
            chain(v.scalar_tensor_tensor(out=blk_done[:], in0=blk_e[:], scalar=float(REGION), in1=blk_done[:],
                                         op0=ALU.mult, op1=ALU.add))
            chain(v.tensor_scalar(table[:, 0:NB], blk_done[:], float(E * REGION), None, ALU.min))
            chain(v.tensor_scalar(table[:, NB:2 * NB], blk_e[:], float(E - 1), None, ALU.min))
            v.tensor_copy(tails[:], count[0:1, :]).then_inc(table_ready, 1)
            chain(v.tensor_tensor(shift[:], ends[:], nblk[:], ALU.subtract))
            chain(v.tensor_scalar(shift[:], shift[:], float(BLK), None, ALU.mult))
            chain(v.tensor_tensor(shift[:], shift[:], R("first"), ALU.subtract))
            chain(v.tensor_tensor(over[:, 1:E, 0], shift[:, 1:E], shift[:, 0:E - 1], ALU.subtract))
            chain(v.tensor_scalar(out_rows[:], slots[:], shift[0:G, 0:1], None, ALU.add))
            for e in range(1, E):
                chain(v.tensor_scalar(moved[:], slots[:], float(e * REGION), over[0:G, e:e + 1, 0], ALU.is_ge, ALU.mult))
                chain(v.tensor_tensor(out_rows[:], out_rows[:], moved[:], ALU.add))
            v.sem_inc(out_rows_step, 1)

            def take_in(s, k):
                v.wait_ge(in_turned[s], k + 1)
                v.tensor_copy(x_t[s][:], TB[s]).then_inc(xt_ready[s], 1)

            def block(s, k, first=False, final=False):
                if not first:
                    v.wait_ge(out_turned[1 - s], k + s)
                    v.wait_ge(block_stored[1 - s], 16 * (k - 1 + s))
                    v.tensor_copy(rows_out[1 - s][:].rearrange("p c d -> p (c d)"), TB[1 - s]
                                  ).then_inc(rows_out_ready[1 - s], 1)
                if not final:
                    take_in(1 - s, k + s)
                v.wait_ge(y_done[s], k + 1)
                v.tensor_scalar(y_t[s][:], YB[s], w_blk[s][:, WCOLS - 1:WCOLS], None, ALU.add
                                ).then_inc(yt_ready[s], 1)

            take_in(0, 0)
            block(0, 0, first=True)
            block(1, 0)
            with v.Fori(1, NB // 2 - 1) as i:
                block(0, i)
                block(1, i)
            block(0, NB // 2 - 1)
            block(1, NB // 2 - 1, final=True)
            v.wait_ge(out_turned[1], NB // 2)
            v.wait_ge(block_stored[1], 16 * (NB // 2 - 1))
            v.tensor_copy(rows_out[1][:].rearrange("p c d -> p (c d)"), TB[1]).then_inc(rows_out_ready[1], 1)

        mem_b.close()

        mem_c = ExitStack()

        def pair_c(name, shape, dt=F32):
            return pair(name, shape, dt, mem_c)

        w_qkv, w_att, w_g = (sb("w_qkv", [128, 3 * D], F32, mem_c), sb("w_att", [128, D], F32, mem_c),
                             sb("w_g", [128, E2], F32, mem_c))
        q_neg = sb("q_neg", [128, 1], F32, mem_c)
        band, ident_h = sb("band", [128, cw["band"][1]], BF16, mem_c), sb("ident_h", [128, 128], BF16, mem_c)
        h1c, x2c = pair_c("h1c", [128, T]), pair_c("x2c", [128, T])
        ycho = pair_c("ycho", [G, 2 * NG, D])
        place, wdiag = pair_c("place", [G, 2 * NG], I32), pair_c("wdiag", [G, 2 * NG, G])
        sqc, rc, prec = pair_c("sqc", [128, T]), pair_c("rc", [128, T]), pair_c("prec", [128, T])
        x3, h2, h3, xm = pair_c("x3", [128, T]), pair_c("h2", [128, T]), pair_c("h3", [128, T]), pair_c("xm", [128, T])
        xpad, kpad = pair_c("xpad", [128, IMGS, KPAD]), pair_c("kpad", [128, IMGS, KPAD])
        qs = pair_c("qs", [128, T])
        val = pair_c("val", [KW, IMGS * NWIN, D])
        qdiag = [[sb(f"qdiag{s}{k}", [128, UB, HEADS, QB], F32, mem_c) for k in range(2)] for s in range(2)]
        ex = pair_c("ex", [128, UB, KW])
        smin = pair_c("smin", [128, UB])
        ssum = [[sb(f"ssum{s}{k}", [128, UB], F32, mem_c) for k in range(2)] for s in range(2)]
        qsel = pair_c("qsel", [128, UB, QB])
        ex_t = pair_c("ex_t", [KW, UB, 128])
        own = pair_c("own", [128, UB, 128])
        att = pair_c("att", [128, T])
        means = sb("means", [128, NI], F32, mem_c)
        l16, c16, p16 = (sb("l16", [NI, E2], F32, mem_c), sb("c16", [NI, E2], F32, mem_c),
                         sb("p16", [NI, E2], F32, mem_c))
        m16, b16, g16, gdiag = (sb("m16", [NI, 1], F32, mem_c), sb("b16", [NI, 1], F32, mem_c),
                                sb("g16", [NI, 1], F32, mem_c), sb("gdiag", [NI, NI], F32, mem_c))
        pick_i = sb("pick_i", [NI, 1], I32, mem_c)
        gate_bc = sb("gate_bc", [128, NI], F32, mem_c)
        wsel = pair_c("wsel", [128, IMGS, D + 1])
        outs = pair_c("outs", [128, T])

        loaded_c, c_ready = sem("loaded_c"), sem("c_ready")
        h_landed, choice_step, gathered = sems("h_landed"), sems("choice_step"), sems("gathered")
        moe_done, trunk_step = sems("moe_done"), sems("trunk_step")
        qk_done, qk_ready = sems("qk_done"), sems("qk_ready")
        val_done, val_ready, qdiag_ready = sems("val_done"), sems("val_ready"), sems("qdiag_ready")
        scores_done, min_ready, ex_ready = sems("scores_done"), sems("min_ready"), sems("ex_ready")
        soft_step = sems("soft_step")
        ext_done, ext_ready, pv_done, own_ready = sems("ext_done"), sems("ext_ready"), sems("pv_done"), sems("own_ready")
        heads_done, att_ready, proj_done = sems("heads_done"), sems("att_ready"), sems("proj_done")
        tail_step, router_pe, pick_step, pick_exp = (sems("tail_step"), sem("router_pe"), sem("pick_step"),
                                                     sem("pick_exp"))
        gate_ready, wsel_landed = sem("gate_ready"), sems("wsel_landed")
        last_done, out_step, out_stored = sems("last_done"), sems("out_step"), sems("out_stored")
        LNC = 3
        LN0 = LNA * ITERS
        RS0 = RSA * ITERS
        TRUNK = 4
        TAIL = 3
        SOFT = 2
        PICK = 9
        ITEMS = [(u, s) for u in range(NU) for s in range(2)]

        def item(j):
            return ITEMS[j] if 0 <= j < len(ITEMS) else None

        def first(n):
            return isinstance(n, int) and n == 0

        def c_steps(eng, trunk, attention, tail):
            trunk(0)
            attention(0, last=False, more=True)
            tail(0)
            trunk(1)
            if ITERS > 2:
                with eng.Fori(1, ITERS - 1) as i:
                    attention(i, last=True, more=True)
                    tail(i)
                    trunk(i + 1)
            attention(ITERS - 1, last=True, more=False)
            tail(ITERS - 1)

        def c_sync(sp):
            for dst, src in ((w_qkv, "w_qkv"), (w_att, "w_att"), (w_g, "w_g")):
                sp.dma_start(dst[:], a[src]).then_inc(loaded_c, 16)

            def load(n):
                for s in range(2):
                    sp.dma_start(h1c[s][:], h1_dram[:, a_range(n, s)]).then_inc(h_landed[s], 16)
                    sp.dma_start(x2c[s][:], x2_dram[:, a_range(n, s)]).then_inc(h_landed[s], 16)

            def store(q):
                for s in range(2):
                    hold(sp, out_step[s], (IMGS + 1) * (q + 1))
                    sp.dma_start(a["out"][:, a_range(q, s)], outs[s][:]).then_inc(out_stored[s], 16)

            def attention(i, last, more):
                if more:
                    for s in range(2):
                        hold(sp, trunk_step[s], TRUNK * (i + 1))
                    load(i + 1)
                if last:
                    store(i - 1)
                    for s in range(2):
                        hold(sp, out_stored[s], 16 * i)

            def tail(i):
                hold(sp, pick_step, PICK * i + 6)
                for s in range(2):
                    for m in range(IMGS):
                        n = s * IMGS + m
                        e = sp.value_load(pick_i[n:n + 1, 0:1], min_val=0, max_val=E2 - 1)
                        sp.dma_start(wsel[s][:, m, :], a["w_last"][bass.DynSlice(e * 128, 128), :]
                                     ).then_inc(wsel_landed[s], 16)

            load(0)
            c_steps(sp, lambda n: None, attention, tail)
            store(ITERS - 1)
            for s in range(2):
                sp.wait_ge(out_stored[s], 16 * ITERS)

        def c_pool(pool):
            for s in range(2):
                pool.wait_ge(block_stored[s], 16 * (NB // 2))

            def gather(n, s, k):
                pool.indirect_dma_start(
                    out=ycho[s][:, k, :], out_offset=None, in_=expert_out[:, :],
                    in_offset=bass.IndirectOffsetOnAxis(ap=place[s][:, k:k + 1], axis=0)).then_inc(gathered[s], 16)

            def attention(i, last, more):
                todo = [(s, k) for s in range(2) for k in range(2 * NG)] if more else []
                for u, s in ITEMS:
                    if u == 0:
                        pool.wait_ge(qk_ready[s], 2 * i + 1)
                    if u >= 2:
                        pool.wait_ge(scores_done[s], NU * i + u - 1)
                    pool.tensor_tensor(
                        qdiag[s][u % 2][:],
                        qs[s][:, u * UB * QB:(u + 1) * UB * QB].rearrange("p (b q) -> p b q", b=UB).unsqueeze(2)
                        .to_broadcast([128, UB, HEADS, QB]),
                        C("head_rows").unsqueeze(1).unsqueeze(3).to_broadcast([128, UB, HEADS, QB]),
                        ALU.mult).then_inc(qdiag_ready[s], 1)
                    if u >= 2:
                        for s2, k in todo[:2]:
                            if k == 0:
                                hold(pool, choice_step[s2], 2 * i + 3)
                                hold(pool, moe_done[s2], i + 1)
                            gather(i + 1, s2, k)
                        todo = todo[2:]
                assert not todo

            for s in range(2):
                pool.wait_ge(choice_step[s], 1)
                for k in range(2 * NG):
                    gather(0, s, k)
            c_steps(pool, lambda n: None, attention, lambda i: None)

        def c_tensor(pe):
            pe.wait_ge(c_ready, 1)
            for s in range(2):
                pe.wait_ge(rows_out_ready[s], NB // 2)

            def moe(n, fresh):
                for s in range(2):
                    pe.wait_ge(gathered[s], 16 * 2 * NG * (n + 1))
                    pe.wait_ge(choice_step[s], 2 * n + 2)
                    if not fresh:
                        pe.wait_ge(logvar[s], RS0 + LNC * n)
                    for g in range(NG):
                        dst = P[s][0][:, g // 3, (g % 3) * G:(g % 3 + 1) * G]
                        for choice in range(2):
                            k = choice * NG + g
                            last = nc.tensor.matmul(dst, ycho[s][:, k, :], wdiag[s][:, k, :],
                                                    start=(choice == 0), stop=(choice == 1))
                    last.then_inc(moe_done[s], 1)

            def trunk(n):
                if first(n):
                    moe(0, True)
                for s in range(2):
                    pe.wait_ge(trunk_step[s], TRUNK * n + 1)
                    ln_pe(pe, s, prec[s][:], LN0 + LNC * n)
                if not first(n):
                    for s in range(2):
                        pe.wait_ge(tail_step[s], TAIL * n)
                    nc.tensor.matmul(P[0][0][0:NI, 0, 0:E2], means[:], w_g[:], start=True, stop=True
                                     ).then_inc(router_pe, 1)
                    pe.wait_ge(pick_step, PICK * (n - 1) + 1)
                for s in range(2):
                    ln_pe_var(pe, s, sqc[s][:], LN0 + LNC * n)
                for s in range(2):
                    pe.wait_ge(trunk_step[s], TRUNK * n + 3)
                    ln_pe(pe, s, h2[s][:], LN0 + LNC * n + 1)
                for s in range(2):
                    ln_pe_var(pe, s, sqc[s][:], LN0 + LNC * n + 1)
                for k in range(2):
                    for s in range(2):
                        if k == 0:
                            pe.wait_ge(trunk_step[s], TRUNK * n + 4)
                        for g in range(2):
                            last = nc.tensor.matmul(
                                P[s][k][:, g, 0:T2].rearrange("p (m n) -> p m n", m=2), w_qkv[:, k * D:(k + 1) * D],
                                xpad[s][:, 2 * g:2 * g + 2, WIN:WIN + S], start=True, stop=True)
                        last.then_inc(qk_done[s], 1)
                for r in range(NWIN):
                    for s in range(2):
                        if r < 4:
                            pe.wait_ge(qk_ready[s], 2 * n + (1 if r < 2 else 2))
                        else:
                            pe.wait_ge(val_ready[s], NWIN * n + r - 3)
                        for w in range(UB):
                            b = r * UB + w
                            m, j = b // NWIN, b % NWIN
                            last = nc.tensor.matmul(P[s][(r // 2) % 2][0:KW, r % 2, w * D:(w + 1) * D],
                                                    xpad[s][:, m, j * WIN:j * WIN + KW], w_qkv[:, 2 * D:3 * D],
                                                    start=True, stop=True)
                        last.then_inc(val_done[s], 1)

            def last_layer(q):
                pe.wait_ge(pick_step, PICK * (q + 1))
                nc.tensor.matmul(P[0][1][:, 0, 0:NI], C("ones")[0:NI, :], gdiag[:], start=True, stop=True
                                 ).then_inc(router_pe, 1)
                for s in (1, 0):
                    pe.wait_ge(wsel_landed[s], 16 * IMGS * (q + 1))
                    if s == 0:
                        pe.wait_ge(gate_ready, q + 1)
                    for m in range(IMGS):
                        last = nc.tensor.matmul(P[s][1][:, m // 2, (m % 2) * S:(m % 2 + 1) * S], wsel[s][:, m, 0:D],
                                                four(xm[s][:])[:, m, :], start=True, stop=True)
                    last.then_inc(last_done[s], 1)

            def attention(i, last, more):
                def scores(u, s):
                    pe.wait_ge(qdiag_ready[s], NU * i + u + 1)
                    b0 = (u * UB) % NQB
                    nc.tensor.matmul(P[s][0][:, 0, 0:UB * KW], ident_h[:], band[:, b0 * KW:(b0 + UB) * KW],
                                     start=True, stop=False)
                    for b in range(UB):
                        n = u * UB + b
                        m, qb = n // NQB, n % NQB
                        last = nc.tensor.matmul(P[s][0][:, 0, b * KW:(b + 1) * KW],
                                                qdiag[s][u % 2][:, b, :, :].rearrange("p h q -> p (h q)"),
                                                kpad[s][:, m, WIN * (qb // 2):WIN * (qb // 2) + KW],
                                                start=False, stop=(b == UB - 1))
                    last.then_inc(scores_done[s], 1)

                def turn(u, s):
                    pe.wait_ge(ex_ready[s], NU * i + u + 1)
                    for b in range(UB):
                        last = nc.tensor.transpose(P[s][0][0:KW, 1, b * 128:(b + 1) * 128], ex[s][:, b, :],
                                                   C("ident"))
                    last.then_inc(ext_done[s], 1)

                def values(u, s):
                    pe.wait_ge(ext_ready[s], NU * i + u + 1)
                    for b in range(UB):
                        n = u * UB + b
                        m, qb = n // NQB, n % NQB
                        last = nc.tensor.matmul(P[s][1][:, 0, b * 128:(b + 1) * 128], ex_t[s][:, b, :],
                                                val[s][:, m * NWIN + qb // 2, :], start=True, stop=True)
                    last.then_inc(pv_done[s], 1)

                def heads(u, s):
                    pe.wait_ge(own_ready[s], NU * i + u + 1)
                    pe.wait_ge(soft_step[s], SOFT * (NU * i + u + 1))
                    if u:
                        pe.wait_ge(att_ready[s], NU * i + u)
                    for b in range(UB):
                        last = nc.tensor.matmul(P[s][1][:, 1, b * QB:(b + 1) * QB], own[s][:, b, :],
                                                qsel[s][:, b, :], start=True, stop=True)
                    last.then_inc(heads_done[s], 1)

                for s in range(2):
                    pe.wait_ge(val_ready[s], NWIN * (i + 1))
                    scores(0, s)
                if last:
                    last_layer(i - 1)
                for j in range(len(ITEMS) + 2):
                    if item(j):
                        turn(*item(j))
                    if item(j + 2):
                        scores(*item(j + 2))
                    if item(j - 1):
                        u, s = item(j - 1)
                        if u == 0 and last:
                            pe.wait_ge(out_step[s], (IMGS + 1) * (i - 1) + IMGS)
                        values(u, s)
                    if item(j - 2):
                        heads(*item(j - 2))
                for s in range(2):
                    pe.wait_ge(att_ready[s], NU * (i + 1))
                    for g in range(2):
                        done = nc.tensor.matmul(P[s][0][:, g, 0:T2], w_att[:], two(att[s][:])[:, g, :],
                                                start=True, stop=True)
                    done.then_inc(proj_done[s], 1)
                for s in range(2):
                    pe.wait_ge(tail_step[s], TAIL * i + 1)
                    ln_pe(pe, s, h3[s][:], LN0 + LNC * i + 2)
                for s in range(2):
                    ln_pe_var(pe, s, sqc[s][:], LN0 + LNC * i + 2)
                if more:
                    moe(i + 1, False)

            def trunk_after(n):
                if not first(n):
                    for s in range(2):
                        pe.wait_ge(tail_step[s], TAIL * (n - 1) + 2)
                trunk(n)

            c_steps(pe, trunk_after, attention, lambda i: None)
            for s in range(2):
                pe.wait_ge(tail_step[s], TAIL * ITERS)
            nc.tensor.matmul(P[0][0][0:NI, 0, 0:E2], means[:], w_g[:], start=True, stop=True).then_inc(router_pe, 1)
            last_layer(ITERS - 1)

        def c_scalar(act):
            act.preload_act_table_set("natural_log_exp_and_others")
            act.wait_ge(c_ready, 1)

            def norm(n, k):
                for s in range(2):
                    ln_act_square(act, s, sqc[s][:], LN0 + LNC * n + k)
                for s in range(2):
                    ln_act_rstd(act, s, rc[s][:], LN0 + LNC * n + k, RS0 + LNC * n + k)

            def trunk_rest(n):
                norm(n, 1)
                for s in range(2):
                    act.wait_ge(qk_done[s], 2 * n + 1)
                    nc.scalar.activation(two(qs[s][:]), pv(s, 0), ACT.Identity, bias=q_neg[:, 0:1],
                                         scale=-float(HD) ** -0.5).then_inc(qk_ready[s], 1)
                for s in range(2):
                    act.wait_ge(qk_done[s], 2 * n + 2)
                    nc.scalar.activation(two_two(kpad[s][:])[:, :, :, WIN:WIN + S], pv4(s, 1), ACT.Identity,
                                         bias=V("k_b")).then_inc(qk_ready[s], 1)
                for r in range(NWIN):
                    for s in range(2):
                        act.wait_ge(val_done[s], NWIN * n + r + 1)
                        nc.scalar.activation(val[s][:, r * UB:(r + 1) * UB, :].rearrange("p w d -> p (w d)"),
                                             P[s][(r // 2) % 2][0:KW, r % 2, :], ACT.Copy).then_inc(val_ready[s], 1)

            def attention(i, last, more):
                def exps(u, s):
                    act.wait_ge(min_ready[s], NU * i + u + 1)
                    for b in range(UB):
                        done = nc.scalar.activation(ex[s][:, b, :], P[s][0][:, 0, b * KW:(b + 1) * KW], ACT.Exp,
                                                    bias=smin[s][:, b:b + 1], scale=-1.0,
                                                    accum_out=ssum[s][u % 2][:, b:b + 1])
                    done.then_inc(ex_ready[s], 1)

                for j in range(-2, len(ITEMS) + 2):
                    if item(j):
                        u, s = item(j)
                        act.wait_ge(ext_done[s], NU * i + u + 1)
                        nc.scalar.activation(ex_t[s][:].rearrange("p b r -> p (b r)"), P[s][0][0:KW, 1, :], ACT.Copy
                                             ).then_inc(ext_ready[s], 1)
                    if item(j + 2):
                        exps(*item(j + 2))
                    if item(j - 2):
                        u, s = item(j - 2)
                        act.wait_ge(heads_done[s], NU * i + u + 1)
                        nc.scalar.activation(att[s][:, u * UB * QB:(u + 1) * UB * QB], P[s][1][:, 1, 0:UB * QB],
                                             ACT.Identity, bias=V("v_b")).then_inc(att_ready[s], 1)

            def tail(i):
                norm(i, 2)

            def pick(i):
                act.wait_ge(pick_step, PICK * i + 7)
                nc.scalar.activation(p16[:], l16[:], ACT.Exp, accum_out=g16[:]).then_inc(pick_exp, 1)

            def trunk_and_pick(n):
                for s in range(2):
                    ln_act_square(act, s, sqc[s][:], LN0 + LNC * n)
                if not first(n):
                    pick(n - 1)
                for s in range(2):
                    ln_act_rstd(act, s, rc[s][:], LN0 + LNC * n, RS0 + LNC * n)
                trunk_rest(n)

            c_steps(act, trunk_and_pick, attention, tail)
            pick(ITERS - 1)

        def c_vector(v):
            v.wait_ge(loaded_c, 16 * 3)
            for s in range(2):
                v.memset(xpad[s][:], 0.0)
                v.memset(kpad[s][:], 0.0)
            v.tensor_copy(band[:], C("band"))
            v.tensor_copy(ident_h[:], C("ident"))
            v.tensor_scalar(q_neg[:], V("q_b"), -float(HD) ** -0.5, None, ALU.mult).then_inc(c_ready, 1)
            v.wait_ge(c_ready, 1)
            v.wait_ge(out_rows_step, 1)

            def choices(n):
                for s in range(2):
                    v.tensor_copy(place[s][:], out_rows[:, bass.DynSlice(n * 4 * NG + s * 2 * NG, 2 * NG)]
                                  ).then_inc(choice_step[s], 1)
                for s in range(2):
                    w = weights[:, bass.DynSlice(n * 4 * NG + s * 2 * NG, 2 * NG)]
                    v.tensor_tensor(wdiag[s][:], C("ident")[0:G, 0:G].unsqueeze(1).to_broadcast([G, 2 * NG, G]),
                                    w.unsqueeze(2).to_broadcast([G, 2 * NG, G]), ALU.mult).then_inc(choice_step[s], 1)

            def pre(n):
                for s in range(2):
                    v.wait_ge(moe_done[s], n + 1)
                    v.wait_ge(h_landed[s], 32 * n + 32)
                    v.tensor_tensor(two(prec[s][:]), pv(s, 0), two(x2c[s][:]), ALU.add).then_inc(trunk_step[s], 1)

            def trunk(n):
                for s in range(2):
                    v.wait_ge(rstd[s], RS0 + LNC * n + 1)
                    v.scalar_tensor_tensor(out=two(x3[s][:]), in0=pv(s, 1), scalar=V("ln3_g"), in1=two(rc[s][:]),
                                           op0=ALU.mult, op1=ALU.mult).then_inc(trunk_step[s], 1)
                for s in range(2):
                    v.wait_ge(trunk_step[s], TRUNK * n + 2)
                    v.scalar_tensor_tensor(out=h2[s][:], in0=x3[s][:], scalar=V("ln3_b"), in1=h1c[s][:],
                                           op0=ALU.add, op1=ALU.add).then_inc(trunk_step[s], 1)
                for s in range(2):
                    v.wait_ge(rstd[s], RS0 + LNC * n + 2)
                    v.tensor_tensor(two_two(xpad[s][:])[:, :, :, WIN:WIN + S], pv4(s, 1),
                                    two(rc[s][:]).rearrange("p g (m n) -> p g m n", m=2), ALU.mult
                                    ).then_inc(trunk_step[s], 1)

            def last_layer(q):
                v.wait_ge(router_pe, 2 * q + 2)
                v.tensor_copy(gate_bc[:], P[0][1][:, 0, 0:NI]).then_inc(gate_ready, 1)
                v.wait_ge(gate_ready, q + 1)
                for s in (1, 0):
                    v.wait_ge(last_done[s], q + 1)
                    for m in range(IMGS):
                        v.tensor_scalar(four(outs[s][:])[:, m, :], P[s][1][:, m // 2, (m % 2) * S:(m % 2 + 1) * S],
                                        wsel[s][:, m, D:D + 1], gate_bc[:, s * IMGS + m:s * IMGS + m + 1],
                                        ALU.add, ALU.mult).then_inc(out_step[s], 1)
                for s in (1, 0):
                    v.wait_ge(out_step[s], (IMGS + 1) * q + IMGS)
                    v.tensor_tensor(outs[s][:], outs[s][:], h3[s][:], ALU.add).then_inc(out_step[s], 1)

            def attention(i, last, more):
                def minimum(u, s):
                    v.wait_ge(scores_done[s], NU * i + u + 1)
                    v.tensor_reduce(smin[s][:], P[s][0][:, 0, 0:UB * KW].rearrange("p (b k) -> p b k", b=UB), AX_X,
                                    ALU.min).then_inc(min_ready[s], 1)

                minimum(0, 0)
                minimum(0, 1)
                if last:
                    last_layer(i - 1)
                for j in range(len(ITEMS) + 1):
                    if item(j + 2):
                        minimum(*item(j + 2))
                    if item(j - 1):
                        u, s = item(j - 1)
                        k = NU * i + u
                        sums = ssum[s][u % 2]
                        v.wait_ge(ex_ready[s], k + 1)
                        v.reciprocal(sums[:], sums[:]).then_inc(soft_step[s], 1)
                        v.wait_ge(soft_step[s], SOFT * k + 1)
                        if u:
                            v.wait_ge(heads_done[s], k)
                        v.tensor_tensor(qsel[s][:], C("query").unsqueeze(1).to_broadcast([128, UB, QB]),
                                        sums[:].unsqueeze(2).to_broadcast([128, UB, QB]), ALU.mult
                                        ).then_inc(soft_step[s], 1)
                        v.wait_ge(pv_done[s], k + 1)
                        v.tensor_tensor(own[s][:], P[s][1][:, 0, :].rearrange("p (b r) -> p b r", b=UB),
                                        C("head_block").unsqueeze(1).to_broadcast([128, UB, 128]), ALU.mult
                                        ).then_inc(own_ready[s], 1)
                    if j == 2 and more:
                        choices(i + 1)

            def tail(i):
                for s in range(2):
                    v.wait_ge(proj_done[s], i + 1)
                    v.scalar_tensor_tensor(out=two(h3[s][:]), in0=pv(s, 0), scalar=V("attn_b"), in1=two(h2[s][:]),
                                           op0=ALU.add, op1=ALU.add).then_inc(tail_step[s], 1)
                for s in range(2):
                    v.wait_ge(rstd[s], RS0 + LNC * i + 3)
                    v.tensor_tensor(two(xm[s][:]), pv(s, 1), two(rc[s][:]), ALU.mult).then_inc(tail_step[s], 1)

            def router(i):
                for s in range(2):
                    v.wait_ge(tail_step[s], TAIL * i + 2)
                    v.tensor_reduce(means[:, s * IMGS:(s + 1) * IMGS], four(xm[s][:]), AX_X, ALU.add
                                    ).then_inc(tail_step[s], 1)
                c_pick(v, i)

            def trunk_and_router(n):
                if first(n):
                    choices(0)
                    pre(0)
                else:
                    pre(n)
                    router(n - 1)
                trunk(n)

            c_steps(v, trunk_and_router, attention, tail)
            router(ITERS - 1)
            last_layer(ITERS - 1)

        def c_pick(v, i):
            done = [0]

            def step(ins):
                ins.then_inc(pick_step, 1)
                done[0] += 1

            def settle():
                v.wait_ge(pick_step, PICK * i + done[0])

            v.wait_ge(router_pe, 2 * i + 1)
            step(v.scalar_tensor_tensor(out=l16[:], in0=P[0][0][0:NI, 0, 0:E2], scalar=1.0 / S, in1=RR("bg")[0:NI, :],
                                        op0=ALU.mult, op1=ALU.add))
            settle()
            step(v.tensor_reduce(m16[:], l16[:], AX_X, ALU.max))
            settle()
            step(v.scalar_tensor_tensor(out=c16[:], in0=l16[:], scalar=m16[:, 0:1], in1=R("rev16")[0:NI, :],
                                        op0=ALU.is_equal, op1=ALU.mult))
            settle()
            step(v.tensor_reduce(b16[:], c16[:], AX_X, ALU.max))
            settle()
            step(v.tensor_scalar(b16[:], b16[:], -1.0, float(E2), ALU.mult, ALU.add))
            settle()
            step(v.tensor_copy(pick_i[:], b16[:]))
            step(v.tensor_scalar(l16[:], l16[:], m16[:, 0:1], None, ALU.subtract))
            v.wait_ge(pick_exp, i + 1)
            step(v.reciprocal(g16[:], g16[:]))
            settle()
            step(v.tensor_scalar(gdiag[:], C("ident")[0:NI, 0:NI], g16[:, 0:1], None, ALU.mult))
            assert done[0] == PICK

        mem_c.close()

        block = ctx.enter_context(nc.Block())

        @block.sync
        def _(sp):
            a_sync(sp)
            b_sync(sp)
            c_sync(sp)

        @block.gpsimd
        def _(pool):
            a_pool(pool)
            c_pool(pool)

        @block.scalar
        def _(act):
            a_scalar(act)
            b_scalar(act)
            c_scalar(act)

        @block.vector
        def _(v):
            a_vector(v)
            b_vector(v)
            c_vector(v)

        @block.tensor
        def _(pe):
            a_tensor(pe)
            b_tensor(pe)
            c_tensor(pe)


def kernel(**inputs):
    import concourse.bacc as _bacc
    from concourse.bass_utils import run_bass_kernel_spmd as _run

    f = {k: np.asarray(v) for k, v in inputs.items()}
    images = f["x"].shape[0]
    steps = images // IMGS

    def chunks(w, n):
        return w.reshape(n, 128)

    x = f["x"].reshape(steps, IMGS, CHANNELS, GW, PATCH, GH, PATCH).transpose(0, 2, 4, 6, 1, 3, 5)
    x = x.reshape(steps, KC, 128, IMGS * NPATCH).transpose(0, 2, 1, 3)
    w_tok = f["L0_tok_W"].reshape(D, PATCH, PATCH, CHANNELS).transpose(3, 1, 2, 0).reshape(KC, 128, D).transpose(1, 0, 2)
    in_w, in_b = f["L0_attn_in_proj_w"].reshape(6, 128, D), f["L0_attn_in_proj_b"].reshape(6, 128)
    de_w, de_b = f["L0_attn_delta_w"].reshape(2, 128, D), f["L0_attn_delta_b"].reshape(2, 128)
    order_w = np.stack([de_w[0], de_w[1], in_w[4], in_w[5], in_w[0], in_w[1], in_w[2], in_w[3]])
    order_b = np.stack([de_b[0], de_b[1], in_b[4], in_b[5], in_b[0], in_b[1], in_b[2], in_b[3]])
    conv_w = f["L0_attn_conv_w"].reshape(2, 128, 4).transpose(1, 0, 2).reshape(128, 8)
    parts = {
        "ln_w": f["L0_attn_ln_w"], "ln_b": f["L0_attn_ln_b"], "in_b": order_b.T, "conv_w": conv_w,
        "conv_b": f["L0_attn_conv_b"].reshape(2, 128).T, "state_mix": f["L0_attn_state_mix"].reshape(2, 128).T,
        "skip": f["L0_attn_skip_scale"].reshape(2, 128).T, "out_b": f["L0_attn_out_proj_b"], "tok_b": f["L0_tok_b"],
        "cls": f["L0_tok_cls_token"], "mr_b": f["L0_ffn_mr_b"].T, "ln1_g": f["L0_ffn_ln1_g"],
        "ln1_b": f["L0_ffn_ln1_b"], "mv_b": f["L0_ffn_mv_b"].T, "ln2_g": f["L0_ffn_ln2_g"],
        "ln2_b": f["L0_ffn_ln2_b"], "ln3_g": f["L0_ffn_ln3_g"], "ln3_b": f["L0_ffn_ln3_b"],
        "q_b": f["L1_attn_b_qkv"][0:D], "k_b": f["L1_attn_b_qkv"][D:2 * D], "v_b": f["L1_attn_b_qkv"][2 * D:],
        "attn_b": f["L1_attn_b_out"],
    }
    col = np.concatenate([parts[k].reshape(128, n) for k, (_, n) in COLS.items()], axis=1)
    rparts = {"pos": f["L0_tok_pos_emb"], "alpha": f["L0_ffn_mv_alpha"], "gate_b": f["L0_ffn_gate_b"],
              "bg": f["L1_ffn_bg"]}
    row = np.concatenate([rparts[k].reshape(1, n) for k, (_, n) in ROWS.items()], axis=1)
    w_exp = np.concatenate([
        f["L0_ffn_e_w1"],
        f["L0_ffn_e_w2"].reshape(E, FC, 128, D).transpose(0, 2, 1, 3).reshape(E, 128, FC * D),
        f["L0_ffn_e_b1"].reshape(E, FC, 128).transpose(0, 2, 1),
        f["L0_ffn_e_b2"][:, :, None],
    ], axis=2).reshape(E * 128, -1)
    w_last = np.concatenate([f["L1_ffn_We"], f["L1_ffn_be"][:, :, None]], axis=2).reshape(E2 * 128, D + 1)
    arrays = {
        "x": x, "w_tok": w_tok, "w_in": order_w.transpose(2, 0, 1),
        "w_out": f["L0_attn_out_proj_w"].reshape(D, 2, 128).transpose(2, 1, 0),
        "w_mr": f["L0_ffn_mr_w"].transpose(1, 0, 2), "w_mv": f["L0_ffn_mv_w"].transpose(1, 0, 2),
        "w_gate": f["L0_ffn_gate_w"], "col": col, "row": row, "w_exp": w_exp, "w_last": w_last,
        "w_qkv": f["L1_attn_w_qkv"], "w_att": f["L1_attn_w_out"], "w_g": f["L1_ffn_Wg"],
        "cst": const_tiles()[1], "crow": const_rows(images)[1],
    }
    arrays = {k: np.ascontiguousarray(v) for k, v in arrays.items()}
    nc = _bacc.Bacc("TRN2", target_bir_lowering=False, num_devices=1)
    a = {k: nc.dram_tensor(f"{k}_in", v.shape, mybir.dt.from_np(v.dtype), kind="ExternalInput").ap()
         for k, v in arrays.items()}
    a["out"] = nc.dram_tensor("out", (128, images * S), F32, kind="ExternalOutput").ap()
    build(nc, images, a)
    r = _run(nc, [{f"{k}_in": v for k, v in arrays.items()}], core_ids=[0])
    out = r.results[0]["out"]
    return np.ascontiguousarray(out.reshape(D, images, S).transpose(1, 2, 0))
```

```python
from contextlib import ExitStack

import numpy as np

import concourse.bass as bass
from concourse import mybir

F32 = mybir.dt.float32
I32 = mybir.dt.int32
BF16 = mybir.dt.bfloat16
ALU = mybir.AluOpType
ACT = mybir.ActivationFunctionType
AX_X = mybir.AxisListType.X

D = 128
PATCH = 16
CHANNELS = 3
KC = CHANNELS * PATCH * PATCH // 128
GW, GH = 176 // PATCH, 208 // PATCH
NPATCH = GW * GH
S = NPATCH + 1
IMGS = 4
T = IMGS * S
T2 = T // 2
G = 96
NG = T // G
E = 8
FF = 512
FC = FF // 128
BLK = 512
CB = BLK // 128
HEADS = 8
HD = D // HEADS
WIN = 32
QB = 16
NQB = S // QB
KW = 96
KPAD = 224
NWIN = (NQB + 1) // 2
UB = 4
NU = IMGS * NQB // UB
NI = 2 * IMGS
E2 = 16
EPS = 1e-5
OUT = 1e30

COLS = {}
for _name, _n in (("ln_w", 1), ("ln_b", 1), ("in_b", 8), ("conv_w", 8), ("conv_b", 2), ("state_mix", 2),
                  ("skip", 2), ("out_b", 1), ("tok_b", 1), ("cls", 1), ("mr_b", 3), ("ln1_g", 1), ("ln1_b", 1),
                  ("mv_b", 3), ("ln2_g", 1), ("ln2_b", 1), ("ln3_g", 1), ("ln3_b", 1), ("q_b", 1), ("k_b", 1),
                  ("v_b", 1), ("attn_b", 1)):
    COLS[_name] = (sum(n for _, n in COLS.values()), _n)
NCOLS = sum(n for _, n in COLS.values())
ROWS = {}
for _name, _n in (("pos", S), ("alpha", 3), ("gate_b", E), ("bg", E2)):
    ROWS[_name] = (sum(n for _, n in ROWS.values()), _n)
NROWS = sum(n for _, n in ROWS.values())


def sizes(images):
    tokens = images * S
    region = -(-tokens // BLK) * BLK + BLK
    blocks = (2 * tokens + E * (BLK - 1)) // BLK
    blocks += blocks % 2
    return tokens, region, blocks


def const_rows(images):
    tokens, region, blocks = sizes(images)
    kmax = -(-tokens // BLK) + 1
    parts = {
        "first": np.arange(E) * region,
        "rev": np.arange(E, 0, -1),
        "rev16": np.arange(E2, 0, -1),
        "blk": np.arange(blocks),
        "kblk": np.arange(kmax) * BLK,
    }
    where, at = {}, 0
    for k, v in parts.items():
        where[k] = (at, len(v))
        at += len(v)
    return where, np.concatenate(list(parts.values())).astype(np.float32)[None, :]


def const_tiles():
    p = np.arange(128)
    band = np.full((128, NQB, KW), OUT, np.float32)
    for b in range(NQB):
        q = b * QB + np.arange(128) % QB
        key = WIN * (b // 2) - WIN + np.arange(KW)
        ok = (abs(key[None, :] - q[:, None]) <= WIN) & (key >= 0)[None, :] & (key < S)[None, :]
        band[:, b, :][ok] = 0.0
    band = np.concatenate([band, band[:, :UB - 1]], axis=1)
    parts = {
        "center": np.eye(128) - 1.0 / D,
        "mean": np.full((128, 128), 1.0 / D),
        "ident": np.eye(128),
        "before": (p[:, None] < p[None, :])[:, :G],
        "ones": np.ones((128, 128)),
        "head_rows": (p[:, None] // HD == np.arange(HEADS)[None, :]),
        "band": band.reshape(128, -1),
    }
    where, at = {}, 0
    for k, v in parts.items():
        where[k] = (at, v.shape[1])
        at += v.shape[1]
    return where, np.concatenate([np.asarray(v, np.float32) for v in parts.values()], axis=1)


def build(nc, images, a):
    tokens, REGION, NB = sizes(images)
    ITERS = images // (2 * IMGS)
    cw, _ = const_tiles()
    rw, _ = const_rows(images)
    KMAX = rw["kblk"][1]
    assert S % QB == 0 and S % 4 == 0 and T % G == 0 and IMGS * NQB % UB == 0

    with ExitStack() as ctx:
        def sem(name):
            return ctx.enter_context(nc.semaphore(name))

        def sems(name):
            return [sem(f"{name}{s}") for s in range(2)]

        def sb(name, shape, dt=F32, where=ctx):
            return where.enter_context(nc.sbuf_tensor(name, shape, dt))

        expert_in = nc.dram_tensor("expert_in", (E * REGION + BLK, D), F32, kind="Internal").ap()
        expert_out = nc.dram_tensor("expert_out", (NB * BLK, D), F32, kind="Internal").ap()
        h1_dram = nc.dram_tensor("h1_dram", (128, tokens), F32, kind="Internal").ap()
        x2_dram = nc.dram_tensor("x2_dram", (128, tokens), F32, kind="Internal").ap()

        P = [[ctx.enter_context(nc.psum_tensor(f"psum{s}{k}", [128, 2, 512], F32)) for k in range(2)]
             for s in range(2)]

        def pv(s, k):
            return P[s][k][:, :, 0:T2]

        def two(ap):
            return ap.rearrange("p (g n) -> p g n", g=2)

        def four(ap):
            return ap.rearrange("p (m n) -> p m n", m=IMGS)

        def two_two(ap):
            return ap.rearrange("p (g m) n -> p g m n", g=2)

        def pv4(s, k):
            return pv(s, k).rearrange("p g (m n) -> p g m n", m=2)

        cst = sb("cst", [128, sum(n for _, n in cw.values())])
        crow = sb("crow", [128, sum(n for _, n in rw.values())])
        col = sb("col", [128, NCOLS])
        row = sb("row", [128, NROWS])

        def C(name):
            o, n = cw[name]
            return cst[:, o:o + n]

        def R(name):
            o, n = rw[name]
            return crow[:, o:o + n]

        def V(name, k=0):
            o, n = COLS[name]
            return col[:, o + k:o + k + 1]

        def RR(name):
            o, n = ROWS[name]
            return row[:, o:o + n]

        slots = sb("slots", [G, ITERS * 4 * NG])
        weights = sb("weights", [G, ITERS * 4 * NG])
        out_rows = sb("out_rows", [G, ITERS * 4 * NG])
        chosen = sb("chosen", [G, E])
        table = sb("table", [1, 2 * NB], I32)
        tails = sb("tails", [1, E], I32)

        loaded = sem("loaded")
        prep = sem("prep")
        prep_act = sem("prep_act")
        prep_pe = sem("prep_pe")
        consts_ready = sem("consts_ready")
        centered, squared, variance = sems("centered"), sems("squared"), sems("variance")
        logvar, rstd, normed = sems("logvar"), sems("rstd"), sems("normed")

        held = {"sync": sem("held_sync"), "pool": sem("held_pool")}

        def first(n):
            return isinstance(n, int) and n == 0

        def hold(eng, s, value):
            eng.wait_ge(s, value)
            eng.sem_inc(held["pool" if eng is nc.gpsimd else "sync"], 1)

        def ln_pe(pe, s, src, k):
            for g in range(2):
                last = nc.tensor.matmul(P[s][1][:, g, 0:T2], C("center"), two(src)[:, g, :], start=True, stop=True)
            last.then_inc(centered[s], 1)

        def ln_pe_var(pe, s, sq, k):
            pe.wait_ge(squared[s], k + 1)
            for g in range(2):
                last = nc.tensor.matmul(P[s][0][:, g, 0:T2], C("mean"), two(sq)[:, g, :], start=True, stop=True)
            last.then_inc(variance[s], 1)

        def ln_act_square(act, s, sq, k):
            act.wait_ge(centered[s], k + 1)
            nc.scalar.activation(two(sq), pv(s, 1), ACT.Square).then_inc(squared[s], 1)

        def ln_act_rstd(act, s, r, k, kr):
            act.wait_ge(variance[s], k + 1)
            nc.scalar.activation(two(r), pv(s, 0), ACT.Ln, bias=eps_col[:, 0:1]).then_inc(logvar[s], 1)
            act.wait_ge(logvar[s], kr + 1)
            nc.scalar.activation(r, r, ACT.Exp, scale=-0.5).then_inc(rstd[s], 1)

        eps_col = sb("eps_col", [128, 2])

        mem_a = ExitStack()
        w_tok = sb("w_tok", [128, KC, D], F32, mem_a)
        w_in = sb("w_in", [128, 8, 128], F32, mem_a)
        w_out = sb("w_out", [128, 2, D], F32, mem_a)
        w_mr = sb("w_mr", [128, 3, D], F32, mem_a)
        w_mv = sb("w_mv", [128, 3, D], F32, mem_a)
        w_gate = sb("w_gate", [128, E], F32, mem_a)
        in_bias = sb("in_bias", [128, 8], F32, mem_a)
        in_half = sb("in_half", [128, 8], F32, mem_a)
        taps = sb("taps", [128, 8], F32, mem_a)
        conv_b = sb("conv_b", [128, 2], F32, mem_a)
        decay = sb("decay", [128, 2], F32, mem_a)
        decays = [sb(f"decays{c}", [128, T], F32, mem_a) for c in range(2)]
        posb = sb("posb", [128, S], F32, mem_a)
        mr_bias = sb("mr_bias", [128, 1], F32, mem_a)
        alpha = sb("alpha", [128, 3], F32, mem_a)
        tiny = sb("tiny", [128, 8], F32, mem_a)

        def pair(name, shape, dt=F32, where=None):
            return [sb(f"{name}{s}", shape, dt, where or mem_a) for s in range(2)]

        xin = pair("xin", [128, KC, IMGS * NPATCH])
        h0, sq, ra, rb = pair("h0", [128, T]), pair("sq", [128, T]), pair("ra", [128, T]), pair("rb", [128, T])
        xn1, xn2, res = pair("xn1", [128, T]), pair("xn2", [128, T]), pair("res", [128, T])
        unit = [[sb(f"unit{s}{u}", [128, T], F32, mem_a) for u in range(8)] for s in range(2)]
        zproj = [[sb(f"zproj{s}{c}", [128, T], F32, mem_a) for c in range(2)] for s in range(2)]
        pj = [[sb(f"pj{s}{c}", [128, IMGS, S + 3], F32, mem_a) for c in range(2)] for s in range(2)]
        acc = [[sb(f"acc{s}{c}", [128, T], F32, mem_a) for c in range(2)] for s in range(2)]
        h1, x2 = pair("h1", [128, T]), pair("x2", [128, T])
        pool2, pool4 = pair("pool2", [128, T // 2]), pair("pool4", [128, T // 4])
        rows = pair("rows", [G, NG, D])
        logit, lmask, cand = pair("logit", [G, NG, E]), pair("lmask", [G, NG, E]), pair("cand", [G, NG, E])
        pick1, pick2, picks = pair("pick1", [G, NG, E]), pair("pick2", [G, NG, E]), pair("picks", [G, NG, E])
        top1, top2, best = pair("top1", [G, NG]), pair("top2", [G, NG]), pair("best", [G, NG])
        wexp, wsum = pair("wexp", [G, NG]), pair("wsum", [G, NG])
        newly = pair("newly", [G, E])
        slot = pair("slot", [G, 2 * NG])
        slot_i = pair("slot_i", [G, 2 * NG], I32)
        PROJ, DELTA, DRIVE, GATE = (0, 3), (1, 4), (2, 5), (6, 7)

        x_landed, tok_done, embedded = sems("x_landed"), sems("tok_done"), sems("embedded")
        res_done = sems("res_done")
        unit_done, unit_act = sems("unit_done"), sems("unit_act")
        delta_ready, drive_ready = sems("delta_ready"), sems("drive_ready")
        mix_step, summed = sems("mix_step"), sems("summed")
        out_done, h1_ready, h1_stored = sems("out_done"), sems("h1_ready"), sems("h1_stored")
        ffn_step, mr_done = sems("ffn_step"), sems("mr_done")
        mv_done, gelu_done = sems("mv_done"), sems("gelu_done")
        x2_stored = sems("x2_stored")
        turned, rows_ready, route_step = sems("turned"), sems("rows_ready"), sems("route_step")
        wexp_done, rank_done, slots_ready, scattered = (sems("wexp_done"), sems("rank_done"), sems("slots_ready"),
                                                        sems("scattered"))
        chosen_new = sem("chosen_new")
        LNA = 4
        RSA = LNA + 1
        CONV_AT, STATES_AT, GATE_AT = (0, 6), (5, 12), (11, 14)
        MIX = 15
        FFN = 11
        x0, x1, view = xn1, xn2, [[unit[s][u] for u in (0, 1, 2)] for s in range(2)]
        pre = rb

        def logit_bank(s):
            return P[s][0][0:G, 1, 2 * 128:2 * 128 + NG * E]

        def a_range(i, s):
            return bass.DynSlice((2 * i + s) * T, T)

        def a_steps(eng, step):
            step(0, True)
            with eng.Fori(1, ITERS - 1) as i:
                step(i, True)
            step(ITERS - 1, False)

        def a_sync(sp):
            for dst, src in ((cst, "cst"), (crow, "crow"), (col, "col"), (row, "row"), (w_tok, "w_tok"),
                             (w_in, "w_in"), (w_out, "w_out"), (w_mr, "w_mr"), (w_mv, "w_mv"), (w_gate, "w_gate")):
                src = a[src]
                if src.shape[0] == 1:
                    src = src.to_broadcast([128, src.shape[1]])
                sp.dma_start(dst[:], src).then_inc(loaded, 16)
            def load(n):
                for s in range(2):
                    if not first(n):
                        hold(sp, tok_done[s], 2 * n)
                    sp.dma_start(xin[s][:], a["x"][bass.DynSlice(2 * n + s, 1)].rearrange("o p k n -> (o p) k n")
                                 ).then_inc(x_landed[s], 16)

            def step(i, more):
                if more:
                    load(i + 1)
                for s in range(2):
                    hold(sp, h1_ready[s], i + 1)
                    sp.dma_start(h1_dram[:, a_range(i, s)], h1[s][:]).then_inc(h1_stored[s], 16)
                for s in range(2):
                    hold(sp, ffn_step[s], FFN * i + 11)
                    sp.dma_start(x2_dram[:, a_range(i, s)], x2[s][:]).then_inc(x2_stored[s], 16)

            load(0)
            a_steps(sp, step)
            for s in range(2):
                sp.wait_ge(h1_stored[s], 16 * ITERS)
                sp.wait_ge(x2_stored[s], 16 * ITERS)

        NLOADS = 10

        def a_prep_vector(v):
            n = [0]

            def step(ins):
                n[0] += 1
                ins.then_inc(prep, 1)

            def settle():
                v.wait_ge(prep, n[0])

            step(v.memset(eps_col[:, 0:1], EPS))
            step(v.memset(eps_col[:, 1:2], EPS * EPS))
            step(v.memset(chosen[:], 0.0))
            for s in range(2):
                for c in range(2):
                    step(v.memset(pj[s][c][:], 0.0))
            v.wait_ge(loaded, 16 * NLOADS)
            v.wait_ge(prep_pe, 1)
            step(v.tensor_scalar(w_in[:], w_in[:], V("ln_w"), None, ALU.mult))
            o, _ = COLS["in_b"]
            step(v.tensor_tensor(in_bias[:], P[0][0][:, 0, 0:8], col[:, o:o + 8], ALU.add))
            settle()
            step(v.tensor_scalar(in_half[:], in_bias[:], 0.5, None, ALU.mult))
            for c in range(2):
                o, _ = COLS["conv_w"]
                step(v.tensor_scalar(taps[:, 4 * c:4 * c + 4], col[:, o + 4 * c:o + 4 * c + 4], V("skip", c), None,
                                     ALU.mult))
                step(v.tensor_scalar(conv_b[:, c:c + 1], V("conv_b", c), V("skip", c), 2.0, ALU.mult, ALU.mult))
            step(v.tensor_scalar(w_out[:], w_out[:], 0.25, None, ALU.mult))
            v.wait_ge(prep_act, 1)
            step(v.tensor_scalar(decay[:], decay[:], 0.5, 0.5, ALU.mult, ALU.add))
            settle()
            for c in range(2):
                step(v.tensor_copy(decays[c][:], decay[:, c:c + 1].to_broadcast([128, T])))
            settle()
            for c in range(2):
                step(v.memset(four(decays[c][:])[:, :, 0:1], 0.0))
            step(v.tensor_scalar(posb[:], RR("pos"), V("tok_b"), None, ALU.add))
            settle()
            step(v.tensor_tensor(posb[:, 0:1], RR("pos")[:, 0:1], V("cls"), ALU.add))
            settle()
            for s in range(2):
                step(v.tensor_copy(four(h0[s][:])[:, :, 0], posb[:, 0:1].to_broadcast([128, IMGS])))
            for r in range(3):
                step(v.tensor_scalar(w_mr[:, r, :], w_mr[:, r, :], 1.0 / (3 * 2 ** r), None, ALU.mult))
            step(v.tensor_tensor(tiny[:, 0:1], V("mr_b", 0), V("mr_b", 1), ALU.add))
            settle()
            step(v.tensor_tensor(tiny[:, 1:2], tiny[:, 0:1], V("mr_b", 2), ALU.add))
            settle()
            step(v.tensor_scalar(mr_bias[:], tiny[:, 1:2], 1.0 / 3, None, ALU.mult))
            step(v.tensor_reduce(tiny[:, 2:3], RR("alpha"), AX_X, ALU.max))
            settle()
            step(v.tensor_scalar(alpha[:], RR("alpha"), tiny[:, 2:3], None, ALU.subtract))
            settle()
            v.sem_inc(consts_ready, 1)
            v.wait_ge(prep_act, 2)
            step(v.tensor_reduce(tiny[:, 3:4], alpha[:], AX_X, ALU.add))
            settle()
            step(v.reciprocal(tiny[:, 4:5], tiny[:, 3:4]))
            settle()
            step(v.tensor_scalar(alpha[:], alpha[:], tiny[:, 4:5], None, ALU.mult))
            settle()
            v.sem_inc(consts_ready, 1)

        def a_prep_scalar(act):
            act.wait_ge(loaded, 16 * NLOADS)
            o, _ = COLS["state_mix"]
            nc.scalar.activation(decay[:], col[:, o:o + 2], ACT.Tanh, scale=0.5).then_inc(prep_act, 1)
            act.wait_ge(consts_ready, 1)
            nc.scalar.activation(alpha[:], alpha[:], ACT.Exp).then_inc(prep_act, 1)

        def a_prep_tensor(pe):
            pe.wait_ge(loaded, 16 * NLOADS)
            for u in range(8):
                last = nc.tensor.matmul(P[0][0][:, 0, u:u + 1], w_in[:, u, :], V("ln_b"), start=True, stop=True)
            last.then_inc(prep_pe, 1)

        def a_tensor(pe):
            a_prep_tensor(pe)
            pe.wait_ge(consts_ready, 2)

            def embed(n):
                for s in range(2):
                    pe.wait_ge(x_landed[s], 16 * n + 16)
                    if not first(n):
                        pe.wait_ge(unit_act[s], 8 * n - 1)
                    for g in range(2):
                        for k in range(KC):
                            last = nc.tensor.matmul(P[s][0][:, g, 0:2 * NPATCH], w_tok[:, k, :],
                                                    xin[s][:, k, g * 2 * NPATCH:(g + 1) * 2 * NPATCH],
                                                    start=(k == 0), stop=(k == KC - 1))
                        last.then_inc(tok_done[s], 1)

            def center0(n):
                for s in range(2):
                    pe.wait_ge(embedded[s], 2 * n + 2)
                    if not first(n):
                        pe.wait_ge(ffn_step[s], FFN * (n - 1) + 10)
                    ln_pe(pe, s, h0[s][:], LNA * n)

            def ranks(i):
                for s in range(2):
                    if not (isinstance(i, int) and i == ITERS - 1):
                        pe.wait_ge(unit_act[s], 8 * (i + 1) + 2)
                    pe.wait_ge(route_step[s], ROUTE * i + 13)
                    if s or not first(i):
                        pe.wait_ge(chosen_new, 2 * i + s)
                    dst = P[s][1][0:G, 1, 0:NG * E].rearrange("p (g e) -> p g e", e=E)
                    nc.tensor.matmul(dst, C("before")[0:G, :], picks[s][:], start=True, stop=False)
                    for g in range(NG - 1):
                        nc.tensor.matmul(dst[:, g + 1:NG, :], C("ones")[0:G, 0:G],
                                         picks[s][:, g:g + 1, :].to_broadcast([G, NG - 1 - g, E]),
                                         start=False, stop=False)
                    nc.tensor.matmul(dst, C("ones")[0:G, 0:G], chosen[:].unsqueeze(1).to_broadcast([G, NG, E]),
                                     start=False, stop=True).then_inc(rank_done[s], 1)

            def step(i, more):
                for s in range(2):
                    if not first(i):
                        pe.wait_ge(rows_ready[s], 2 * i)
                    ln_pe_var(pe, s, sq[s][:], LNA * i)
                for u in range(8):
                    if u == 3 and not first(i):
                        ranks(i - 1)
                    for s in range(2):
                        if u == 0:
                            pe.wait_ge(normed[s], 2 * i + 1)
                        if u == 1:
                            pe.wait_ge(normed[s], 2 * i + 2)
                        if u == 3 and not first(i):
                            pe.wait_ge(route_step[s], ROUTE * (i - 1) + 16)
                        if u >= 2:
                            pe.wait_ge(unit_act[s], 8 * i + u - 1)
                        for g in range(2):
                            last = nc.tensor.matmul(P[s][u % 2][:, g, 0:T2], w_in[:, u, :], two(xn2[s][:])[:, g, :],
                                                    start=True, stop=True)
                        last.then_inc(unit_done[s], 1)
                if more:
                    embed(i + 1)
                for c in range(2):
                    for s in range(2):
                        if c == 0:
                            pe.wait_ge(mix_step[s], MIX * i + GATE_AT[0] + 1)
                            pe.wait_ge(unit_act[s], 8 * i + 8)
                        else:
                            pe.wait_ge(mix_step[s], MIX * (i + 1))
                        for g in range(2):
                            last = nc.tensor.matmul(P[s][1][:, g, 0:T2], w_out[:, c, :], two(acc[s][c][:])[:, g, :],
                                                    start=(c == 0), stop=(c == 1))
                        if c == 1:
                            last.then_inc(out_done[s], 1)
                for s in range(2):
                    pe.wait_ge(h1_ready[s], i + 1)
                    ln_pe(pe, s, h1[s][:], LNA * i + 1)
                for s in range(2):
                    if more:
                        pe.wait_ge(embedded[s], 2 * i + 4)
                    ln_pe_var(pe, s, sq[s][:], LNA * i + 1)
                for r in range(3):
                    for s in range(2):
                        pe.wait_ge(ffn_step[s], FFN * i + 1 + r)
                        for g in range(2):
                            src = two((x0, pool2, pool4)[r][s][:])[:, g, :]
                            if r:
                                src = src.unsqueeze(2).to_broadcast([128, T2 >> r, 1 << r])
                            last = nc.tensor.matmul(P[s][0][:, g, 0:T2], w_mr[:, r, :], src,
                                                    start=(r == 0), stop=(r == 2))
                        if r == 2:
                            last.then_inc(mr_done[s], 1)
                for s in range(2):
                    pe.wait_ge(ffn_step[s], FFN * i + 4)
                    ln_pe(pe, s, pre[s][:], LNA * i + 2)
                for s in range(2):
                    ln_pe_var(pe, s, sq[s][:], LNA * i + 2)
                for k in range(3):
                    for s in range(2):
                        if k == 0:
                            pe.wait_ge(ffn_step[s], FFN * i + 6)
                        if k == 2:
                            pe.wait_ge(gelu_done[s], 3 * i + 1)
                        for g in range(2):
                            last = nc.tensor.matmul(P[s][k % 2][:, g, 0:T2], w_mv[:, k, :], two(x1[s][:])[:, g, :],
                                                    start=True, stop=True)
                        last.then_inc(mv_done[s], 1)
                for s in range(2):
                    pe.wait_ge(ffn_step[s], FFN * i + 9)
                    ln_pe(pe, s, pre[s][:], LNA * i + 3)
                for s in range(2):
                    ln_pe_var(pe, s, sq[s][:], LNA * i + 3)
                if more:
                    center0(i + 1)
                for s in range(2):
                    pe.wait_ge(ffn_step[s], FFN * i + 11)
                    for g in range(NG):
                        nc.tensor.transpose(P[s][0][0:G, g // 4, (g % 4) * 128:(g % 4 + 1) * 128],
                                            x2[s][:, g * G:(g + 1) * G], C("ident"))
                    for g in range(NG):
                        last = nc.tensor.matmul(logit_bank(s)[:, g * E:(g + 1) * E], x2[s][:, g * G:(g + 1) * G],
                                                w_gate[:], start=True, stop=True)
                    last.then_inc(turned[s], 1)

            embed(0)
            center0(0)
            a_steps(pe, step)
            ranks(ITERS - 1)

        ROUTE = 25

        def a_scalar(act):
            a_prep_scalar(act)
            act.wait_ge(consts_ready, 2)
            act.preload_act_table_set("natural_log_exp_and_others")

            def second_weight(i):
                for s in range(2):
                    act.wait_ge(route_step[s], ROUTE * i + 14)
                    nc.scalar.activation(wexp[s][:], wexp[s][:], ACT.Exp).then_inc(wexp_done[s], 1)

            def step(i, more):
                if not first(i):
                    second_weight(i - 1)
                for s in range(2):
                    act.wait_ge(variance[s], LNA * i + 1)
                    nc.scalar.activation(two(rb[s][:]), pv(s, 0), ACT.Ln, bias=eps_col[:, 1:2], scale=1.0 + EPS
                                         ).then_inc(logvar[s], 1)
                    nc.scalar.activation(two(ra[s][:]), pv(s, 0), ACT.Ln, bias=eps_col[:, 0:1]).then_inc(logvar[s], 1)
                    act.wait_ge(logvar[s], RSA * i + 1)
                    nc.scalar.activation(rb[s][:], rb[s][:], ACT.Exp, scale=-0.5).then_inc(rstd[s], 1)
                for s in range(2):
                    act.wait_ge(logvar[s], RSA * i + 2)
                    nc.scalar.activation(ra[s][:], ra[s][:], ACT.Exp, scale=-0.5).then_inc(rstd[s], 1)
                act.preload_act_table_set("gelu_apprx_tanh_and_others")
                for u in range(8):
                    for s in range(2):
                        act.wait_ge(unit_done[s], 8 * i + u + 1)
                        half = u not in DRIVE
                        ins = nc.scalar.activation(two(unit[s][u][:]), pv(s, u % 2), ACT.Tanh,
                                                   bias=(in_half if half else in_bias)[:, u:u + 1],
                                                   scale=0.5 if half else 1.0)
                        if u in PROJ:
                            ins = nc.scalar.activation(two(zproj[s][PROJ.index(u)][:]), pv(s, u % 2), ACT.Identity,
                                                       bias=in_bias[:, u:u + 1])
                        ins.then_inc(unit_act[s], 1)
                act.preload_act_table_set("natural_log_exp_and_others")
                for n in (1, 2):
                    for s in range(2):
                        ln_act_square(act, s, sq[s][:], LNA * i + n)
                    for s in range(2):
                        ln_act_rstd(act, s, ra[s][:], LNA * i + n, RSA * i + n + 1)
                act.preload_act_table_set("gelu_apprx_tanh_and_others")
                for k in range(3):
                    for s in range(2):
                        act.wait_ge(mv_done[s], 3 * i + k + 1)
                        nc.scalar.activation(two(view[s][k][:]), pv(s, k % 2), ACT.Gelu_apprx_tanh,
                                             bias=V("mv_b", k)).then_inc(gelu_done[s], 1)
                act.preload_act_table_set("natural_log_exp_and_others")
                for s in range(2):
                    ln_act_square(act, s, sq[s][:], LNA * i + 3)
                for s in range(2):
                    ln_act_rstd(act, s, ra[s][:], LNA * i + 3, RSA * i + 4)
                if more:
                    for s in range(2):
                        ln_act_square(act, s, sq[s][:], LNA * (i + 1))
                for s in range(2):
                    act.wait_ge(turned[s], i + 1)
                    if not first(i):
                        act.wait_ge(scattered[s], 16 * 2 * NG * i)
                    for b, (g0, g1) in enumerate(((0, 4), (4, NG))):
                        if b:
                            act.wait_ge(route_step[s], ROUTE * i + 1)
                        nc.scalar.activation(rows[s][:, g0:g1, :].rearrange("p g d -> p (g d)"),
                                             P[s][0][0:G, b, 0:(g1 - g0) * 128], ACT.Copy).then_inc(rows_ready[s], 1)

            for s in range(2):
                ln_act_square(act, s, sq[s][:], 0)
            a_steps(act, step)
            second_weight(ITERS - 1)

        def a_vector(v):
            a_prep_vector(v)

            def embedding(n):
                for s in range(2):
                    if not first(n):
                        v.wait_ge(res_done[s], n)
                    for g in range(2):
                        v.wait_ge(tok_done[s], 2 * n + g + 1)
                        v.tensor_tensor(four(h0[s][:])[:, 2 * g:2 * g + 2, 1:S],
                                        P[s][0][:, g, 0:2 * NPATCH].rearrange("p (m n) -> p m n", m=2),
                                        posb[:, 1:S].unsqueeze(1).to_broadcast([128, 2, NPATCH]),
                                        ALU.add).then_inc(embedded[s], 1)

            def conv_in(i, c):
                k = MIX * i + CONV_AT[c]
                for s in range(2):
                    v.wait_ge(unit_act[s], 8 * i + PROJ[c] + 1)
                    v.scalar_tensor_tensor(out=pj[s][c][:, :, 3:], in0=four(unit[s][PROJ[c]][:]), scalar=1.0,
                                           in1=four(zproj[s][c][:]), op0=ALU.add, op1=ALU.mult
                                           ).then_inc(mix_step[s], 1)
                for s in range(2):
                    v.wait_ge(mix_step[s], k + 1)
                    v.tensor_scalar(four(acc[s][c][:]), pj[s][c][:, :, 3:], taps[:, 4 * c + 3:4 * c + 4],
                                    conv_b[:, c:c + 1], ALU.mult, ALU.add).then_inc(mix_step[s], 1)
                for s in range(2):
                    v.wait_ge(unit_act[s], 8 * i + DELTA[c] + 1)
                    v.tensor_scalar(unit[s][DELTA[c]][:], unit[s][DELTA[c]][:], 1.0, 2e-4, ALU.add, ALU.max
                                    ).then_inc(delta_ready[s], 1)

            def conv_taps(i, c):
                k = MIX * i + CONV_AT[c]
                for n, tap in enumerate((2, 1, 0)):
                    for s in range(2):
                        v.wait_ge(mix_step[s], k + 2 + n)
                        v.scalar_tensor_tensor(out=four(acc[s][c][:]), in0=pj[s][c][:, :, tap:tap + S],
                                               scalar=taps[:, 4 * c + tap:4 * c + tap + 1],
                                               in1=four(acc[s][c][:]), op0=ALU.mult, op1=ALU.add
                                               ).then_inc(mix_step[s], 1)

            def states(i, c):
                for s in range(2):
                    v.wait_ge(drive_ready[s], 2 * i + c + 1)
                    v.tensor_tensor_scan(unit[s][DRIVE[c]][:], decays[c][:], unit[s][DELTA[c]][:], 0.0,
                                         ALU.mult, ALU.add).then_inc(mix_step[s], 1)

            def sum_states(i):
                for s in range(2):
                    v.wait_ge(mix_step[s], MIX * i + STATES_AT[1] + 1)
                    v.tensor_tensor(acc[s][1][:], acc[s][1][:], unit[s][DRIVE[1]][:], ALU.add
                                    ).then_inc(mix_step[s], 1)

            def gate(i, c):
                for s in range(2):
                    if c == 0:
                        v.wait_ge(summed[s], i + 1)
                    else:
                        v.wait_ge(mix_step[s], MIX * i + GATE_AT[1])
                    v.wait_ge(unit_act[s], 8 * i + GATE[c] + 1)
                    v.scalar_tensor_tensor(out=acc[s][c][:], in0=unit[s][GATE[c]][:], scalar=1.0,
                                           in1=acc[s][c][:], op0=ALU.add, op1=ALU.mult).then_inc(mix_step[s], 1)

            def step(i, more):
                for s in range(2):
                    v.wait_ge(rstd[s], RSA * i + 1)
                    v.tensor_tensor(two(xn2[s][:]), pv(s, 1), two(rb[s][:]), ALU.mult).then_inc(normed[s], 1)
                for s in range(2):
                    v.wait_ge(rstd[s], RSA * i + 2)
                    v.tensor_tensor(two(xn1[s][:]), pv(s, 1), two(ra[s][:]), ALU.mult).then_inc(normed[s], 1)
                conv_in(i, 0)
                if not first(i):
                    a_route_rows(v, i - 1)
                conv_taps(i, 0)
                states(i, 0)
                conv_in(i, 1)
                conv_taps(i, 1)
                gate(i, 0)
                states(i, 1)
                if more:
                    embedding(i + 1)
                sum_states(i)
                gate(i, 1)
                for s in range(2):
                    v.wait_ge(out_done[s], i + 1)
                    v.wait_ge(res_done[s], i + 1)
                    if not first(i):
                        v.wait_ge(h1_stored[s], 16 * i)
                    v.scalar_tensor_tensor(out=two(h1[s][:]), in0=pv(s, 1), scalar=V("out_b"), in1=two(res[s][:]),
                                           op0=ALU.add, op1=ALU.add).then_inc(h1_ready[s], 1)
                for s in range(2):
                    v.wait_ge(rstd[s], RSA * i + 3)
                    v.tensor_tensor(two(x0[s][:]), pv(s, 1), two(ra[s][:]), ALU.mult).then_inc(ffn_step[s], 1)
                for s in range(2):
                    v.wait_ge(ffn_step[s], FFN * i + 1)
                    p2 = x0[s][:].rearrange("p (n k) -> p n k", k=2)
                    v.tensor_tensor(pool2[s][:], p2[:, :, 0], p2[:, :, 1], ALU.add).then_inc(ffn_step[s], 1)
                for s in range(2):
                    v.wait_ge(ffn_step[s], FFN * i + 2)
                    p4 = pool2[s][:].rearrange("p (n k) -> p n k", k=2)
                    v.tensor_tensor(pool4[s][:], p4[:, :, 0], p4[:, :, 1], ALU.add).then_inc(ffn_step[s], 1)
                for s in range(2):
                    v.wait_ge(mr_done[s], i + 1)
                    v.scalar_tensor_tensor(out=two(pre[s][:]), in0=pv(s, 0), scalar=mr_bias[:, 0:1],
                                           in1=two(x0[s][:]), op0=ALU.add, op1=ALU.add).then_inc(ffn_step[s], 1)
                for s in range(2):
                    v.wait_ge(rstd[s], RSA * i + 4)
                    v.scalar_tensor_tensor(out=two(x1[s][:]), in0=pv(s, 1), scalar=V("ln1_g"), in1=two(ra[s][:]),
                                           op0=ALU.mult, op1=ALU.mult).then_inc(ffn_step[s], 1)
                for s in range(2):
                    v.wait_ge(ffn_step[s], FFN * i + 5)
                    v.tensor_scalar(x1[s][:], x1[s][:], V("ln1_b"), None, ALU.add).then_inc(ffn_step[s], 1)
                for k in range(3):
                    for s in range(2):
                        v.wait_ge(gelu_done[s], 3 * i + k + 1)
                        if k:
                            v.wait_ge(ffn_step[s], FFN * i + 6 + k)
                        v.scalar_tensor_tensor(out=pre[s][:], in0=view[s][k][:], scalar=alpha[:, k:k + 1],
                                               in1=(pre if k else x1)[s][:], op0=ALU.mult, op1=ALU.add
                                               ).then_inc(ffn_step[s], 1)
                for s in range(2):
                    v.wait_ge(rstd[s], RSA * i + 5)
                    if not first(i):
                        v.wait_ge(x2_stored[s], 16 * i)
                    v.scalar_tensor_tensor(out=two(x2[s][:]), in0=pv(s, 1), scalar=V("ln2_g"), in1=two(ra[s][:]),
                                           op0=ALU.mult, op1=ALU.mult).then_inc(ffn_step[s], 1)
                for s in range(2):
                    v.wait_ge(ffn_step[s], FFN * i + 10)
                    v.tensor_scalar(x2[s][:], x2[s][:], V("ln2_b"), None, ALU.add).then_inc(ffn_step[s], 1)
                a_route_top(v, i)

            embedding(0)
            a_steps(v, step)
            a_route_rows(v, ITERS - 1)

        def a_route_top(v, i):
            def over_e(ap):
                return ap.unsqueeze(2).to_broadcast([G, NG, E])

            rev = R("rev")[0:G, :].unsqueeze(1).to_broadcast([G, NG, E])
            done = [[0, 0]]

            def both(make):
                n = done[0][0]
                for s in range(2):
                    if n:
                        v.wait_ge(route_step[s], ROUTE * i + n)
                    make(s).then_inc(route_step[s], 1)
                done[0][0] += 1

            for s in range(2):
                v.wait_ge(turned[s], i + 1)
                v.tensor_tensor(logit[s][:], logit_bank(s).rearrange("p (g e) -> p g e", e=E),
                                RR("gate_b")[0:G, :].unsqueeze(1).to_broadcast([G, NG, E]), ALU.add
                                ).then_inc(route_step[s], 1)
            done[0][0] = 1
            for top, pick, src in ((top1, pick1, logit), (top2, pick2, lmask)):
                both(lambda s: v.tensor_reduce(top[s][:], src[s][:], AX_X, ALU.max))
                both(lambda s: v.tensor_tensor(cand[s][:], src[s][:], over_e(top[s][:]), ALU.is_equal))
                both(lambda s: v.tensor_tensor(cand[s][:], cand[s][:], rev, ALU.mult))
                both(lambda s: v.tensor_reduce(best[s][:], cand[s][:], AX_X, ALU.max))
                both(lambda s: v.tensor_tensor(pick[s][:], cand[s][:], over_e(best[s][:]), ALU.is_equal))
                if top is top1:
                    both(lambda s: v.scalar_tensor_tensor(out=lmask[s][:], in0=pick1[s][:], scalar=-3e38,
                                                          in1=logit[s][:], op0=ALU.mult, op1=ALU.add))
            both(lambda s: v.tensor_tensor(picks[s][:], pick1[s][:], pick2[s][:], ALU.add))
            both(lambda s: v.tensor_tensor(wexp[s][:], top2[s][:], top1[s][:], ALU.subtract))
            both(lambda s: v.tensor_reduce(newly[s][:], picks[s][:].rearrange("p g e -> p e g"), AX_X, ALU.add))
            assert done[0][0] == 15

        def a_route_rows(v, i):
            done = [15]

            def both(make):
                for s in range(2):
                    v.wait_ge(route_step[s], ROUTE * i + done[0])
                    make(s).then_inc(route_step[s], 1)
                done[0] += 1

            for s in range(2):
                v.wait_ge(rank_done[s], i + 1)
                v.wait_ge(route_step[s], ROUTE * i + 15)
                if s or not first(i):
                    v.wait_ge(chosen_new, 2 * i + s)
                v.tensor_tensor(chosen[:], chosen[:], newly[s][:], ALU.add).then_inc(chosen_new, 1)
                v.tensor_tensor(cand[s][:], P[s][1][0:G, 1, 0:NG * E].rearrange("p (g e) -> p g e", e=E),
                                R("first")[0:G, :].unsqueeze(1).to_broadcast([G, NG, E]), ALU.add
                                ).then_inc(route_step[s], 1)
            done[0] = 16
            for choice, pick in ((0, pick1), (1, pick2)):
                both(lambda s: v.tensor_tensor(logit[s][:], cand[s][:], pick[s][:], ALU.mult))
                both(lambda s: v.tensor_reduce(slot[s][:, choice * NG:(choice + 1) * NG], logit[s][:], AX_X,
                                               ALU.add))
            both(lambda s: v.tensor_copy(slots[:, bass.DynSlice(i * 4 * NG + s * 2 * NG, 2 * NG)], slot[s][:]))
            for s in range(2):
                if not first(i):
                    v.wait_ge(scattered[s], 16 * 2 * NG * i)
                v.tensor_copy(slot_i[s][:], slot[s][:]).then_inc(slots_ready[s], 1)
            for s in range(2):
                v.wait_ge(wexp_done[s], i + 1)
            both(lambda s: v.tensor_scalar(wsum[s][:], wexp[s][:], 1.0, None, ALU.add))

            def at(tile, s, choice):
                return tile[:, bass.DynSlice(i * 4 * NG + s * 2 * NG + choice * NG, NG)]

            both(lambda s: v.reciprocal(wsum[s][:], wsum[s][:]))
            both(lambda s: v.tensor_copy(at(weights, s, 0), wsum[s][:]))
            both(lambda s: v.tensor_tensor(at(weights, s, 1), wexp[s][:], wsum[s][:], ALU.mult))
            assert done[0] == ROUTE

        def a_pool(pool):
            def scatter(i):
                for s in range(2):
                    hold(pool, rows_ready[s], 2 * i + 2)
                    hold(pool, slots_ready[s], i + 1)
                    for choice in range(2):
                        for g in range(NG):
                            n = choice * NG + g
                            pool.indirect_dma_start(
                                out=expert_in[:, :],
                                out_offset=bass.IndirectOffsetOnAxis(ap=slot_i[s][:, n:n + 1], axis=0),
                                in_=rows[s][:, g, :], in_offset=None).then_inc(scattered[s], 16)

            def step(i, more):
                for s in range(2):
                    pool.wait_ge(embedded[s], 2 * i + 2)
                    pool.wait_ge(normed[s], 2 * i + 2)
                    pool.tensor_tensor(res[s][:], h0[s][:], xn1[s][:], ALU.add).then_inc(res_done[s], 1)
                for c in range(2):
                    for s in range(2):
                        pool.wait_ge(delta_ready[s], 2 * i + c + 1)
                        pool.wait_ge(unit_act[s], 8 * i + DRIVE[c] + 1)
                        pool.tensor_tensor(unit[s][DELTA[c]][:], unit[s][DELTA[c]][:], unit[s][DRIVE[c]][:], ALU.mult
                                           ).then_inc(drive_ready[s], 1)
                    if c == 0:
                        for s in range(2):
                            pool.wait_ge(mix_step[s], MIX * i + STATES_AT[0] + 1)
                            pool.tensor_tensor(acc[s][0][:], acc[s][0][:], unit[s][DRIVE[0]][:], ALU.add
                                               ).then_inc(summed[s], 1)
                if not first(i):
                    scatter(i - 1)

            a_steps(pool, step)
            scatter(ITERS - 1)
            for s in range(2):
                pool.wait_ge(scattered[s], 16 * 2 * NG * ITERS)

        mem_a.close()

        mem_b = ExitStack()
        WCOLS = FF + FC * D + FC + D
        w_blk = pair("w_blk", [128, WCOLS], F32, mem_b)
        rows_in, rows_out = pair("rows_in", [128, CB, D], F32, mem_b), pair("rows_out", [128, CB, D], F32, mem_b)
        x_t = pair("x_t", [128, BLK], F32, mem_b)
        hid = pair("hid", [128, FC, BLK], F32, mem_b)
        zeros = sb("zeros", [128, CB * D], F32, mem_b)
        count = sb("count", [128, E], F32, mem_b)
        nblk, ends, ones_e = (sb("nblk", [128, E], F32, mem_b), sb("ends", [128, E], F32, mem_b),
                              sb("ones_e", [128, E], F32, mem_b))
        over = sb("over", [128, E, KMAX], F32, mem_b)
        past = sb("past", [1, NB, E], F32, mem_b)
        blk_e, blk_done = sb("blk_e", [1, NB], F32, mem_b), sb("blk_done", [1, NB], F32, mem_b)
        shift = sb("shift", [128, E], F32, mem_b)
        moved = sb("moved", [G, ITERS * 4 * NG], F32, mem_b)

        count_done, table_step, table_ready = sem("count_done"), sem("table_step"), sem("table_ready")
        out_rows_step, zero_filled = sem("out_rows_step"), sem("zero_filled")
        w_landed, r_landed, block_stored = sems("w_landed"), sems("r_landed"), sems("block_stored")
        in_turned, xt_ready, hid_done, hid_ready = (sems("in_turned"), sems("xt_ready"), sems("hid_done"),
                                                    sems("hid_ready"))
        y_done, rows_out_ready = sems("y_done"), sems("rows_out_ready")
        TB = [P[s][0][:, 0, :] for s in range(2)]
        HB = [[P[s][0][:, 1, :], P[s][1][:, 0, :]] for s in range(2)]
        YB = [P[s][1][:, 1, :] for s in range(2)]

        def b_sync(sp):
            sp.wait_ge(table_ready, 1)
            for e in range(E + 1):
                if e < E:
                    n = sp.value_load(tails[0:1, e:e + 1], min_val=0, max_val=tokens)
                    at = bass.DynSlice(n + e * REGION, BLK)
                else:
                    at = slice(E * REGION, E * REGION + BLK)
                sp.dma_start(expert_in[at, :].rearrange("(p c) d -> p (c d)", c=CB), zeros[:]
                             ).then_inc(zero_filled, 16)
            sp.wait_ge(zero_filled, 16 * (E + 1))
            for s in range(2):
                sp.wait_ge(scattered[s], 16 * 2 * NG * ITERS)

            def load(n, s, k, first):
                if not first:
                    hold(sp, in_turned[s], k)
                r = sp.value_load(table[0:1, bass.DynSlice(n, 1)], min_val=0, max_val=E * REGION)
                sp.dma_start(rows_in[s][:].rearrange("p c d -> p (c d)"),
                             expert_in[bass.DynSlice(r, BLK), :].rearrange("(p c) d -> p (c d)", c=CB)
                             ).then_inc(r_landed[s], 16)
                if not first:
                    hold(sp, rows_out_ready[s], k)
                e = sp.value_load(table[0:1, bass.DynSlice(NB + n, 1)], min_val=0, max_val=E - 1)
                sp.dma_start(w_blk[s][:], a["w_exp"][bass.DynSlice(e * 128, 128), :]).then_inc(w_landed[s], 16)

            def store(n, s, k):
                hold(sp, rows_out_ready[s], k + 1)
                sp.dma_start(expert_out[bass.DynSlice(n * BLK, BLK), :].rearrange("(p c) d -> p (c d)", c=CB),
                             rows_out[s][:].rearrange("p c d -> p (c d)")).then_inc(block_stored[s], 16)

            for s in range(2):
                load(s, s, 0, True)
            with sp.Fori(1, NB // 2) as i:
                for s in range(2):
                    load(2 * i + s, s, i, False)
                    store(2 * i + s - 2, s, i - 1)
            for s in range(2):
                store(NB - 2 + s, s, NB // 2 - 1)
            for s in range(2):
                sp.wait_ge(block_stored[s], 16 * (NB // 2))

        def b_tensor(pe):
            pe.wait_ge(chosen_new, 2 * ITERS)
            for s in range(2):
                pe.wait_ge(rows_ready[s], 2 * ITERS)
                pe.wait_ge(slots_ready[s], ITERS)
            nc.tensor.matmul(YB[0][:, 0:E], C("ones")[0:G, :], chosen[:], start=True, stop=True).then_inc(count_done, 1)

            def turn_in(s, k):
                pe.wait_ge(r_landed[s], 16 * k + 16)
                for c in range(CB):
                    last = nc.tensor.transpose(TB[s][:, c * 128:(c + 1) * 128], rows_in[s][:, c, :], C("ident"))
                last.then_inc(in_turned[s], 1)

            def hidden(s, k, c):
                if c == 0:
                    pe.wait_ge(w_landed[s], 16 * k + 16)
                    pe.wait_ge(xt_ready[s], k + 1)
                if c >= 2:
                    pe.wait_ge(hid_ready[s], FC * k + c - 1)
                nc.tensor.matmul(HB[s][c % 2], w_blk[s][:, c * 128:(c + 1) * 128], x_t[s][:], start=True, stop=True
                                 ).then_inc(hid_done[s], 1)

            def outputs(s, k):
                for t in range(CB):
                    for c in range(FC):
                        if t == 0:
                            pe.wait_ge(hid_ready[s], FC * k + c + 1)
                            if c == 0 and not first(k):
                                pe.wait_ge(rows_out_ready[s], k)
                        last = nc.tensor.matmul(YB[s][:, t * 128:(t + 1) * 128], hid[s][:, c, t * 128:(t + 1) * 128],
                                                w_blk[s][:, FF + c * D:FF + (c + 1) * D],
                                                start=(c == 0), stop=(c == FC - 1))
                last.then_inc(y_done[s], 1)

            def block(s, k, final=False):
                for c in range(FC):
                    hidden(s, k, c)
                if not final:
                    turn_in(1 - s, k + s)
                outputs(s, k)

            pe.wait_ge(table_ready, 1)
            turn_in(0, 0)
            block(0, 0)
            block(1, 0)
            with pe.Fori(1, NB // 2 - 1) as i:
                block(0, i)
                block(1, i)
            block(0, NB // 2 - 1)
            block(1, NB // 2 - 1, final=True)

        def b_scalar(act):
            act.preload_act_table(ACT.Gelu_apprx_tanh)

            def block(s, k):
                for c in range(FC):
                    act.wait_ge(hid_done[s], FC * k + c + 1)
                    if c == 0 and not first(k):
                        act.wait_ge(y_done[s], k)
                    nc.scalar.activation(hid[s][:, c, :], HB[s][c % 2], ACT.Gelu_apprx_tanh,
                                         bias=w_blk[s][:, FF + FC * D + c:FF + FC * D + c + 1]
                                         ).then_inc(hid_ready[s], 1)

            for s in range(2):
                block(s, 0)
            with act.Fori(1, NB // 2) as i:
                for s in range(2):
                    block(s, i)

        def b_vector(v):
            n = [0]

            def chain(ins):
                n[0] += 1
                ins.then_inc(table_step, 1)
                v.wait_ge(table_step, n[0])

            chain(v.memset(zeros[:], 0.0))
            chain(v.memset(ones_e[:], 1.0))
            v.wait_ge(count_done, 1)
            chain(v.tensor_copy(count[:], YB[0][:, 0:E]))
            chain(v.tensor_tensor(over[:], count[:].unsqueeze(2).to_broadcast([128, E, KMAX]),
                                  R("kblk").unsqueeze(1).to_broadcast([128, E, KMAX]), ALU.is_gt))
            chain(v.tensor_reduce(nblk[:], over[:], AX_X, ALU.add))
            chain(v.tensor_tensor_scan(ends[:], ones_e[:], nblk[:], 0.0, ALU.mult, ALU.add))
            blk = R("blk")[0:1, :]
            chain(v.tensor_tensor(past[:], blk.unsqueeze(2).to_broadcast([1, NB, E]),
                                  ends[0:1, :].unsqueeze(1).to_broadcast([1, NB, E]), ALU.is_ge))
            chain(v.tensor_reduce(blk_e[:], past[:], AX_X, ALU.add))
            chain(v.tensor_tensor(past[:], past[:], nblk[0:1, :].unsqueeze(1).to_broadcast([1, NB, E]), ALU.mult))
            chain(v.tensor_reduce(blk_done[:], past[:], AX_X, ALU.add))
            chain(v.tensor_tensor(blk_done[:], blk, blk_done[:], ALU.subtract))
            chain(v.tensor_scalar(blk_done[:], blk_done[:], float(BLK), None, ALU.mult))
            chain(v.scalar_tensor_tensor(out=blk_done[:], in0=blk_e[:], scalar=float(REGION), in1=blk_done[:],
                                         op0=ALU.mult, op1=ALU.add))
            chain(v.tensor_scalar(table[:, 0:NB], blk_done[:], float(E * REGION), None, ALU.min))
            chain(v.tensor_scalar(table[:, NB:2 * NB], blk_e[:], float(E - 1), None, ALU.min))
            v.tensor_copy(tails[:], count[0:1, :]).then_inc(table_ready, 1)
            chain(v.tensor_tensor(shift[:], ends[:], nblk[:], ALU.subtract))
            chain(v.tensor_scalar(shift[:], shift[:], float(BLK), None, ALU.mult))
            chain(v.tensor_tensor(shift[:], shift[:], R("first"), ALU.subtract))
            chain(v.tensor_tensor(over[:, 1:E, 0], shift[:, 1:E], shift[:, 0:E - 1], ALU.subtract))
            chain(v.tensor_scalar(out_rows[:], slots[:], shift[0:G, 0:1], None, ALU.add))
            for e in range(1, E):
                chain(v.tensor_scalar(moved[:], slots[:], float(e * REGION), over[0:G, e:e + 1, 0], ALU.is_ge, ALU.mult))
                chain(v.tensor_tensor(out_rows[:], out_rows[:], moved[:], ALU.add))
            v.sem_inc(out_rows_step, 1)

            def take_in(s, k):
                v.wait_ge(in_turned[s], k + 1)
                v.tensor_copy(x_t[s][:], TB[s]).then_inc(xt_ready[s], 1)

            def block(s, k, final=False):
                if not final:
                    take_in(1 - s, k + s)
                v.wait_ge(y_done[s], k + 1)
                if not first(k):
                    v.wait_ge(block_stored[s], 16 * k)
                v.tensor_tensor(rows_out[s][:], YB[s].rearrange("p (c d) -> p c d", c=CB),
                                w_blk[s][:, WCOLS - D:WCOLS].unsqueeze(1).to_broadcast([128, CB, D]), ALU.add
                                ).then_inc(rows_out_ready[s], 1)

            take_in(0, 0)
            block(0, 0)
            block(1, 0)
            with v.Fori(1, NB // 2 - 1) as i:
                block(0, i)
                block(1, i)
            block(0, NB // 2 - 1)
            block(1, NB // 2 - 1, final=True)

        mem_b.close()

        mem_c = ExitStack()

        def pair_c(name, shape, dt=F32):
            return pair(name, shape, dt, mem_c)

        w_qkv, w_att, w_g = (sb("w_qkv", [128, 3 * D], F32, mem_c), sb("w_att", [128, D], F32, mem_c),
                             sb("w_g", [128, E2], F32, mem_c))
        q_neg, att_bias = sb("q_neg", [128, 1], F32, mem_c), sb("att_bias", [128, 1], F32, mem_c)
        band, ident_h = sb("band", [128, cw["band"][1]], BF16, mem_c), sb("ident_h", [128, 128], BF16, mem_c)
        h1c, x2c = pair_c("h1c", [128, T]), pair_c("x2c", [128, T])
        ycho = pair_c("ycho", [G, 2 * NG, D])
        place, ysum = pair_c("place", [G, 2 * NG], I32), pair_c("ysum", [G, NG, D])
        sqc, rc, prec = pair_c("sqc", [128, T]), pair_c("rc", [128, T]), pair_c("prec", [128, T])
        x3, h2, h3, xm = pair_c("x3", [128, T]), pair_c("h2", [128, T]), pair_c("h3", [128, T]), pair_c("xm", [128, T])
        xpad, kpad = pair_c("xpad", [128, IMGS, KPAD]), pair_c("kpad", [128, IMGS, KPAD])
        qs = pair_c("qs", [128, T])
        val = pair_c("val", [KW, IMGS * NWIN, D])
        qdiag = [[sb(f"qdiag{s}{k}", [128, UB, HEADS, QB], F32, mem_c) for k in range(2)] for s in range(2)]
        ex = [[sb(f"ex{s}{k}", [128, UB, KW], F32, mem_c) for k in range(2)] for s in range(2)]
        smin = [[sb(f"smin{s}{k}", [128, UB], F32, mem_c) for k in range(2)] for s in range(2)]
        ssum = [[sb(f"ssum{s}{k}", [128, UB], F32, mem_c) for k in range(2)] for s in range(2)]
        ex_t = pair_c("ex_t", [KW, UB, 128])
        own = pair_c("own", [128, UB, HEADS, QB])
        att = pair_c("att", [128, T])
        means = sb("means", [128, NI], F32, mem_c)
        l16, c16, p16 = (sb("l16", [NI, E2], F32, mem_c), sb("c16", [NI, E2], F32, mem_c),
                         sb("p16", [NI, E2], F32, mem_c))
        m16, b16, g16, gdiag = (sb("m16", [NI, 1], F32, mem_c), sb("b16", [NI, 1], F32, mem_c),
                                sb("g16", [NI, 1], F32, mem_c), sb("gdiag", [NI, NI], F32, mem_c))
        pick_i = sb("pick_i", [NI, 1], I32, mem_c)
        gate_bc = sb("gate_bc", [128, NI], F32, mem_c)
        wsel = pair_c("wsel", [128, IMGS, D + 1])
        outs = pair_c("outs", [128, T])

        loaded_c, c_ready = sem("loaded_c"), sem("c_ready")
        h_landed, choice_step, gathered = sems("h_landed"), sems("choice_step"), sems("gathered")
        ysum_step = sems("ysum_step")
        moe_done, trunk_step = sems("moe_done"), sems("trunk_step")
        qk_done, qk_ready = sems("qk_done"), sems("qk_ready")
        val_done, val_ready, qdiag_ready = sems("val_done"), sems("val_ready"), sems("qdiag_ready")
        scores_done, min_ready, ex_ready = sems("scores_done"), sems("min_ready"), sems("ex_ready")
        soft_step = sems("soft_step")
        ext_done, ext_ready, pv_done, own_ready = sems("ext_done"), sems("ext_ready"), sems("pv_done"), sems("own_ready")
        att_ready, proj_done = sems("att_ready"), sems("proj_done")
        bias_done = sem("bias_done")
        tail_step, router_pe, pick_step, pick_exp = (sems("tail_step"), sem("router_pe"), sem("pick_step"),
                                                     sem("pick_exp"))
        gate_ready, wsel_landed = sem("gate_ready"), sems("wsel_landed")
        last_done, out_step, out_stored = sems("last_done"), sems("out_step"), sems("out_stored")
        LNC = 3
        LN0 = LNA * ITERS
        RS0 = RSA * ITERS
        TRUNK = 4
        TAIL = 3
        SOFT = 2
        AHEAD = 3
        PICK = 9
        ITEMS = [(u, s) for u in range(NU) for s in range(2)]

        def item(j):
            return ITEMS[j] if 0 <= j < len(ITEMS) else None

        def val_bank(r, s):
            return (P[s][1][0:KW, 0, :], P[s][0][0:KW, 1, :])[r % 2]

        def score_bank(u, s):
            return (P[s][0][:, 0, 0:UB * KW], P[s][1][:, 1, 0:UB * KW])[u % 2]

        def c_steps(eng, trunk, attention, tail):
            trunk(0, True)
            attention(0, last=False, more=True)
            tail(0)
            trunk(1, True)
            with eng.Fori(1, ITERS - 2) as i:
                attention(i, last=True, more=True)
                tail(i)
                trunk(i + 1, True)
            attention(ITERS - 2, last=True, more=True)
            tail(ITERS - 2)
            trunk(ITERS - 1, False)
            attention(ITERS - 1, last=True, more=False)
            tail(ITERS - 1, more=False)

        def c_sync(sp):
            for dst, src in ((w_qkv, "w_qkv"), (w_att, "w_att"), (w_g, "w_g")):
                sp.dma_start(dst[:], a[src]).then_inc(loaded_c, 16)

            def load(n):
                for s in range(2):
                    sp.dma_start(h1c[s][:], h1_dram[:, a_range(n, s)]).then_inc(h_landed[s], 16)
                    sp.dma_start(x2c[s][:], x2_dram[:, a_range(n, s)]).then_inc(h_landed[s], 16)

            def store(q):
                for s in range(2):
                    hold(sp, out_step[s], (IMGS + 1) * (q + 1))
                    sp.dma_start(a["out"][:, a_range(q, s)], outs[s][:]).then_inc(out_stored[s], 16)

            def attention(i, last, more):
                if more:
                    for s in range(2):
                        hold(sp, trunk_step[s], TRUNK * (i + 1))
                    load(i + 1)
                if last:
                    store(i - 1)
                    for s in range(2):
                        hold(sp, out_stored[s], 16 * i)

            def tail(i, more=True):
                hold(sp, pick_step, PICK * i + 6)
                for s in range(2):
                    for m in range(IMGS):
                        n = s * IMGS + m
                        e = sp.value_load(pick_i[n:n + 1, 0:1], min_val=0, max_val=E2 - 1)
                        sp.dma_start(wsel[s][:, m, :], a["w_last"][bass.DynSlice(e * 128, 128), :]
                                     ).then_inc(wsel_landed[s], 16)

            load(0)
            c_steps(sp, lambda n, more: None, attention, tail)
            store(ITERS - 1)
            for s in range(2):
                sp.wait_ge(out_stored[s], 16 * ITERS)

        def c_pool(pool):
            for s in range(2):
                pool.wait_ge(block_stored[s], 16 * (NB // 2))

            def gather(n, s, k):
                pool.indirect_dma_start(
                    out=ycho[s][:, k, :], out_offset=None, in_=expert_out[:, :],
                    in_offset=bass.IndirectOffsetOnAxis(ap=place[s][:, k:k + 1], axis=0)).then_inc(gathered[s], 16)

            def weighted_sum(n, s):
                pool.wait_ge(gathered[s], 16 * 2 * NG * (n + 1))
                w = weights[:, bass.DynSlice(n * 4 * NG + s * 2 * NG, 2 * NG)]
                pool.tensor_tensor(ycho[s][:], ycho[s][:], w.unsqueeze(2).to_broadcast([G, 2 * NG, D]), ALU.mult
                                   ).then_inc(ysum_step[s], 1)
                pool.wait_ge(ysum_step[s], 2 * n + 1)
                pool.tensor_tensor(ysum[s][:], ycho[s][:, 0:NG, :], ycho[s][:, NG:, :], ALU.add
                                   ).then_inc(ysum_step[s], 1)

            def attention(i, last, more):
                def fetch(s, k):
                    if k == 0:
                        hold(pool, choice_step[s], i + 2)
                        hold(pool, moe_done[s], i + 1)
                    gather(i + 1, s, k)

                todo = list(range(2 * NG)) if more else []
                for k in todo:
                    fetch(0, k)
                if more:
                    weighted_sum(i + 1, 0)
                for u, s in ITEMS:
                    if u == 0:
                        pool.wait_ge(qk_ready[s], 2 * i + 1)
                    if u >= 2:
                        pool.wait_ge(scores_done[s], NU * i + u - 1)
                    pool.tensor_tensor(
                        qdiag[s][u % 2][:],
                        qs[s][:, u * UB * QB:(u + 1) * UB * QB].rearrange("p (b q) -> p b q", b=UB).unsqueeze(2)
                        .to_broadcast([128, UB, HEADS, QB]),
                        C("head_rows").unsqueeze(1).unsqueeze(3).to_broadcast([128, UB, HEADS, QB]),
                        ALU.mult).then_inc(qdiag_ready[s], 1)
                    if u >= 2 and todo:
                        fetch(1, todo.pop(0))
                assert not todo
                if more:
                    weighted_sum(i + 1, 1)

            for s in range(2):
                pool.wait_ge(choice_step[s], 1)
                for k in range(2 * NG):
                    gather(0, s, k)
            for s in range(2):
                weighted_sum(0, s)
            c_steps(pool, lambda n, more: None, attention, lambda i, more=True: None)

        def c_tensor(pe):
            pe.wait_ge(c_ready, 1)
            for s in range(2):
                pe.wait_ge(rows_out_ready[s], NB // 2)
            nc.tensor.matmul(P[1][1][:, 1, 0:1], w_att[:], V("v_b"), start=True, stop=True).then_inc(bias_done, 1)

            def scores(i, u, s):
                pe.wait_ge(qdiag_ready[s], NU * i + u + 1)
                if u == 0:
                    pe.wait_ge(qk_ready[s], 2 * i + 2)
                b0 = (u * UB) % NQB
                bank = score_bank(u, s)
                nc.tensor.matmul(bank, ident_h[:], band[:, b0 * KW:(b0 + UB) * KW], start=True, stop=False)
                for b in range(UB):
                    n = u * UB + b
                    m, qb = n // NQB, n % NQB
                    done = nc.tensor.matmul(bank[:, b * KW:(b + 1) * KW],
                                            qdiag[s][u % 2][:, b, :, :].rearrange("p h q -> p (h q)"),
                                            kpad[s][:, m, WIN * (qb // 2):WIN * (qb // 2) + KW],
                                            start=False, stop=(b == UB - 1))
                done.then_inc(scores_done[s], 1)

            def moe(n, s, bank):
                if bank == 0:
                    pe.wait_ge(ysum_step[s], 2 * n + 2)
                for g in range(bank * NG // 2, (bank + 1) * NG // 2):
                    last = nc.tensor.transpose(P[s][0][:, bank, (g % 3) * G:(g % 3 + 1) * G], ysum[s][:, g, :],
                                               C("ident")[0:G, 0:G])
                if bank == 1:
                    last.then_inc(moe_done[s], 1)

            def last_layer(q):
                pe.wait_ge(pick_step, PICK * (q + 1))
                nc.tensor.matmul(P[1][1][:, 0, 0:NI], C("ones")[0:NI, :], gdiag[:], start=True, stop=True
                                 ).then_inc(router_pe, 1)
                for s in range(2):
                    pe.wait_ge(wsel_landed[s], 16 * IMGS * (q + 1))
                    if s == 1:
                        pe.wait_ge(gate_ready, q + 1)
                    for m in range(IMGS):
                        last = nc.tensor.matmul(P[s][1][:, m // 2, (m % 2) * S:(m % 2 + 1) * S], wsel[s][:, m, 0:D],
                                                four(xm[s][:])[:, m, :], start=True, stop=True)
                    last.then_inc(last_done[s], 1)

            def trunk(n, more):
                if first(n):
                    for s in range(2):
                        moe(0, s, 0)
                        moe(0, s, 1)
                for s in range(2):
                    if not first(n):
                        pe.wait_ge(tail_step[s], TAIL * (n - 1) + 2)
                    pe.wait_ge(trunk_step[s], TRUNK * n + 1)
                    ln_pe(pe, s, prec[s][:], LN0 + LNC * n)
                if not first(n):
                    for s in range(2):
                        pe.wait_ge(tail_step[s], TAIL * n)
                    nc.tensor.matmul(P[0][0][0:NI, 0, 0:E2], means[:], w_g[:], start=True, stop=True
                                     ).then_inc(router_pe, 1)
                    pe.wait_ge(pick_step, PICK * (n - 1) + 1)
                for s in range(2):
                    ln_pe_var(pe, s, sqc[s][:], LN0 + LNC * n)
                for s in range(2):
                    pe.wait_ge(trunk_step[s], TRUNK * n + 3)
                    ln_pe(pe, s, h2[s][:], LN0 + LNC * n + 1)
                for s in range(2):
                    ln_pe_var(pe, s, sqc[s][:], LN0 + LNC * n + 1)
                for k in range(2):
                    for s in range(2):
                        if k == 0:
                            pe.wait_ge(trunk_step[s], TRUNK * n + 4)
                        else:
                            pe.wait_ge(qk_ready[s], 2 * n + 1)
                        for g in range(2):
                            last = nc.tensor.matmul(
                                P[s][0][:, g, 0:T2].rearrange("p (m n) -> p m n", m=2), w_qkv[:, k * D:(k + 1) * D],
                                xpad[s][:, 2 * g:2 * g + 2, WIN:WIN + S], start=True, stop=True)
                        last.then_inc(qk_done[s], 1)
                    if k == 0 and not first(n):
                        last_layer(n - 1)
                for r in range(NWIN):
                    if r == NWIN - 2:
                        for s in range(2):
                            scores(n, 0, s)
                    for s in range(2):
                        if r == 0:
                            if not first(n):
                                pe.wait_ge(out_step[s], (IMGS + 1) * (n - 1) + IMGS)
                        elif r == 1:
                            pe.wait_ge(qk_ready[s], 2 * n + 2)
                        else:
                            pe.wait_ge(val_ready[s], NWIN * n + r - 1)
                        for w in range(UB):
                            b = r * UB + w
                            m, j = b // NWIN, b % NWIN
                            last = nc.tensor.matmul(val_bank(r, s)[:, w * D:(w + 1) * D],
                                                    xpad[s][:, m, j * WIN:j * WIN + KW], w_qkv[:, 2 * D:3 * D],
                                                    start=True, stop=True)
                        last.then_inc(val_done[s], 1)

            def attention(i, last, more):
                def turn(u, s):
                    if u == 0:
                        pe.wait_ge(val_ready[s], NWIN * (i + 1) - 1)
                    pe.wait_ge(soft_step[s], SOFT * (NU * i + u + 1))
                    for b in range(UB):
                        done = nc.tensor.transpose(P[s][0][0:KW, 1, b * 128:(b + 1) * 128], ex[s][u % 2][:, b, :],
                                                   C("ident"))
                    done.then_inc(ext_done[s], 1)

                def values(u, s):
                    pe.wait_ge(ext_ready[s], NU * i + u + 1)
                    if u == 0:
                        pe.wait_ge(val_ready[s], NWIN * (i + 1))
                    else:
                        pe.wait_ge(own_ready[s], NU * i + u)
                    b = 0
                    while b < UB:
                        n = u * UB + b
                        m, j = n // NQB, n % NQB // 2
                        c = 2 if b + 1 < UB and n % NQB % 2 == 0 and n % NQB + 1 < NQB else 1
                        done = nc.tensor.matmul(P[s][1][:, 0, b * 128:(b + c) * 128], val[s][:, m * NWIN + j, :],
                                                ex_t[s][:, b:b + c, :].rearrange("p b r -> p (b r)"),
                                                start=True, stop=True)
                        b += c
                    done.then_inc(pv_done[s], 1)

                for j in range(2, AHEAD):
                    scores(i, *item(j))
                for j in range(len(ITEMS) + 1):
                    if item(j):
                        turn(*item(j))
                    if item(j + AHEAD):
                        scores(i, *item(j + AHEAD))
                    if j == len(ITEMS) and more:
                        moe(i + 1, 0, 0)
                    if item(j - 1):
                        values(*item(j - 1))
                if more:
                    moe(i + 1, 0, 1)
                for s in range(2):
                    pe.wait_ge(att_ready[s], NU * (i + 1))
                    for g in range(2):
                        done = nc.tensor.matmul(P[s][1][:, g, 0:T2], w_att[:], two(att[s][:])[:, g, :],
                                                start=True, stop=True)
                    done.then_inc(proj_done[s], 1)
                    if more:
                        moe(i + 1, 1, s)
                for s in range(2):
                    pe.wait_ge(tail_step[s], TAIL * i + 1)
                    ln_pe(pe, s, h3[s][:], LN0 + LNC * i + 2)
                for s in range(2):
                    if more:
                        pe.wait_ge(trunk_step[s], TRUNK * (i + 1) + 1)
                    ln_pe_var(pe, s, sqc[s][:], LN0 + LNC * i + 2)

            c_steps(pe, trunk, attention, lambda i, more=True: None)
            for s in range(2):
                pe.wait_ge(tail_step[s], TAIL * ITERS)
            nc.tensor.matmul(P[0][0][0:NI, 0, 0:E2], means[:], w_g[:], start=True, stop=True).then_inc(router_pe, 1)
            last_layer(ITERS - 1)

        def c_scalar(act):
            act.preload_act_table_set("natural_log_exp_and_others")
            act.wait_ge(c_ready, 1)

            def norm(n, k):
                for s in range(2):
                    ln_act_square(act, s, sqc[s][:], LN0 + LNC * n + k)
                for s in range(2):
                    ln_act_rstd(act, s, rc[s][:], LN0 + LNC * n + k, RS0 + LNC * n + k)

            def exps(i, u, s):
                act.wait_ge(min_ready[s], NU * i + u + 1)
                for b in range(UB):
                    done = nc.scalar.activation(ex[s][u % 2][:, b, :], score_bank(u, s)[:, b * KW:(b + 1) * KW],
                                                ACT.Exp, bias=smin[s][u % 2][:, b:b + 1], scale=-1.0,
                                                accum_out=ssum[s][u % 2][:, b:b + 1])
                done.then_inc(ex_ready[s], 1)

            def trunk_rest(n):
                norm(n, 1)
                for s in range(2):
                    act.wait_ge(qk_done[s], 2 * n + 1)
                    nc.scalar.activation(two(qs[s][:]), pv(s, 0), ACT.Identity, bias=q_neg[:, 0:1],
                                         scale=-float(HD) ** -0.5).then_inc(qk_ready[s], 1)
                for s in range(2):
                    act.wait_ge(qk_done[s], 2 * n + 2)
                    nc.scalar.activation(two_two(kpad[s][:])[:, :, :, WIN:WIN + S], pv4(s, 0), ACT.Identity,
                                         bias=V("k_b")).then_inc(qk_ready[s], 1)
                for r in range(NWIN):
                    if r == NWIN - 1:
                        for s in range(2):
                            exps(n, 0, s)
                    for s in range(2):
                        act.wait_ge(val_done[s], NWIN * n + r + 1)
                        nc.scalar.activation(val[s][:, r * UB:(r + 1) * UB, :].rearrange("p w d -> p (w d)"),
                                             val_bank(r, s), ACT.Copy).then_inc(val_ready[s], 1)

            def attention(i, last, more):
                for j in range(2 - AHEAD, len(ITEMS)):
                    if item(j):
                        u, s = item(j)
                        act.wait_ge(ext_done[s], NU * i + u + 1)
                        nc.scalar.activation(ex_t[s][:].rearrange("p b r -> p (b r)"), P[s][0][0:KW, 1, :], ACT.Copy
                                             ).then_inc(ext_ready[s], 1)
                    if item(j + AHEAD):
                        exps(i, *item(j + AHEAD))

            def tail(i, more=True):
                norm(i, 2)

            def pick(i):
                act.wait_ge(pick_step, PICK * i + 7)
                nc.scalar.activation(p16[:], l16[:], ACT.Exp, accum_out=g16[:]).then_inc(pick_exp, 1)

            def trunk_and_pick(n, more):
                for s in range(2):
                    ln_act_square(act, s, sqc[s][:], LN0 + LNC * n)
                if not first(n):
                    pick(n - 1)
                for s in range(2):
                    ln_act_rstd(act, s, rc[s][:], LN0 + LNC * n, RS0 + LNC * n)
                trunk_rest(n)

            c_steps(act, trunk_and_pick, attention, tail)
            pick(ITERS - 1)

        def c_vector(v):
            v.wait_ge(loaded_c, 16 * 3)
            for s in range(2):
                v.memset(xpad[s][:], 0.0)
                v.memset(kpad[s][:], 0.0)
            v.tensor_copy(band[:], C("band"))
            v.tensor_copy(ident_h[:], C("ident"))
            v.tensor_scalar(q_neg[:], V("q_b"), -float(HD) ** -0.5, None, ALU.mult).then_inc(c_ready, 1)
            v.wait_ge(c_ready, 1)
            v.wait_ge(bias_done, 1)
            v.tensor_tensor(att_bias[:], P[1][1][:, 1, 0:1], V("attn_b"), ALU.add).then_inc(c_ready, 1)
            v.wait_ge(c_ready, 2)
            v.wait_ge(out_rows_step, 1)

            def row_numbers(n, streams):
                for s in streams:
                    v.tensor_copy(place[s][:], out_rows[:, bass.DynSlice(n * 4 * NG + s * 2 * NG, 2 * NG)]
                                  ).then_inc(choice_step[s], 1)

            def pre(n):
                for s in range(2):
                    v.wait_ge(moe_done[s], n + 1)
                    v.wait_ge(h_landed[s], 32 * n + 32)
                    v.tensor_tensor(two(prec[s][:]), pv(s, 0), two(x2c[s][:]), ALU.add).then_inc(trunk_step[s], 1)

            def trunk(n):
                for s in range(2):
                    v.wait_ge(rstd[s], RS0 + LNC * n + 1)
                    v.scalar_tensor_tensor(out=two(x3[s][:]), in0=pv(s, 1), scalar=V("ln3_g"), in1=two(rc[s][:]),
                                           op0=ALU.mult, op1=ALU.mult).then_inc(trunk_step[s], 1)
                for s in range(2):
                    v.wait_ge(trunk_step[s], TRUNK * n + 2)
                    v.scalar_tensor_tensor(out=h2[s][:], in0=x3[s][:], scalar=V("ln3_b"), in1=h1c[s][:],
                                           op0=ALU.add, op1=ALU.add).then_inc(trunk_step[s], 1)
                for s in range(2):
                    v.wait_ge(rstd[s], RS0 + LNC * n + 2)
                    v.tensor_tensor(two_two(xpad[s][:])[:, :, :, WIN:WIN + S], pv4(s, 1),
                                    two(rc[s][:]).rearrange("p g (m n) -> p g m n", m=2), ALU.mult
                                    ).then_inc(trunk_step[s], 1)

            def gates(q):
                v.wait_ge(router_pe, 2 * q + 2)
                v.tensor_copy(gate_bc[:], P[1][1][:, 0, 0:NI]).then_inc(gate_ready, 1)
                v.wait_ge(gate_ready, q + 1)

            def last_layer(q, s):
                v.wait_ge(last_done[s], q + 1)
                for m in range(IMGS):
                    v.tensor_scalar(four(outs[s][:])[:, m, :], P[s][1][:, m // 2, (m % 2) * S:(m % 2 + 1) * S],
                                    wsel[s][:, m, D:D + 1], gate_bc[:, s * IMGS + m:s * IMGS + m + 1],
                                    ALU.add, ALU.mult).then_inc(out_step[s], 1)

            def residual(q, s):
                v.wait_ge(out_step[s], (IMGS + 1) * q + IMGS)
                v.tensor_tensor(outs[s][:], outs[s][:], h3[s][:], ALU.add).then_inc(out_step[s], 1)

            def attention(i, last, more):
                def minimum(u, s):
                    v.wait_ge(scores_done[s], NU * i + u + 1)
                    v.tensor_reduce(smin[s][u % 2][:], score_bank(u, s).rearrange("p (b k) -> p b k", b=UB), AX_X,
                                    ALU.min).then_inc(min_ready[s], 1)

                def invert(u, s):
                    sums = ssum[s][u % 2]
                    v.wait_ge(ex_ready[s], NU * i + u + 1)
                    v.reciprocal(sums[:], sums[:]).then_inc(soft_step[s], 1)

                def norm(u, s):
                    sums, w = ssum[s][u % 2], ex[s][u % 2]
                    v.wait_ge(soft_step[s], SOFT * (NU * i + u) + 1)
                    v.tensor_tensor(w[:], w[:], sums[:].unsqueeze(2).to_broadcast([128, UB, KW]), ALU.mult
                                    ).then_inc(soft_step[s], 1)

                def own_head(u, s):
                    v.wait_ge(pv_done[s], NU * i + u + 1)
                    v.tensor_tensor(own[s][:], P[s][1][:, 0, :].rearrange("p (b h q) -> p b h q", b=UB, h=HEADS),
                                    C("head_rows").unsqueeze(1).unsqueeze(3).to_broadcast([128, UB, HEADS, QB]),
                                    ALU.mult).then_inc(own_ready[s], 1)

                def gather_heads(u, s):
                    v.wait_ge(own_ready[s], NU * i + u + 1)
                    v.tensor_reduce(att[s][:, u * UB * QB:(u + 1) * UB * QB].rearrange("p (b q) -> p b q", b=UB),
                                    own[s][:].rearrange("p b h q -> p b q h"), AX_X, ALU.add
                                    ).then_inc(att_ready[s], 1)

                for s in range(2):
                    minimum(0, s)
                for s in range(2):
                    invert(0, s)
                    norm(0, s)
                for j in range(2, AHEAD):
                    minimum(*item(j))
                for j in range(len(ITEMS) + 1):
                    if item(j + AHEAD):
                        minimum(*item(j + AHEAD))
                    if j + AHEAD - 1 >= 2 and item(j + AHEAD - 1):
                        invert(*item(j + AHEAD - 1))
                    if item(j - 1):
                        own_head(*item(j - 1))
                    if j + AHEAD - 1 >= 2 and item(j + AHEAD - 1):
                        norm(*item(j + AHEAD - 1))
                    if item(j - 1):
                        gather_heads(*item(j - 1))
                    if j == 0 and more:
                        row_numbers(i + 1, (1,))

            def tail(i, more=True):
                for s in range(2):
                    v.wait_ge(proj_done[s], i + 1)
                    v.scalar_tensor_tensor(out=two(h3[s][:]), in0=pv(s, 1), scalar=att_bias[:, 0:1], in1=two(h2[s][:]),
                                           op0=ALU.add, op1=ALU.add).then_inc(tail_step[s], 1)
                if more:
                    pre(i + 1)
                for s in range(2):
                    v.wait_ge(rstd[s], RS0 + LNC * i + 3)
                    v.tensor_tensor(two(xm[s][:]), pv(s, 1), two(rc[s][:]), ALU.mult).then_inc(tail_step[s], 1)

            def router(i):
                for s in range(2):
                    v.wait_ge(tail_step[s], TAIL * i + 2)
                    v.tensor_reduce(means[:, s * IMGS:(s + 1) * IMGS], four(xm[s][:]), AX_X, ALU.add
                                    ).then_inc(tail_step[s], 1)
                c_pick(v, i)

            def trunk_and_router(n, more):
                if first(n):
                    row_numbers(0, (0, 1))
                    pre(0)
                if more:
                    row_numbers(n + 1, (0,))
                if not first(n):
                    router(n - 1)
                trunk(n)
                if not first(n):
                    gates(n - 1)
                    for s in range(2):
                        last_layer(n - 1, s)
                    for s in range(2):
                        residual(n - 1, s)

            c_steps(v, trunk_and_router, attention, tail)
            router(ITERS - 1)
            gates(ITERS - 1)
            for s in range(2):
                last_layer(ITERS - 1, s)
            for s in range(2):
                residual(ITERS - 1, s)

        def c_pick(v, i):
            done = [0]

            def step(ins):
                ins.then_inc(pick_step, 1)
                done[0] += 1

            def settle():
                v.wait_ge(pick_step, PICK * i + done[0])

            v.wait_ge(router_pe, 2 * i + 1)
            step(v.scalar_tensor_tensor(out=l16[:], in0=P[0][0][0:NI, 0, 0:E2], scalar=1.0 / S, in1=RR("bg")[0:NI, :],
                                        op0=ALU.mult, op1=ALU.add))
            settle()
            step(v.tensor_reduce(m16[:], l16[:], AX_X, ALU.max))
            settle()
            step(v.scalar_tensor_tensor(out=c16[:], in0=l16[:], scalar=m16[:, 0:1], in1=R("rev16")[0:NI, :],
                                        op0=ALU.is_equal, op1=ALU.mult))
            settle()
            step(v.tensor_reduce(b16[:], c16[:], AX_X, ALU.max))
            settle()
            step(v.tensor_scalar(b16[:], b16[:], -1.0, float(E2), ALU.mult, ALU.add))
            settle()
            step(v.tensor_copy(pick_i[:], b16[:]))
            step(v.tensor_scalar(l16[:], l16[:], m16[:, 0:1], None, ALU.subtract))
            v.wait_ge(pick_exp, i + 1)
            step(v.reciprocal(g16[:], g16[:]))
            settle()
            step(v.tensor_scalar(gdiag[:], C("ident")[0:NI, 0:NI], g16[:, 0:1], None, ALU.mult))
            assert done[0] == PICK

        mem_c.close()

        block = ctx.enter_context(nc.Block())

        @block.sync
        def _(sp):
            a_sync(sp)
            b_sync(sp)
            c_sync(sp)

        @block.gpsimd
        def _(pool):
            a_pool(pool)
            c_pool(pool)

        @block.scalar
        def _(act):
            a_scalar(act)
            b_scalar(act)
            c_scalar(act)

        @block.vector
        def _(v):
            a_vector(v)
            b_vector(v)
            c_vector(v)

        @block.tensor
        def _(pe):
            a_tensor(pe)
            b_tensor(pe)
            c_tensor(pe)


def kernel(**inputs):
    import concourse.bacc as _bacc
    from concourse.bass_utils import run_bass_kernel_spmd as _run

    f = {k: np.asarray(v) for k, v in inputs.items()}
    images = f["x"].shape[0]
    steps = images // IMGS

    def chunks(w, n):
        return w.reshape(n, 128)

    x = f["x"].reshape(steps, IMGS, CHANNELS, GW, PATCH, GH, PATCH).transpose(0, 2, 4, 6, 1, 3, 5)
    x = x.reshape(steps, KC, 128, IMGS * NPATCH).transpose(0, 2, 1, 3)
    w_tok = f["L0_tok_W"].reshape(D, PATCH, PATCH, CHANNELS).transpose(3, 1, 2, 0).reshape(KC, 128, D).transpose(1, 0, 2)
    in_w, in_b = f["L0_attn_in_proj_w"].reshape(6, 128, D), f["L0_attn_in_proj_b"].reshape(6, 128)
    de_w, de_b = f["L0_attn_delta_w"].reshape(2, 128, D), f["L0_attn_delta_b"].reshape(2, 128)
    order_w = np.stack([in_w[0], de_w[0], in_w[4], in_w[1], de_w[1], in_w[5], in_w[2], in_w[3]])
    order_b = np.stack([in_b[0], de_b[0], in_b[4], in_b[1], de_b[1], in_b[5], in_b[2], in_b[3]])
    conv_w = f["L0_attn_conv_w"].reshape(2, 128, 4).transpose(1, 0, 2).reshape(128, 8)
    parts = {
        "ln_w": f["L0_attn_ln_w"], "ln_b": f["L0_attn_ln_b"], "in_b": order_b.T, "conv_w": conv_w,
        "conv_b": f["L0_attn_conv_b"].reshape(2, 128).T, "state_mix": f["L0_attn_state_mix"].reshape(2, 128).T,
        "skip": f["L0_attn_skip_scale"].reshape(2, 128).T, "out_b": f["L0_attn_out_proj_b"], "tok_b": f["L0_tok_b"],
        "cls": f["L0_tok_cls_token"], "mr_b": f["L0_ffn_mr_b"].T, "ln1_g": f["L0_ffn_ln1_g"],
        "ln1_b": f["L0_ffn_ln1_b"], "mv_b": f["L0_ffn_mv_b"].T, "ln2_g": f["L0_ffn_ln2_g"],
        "ln2_b": f["L0_ffn_ln2_b"], "ln3_g": f["L0_ffn_ln3_g"], "ln3_b": f["L0_ffn_ln3_b"],
        "q_b": f["L1_attn_b_qkv"][0:D], "k_b": f["L1_attn_b_qkv"][D:2 * D], "v_b": f["L1_attn_b_qkv"][2 * D:],
        "attn_b": f["L1_attn_b_out"],
    }
    col = np.concatenate([parts[k].reshape(128, n) for k, (_, n) in COLS.items()], axis=1)
    rparts = {"pos": f["L0_tok_pos_emb"], "alpha": f["L0_ffn_mv_alpha"], "gate_b": f["L0_ffn_gate_b"],
              "bg": f["L1_ffn_bg"]}
    row = np.concatenate([rparts[k].reshape(1, n) for k, (_, n) in ROWS.items()], axis=1)
    w_exp = np.concatenate([
        f["L0_ffn_e_w1"],
        f["L0_ffn_e_w2"].reshape(E, FC, 128, D).transpose(0, 2, 1, 3).reshape(E, 128, FC * D),
        f["L0_ffn_e_b1"].reshape(E, FC, 128).transpose(0, 2, 1),
        np.broadcast_to(f["L0_ffn_e_b2"][:, None, :], (E, 128, D)),
    ], axis=2).reshape(E * 128, -1)
    w_last = np.concatenate([f["L1_ffn_We"], f["L1_ffn_be"][:, :, None]], axis=2).reshape(E2 * 128, D + 1)
    arrays = {
        "x": x, "w_tok": w_tok, "w_in": order_w.transpose(2, 0, 1),
        "w_out": f["L0_attn_out_proj_w"].reshape(D, 2, 128).transpose(2, 1, 0),
        "w_mr": f["L0_ffn_mr_w"].transpose(1, 0, 2), "w_mv": f["L0_ffn_mv_w"].transpose(1, 0, 2),
        "w_gate": f["L0_ffn_gate_w"], "col": col, "row": row, "w_exp": w_exp, "w_last": w_last,
        "w_qkv": f["L1_attn_w_qkv"], "w_att": f["L1_attn_w_out"], "w_g": f["L1_ffn_Wg"],
        "cst": const_tiles()[1], "crow": const_rows(images)[1],
    }
    arrays = {k: np.ascontiguousarray(v) for k, v in arrays.items()}
    nc = _bacc.Bacc("TRN2", target_bir_lowering=False, num_devices=1)
    a = {k: nc.dram_tensor(f"{k}_in", v.shape, mybir.dt.from_np(v.dtype), kind="ExternalInput").ap()
         for k, v in arrays.items()}
    a["out"] = nc.dram_tensor("out", (128, images * S), F32, kind="ExternalOutput").ap()
    build(nc, images, a)
    r = _run(nc, [{f"{k}_in": v for k, v in arrays.items()}], core_ids=[0])
    out = r.results[0]["out"]
    return np.ascontiguousarray(out.reshape(D, images, S).transpose(1, 2, 0))
```
